# Optimizing a Trainium2 kernel written in Bass

```python
import numpy as np
import jax
import jax.numpy as jnp

def _softmax(x, axis=-1):
    return jax.nn.softmax(x, axis=axis)

def _gelu(x):
    return jax.nn.gelu(x, approximate=True)

def _silu(x):
    return jax.nn.silu(x)

def _sigmoid(x):
    return jax.nn.sigmoid(x)

def _layernorm(x, axis=-1, eps=1e-05):
    m = jnp.mean(x, axis=axis, keepdims=True)
    v = jnp.var(x, axis=axis, keepdims=True)
    return (x - m) / jnp.sqrt(v + eps)

def _scatter_add(tgt, idx, src, axis=0):
    return tgt.at[idx].add(src)

def _segment_sum(src, seg, n):
    return jax.ops.segment_sum(src, seg, n)
kernel_name = 'mk_decoder_preln_d1_seqx_r8_0aefb3'

def setup_inputs(seed: int=0):
    np.random.seed(seed)
    _w = jnp.asarray

    def _rec_inputs():
        import jax
        import jax.numpy as jnp
        _rk = jax.random.key(seed)
        x = 7.22e-05 + 1 * jax.random.normal(jax.random.fold_in(_rk, 1), (16, 128, 256), jnp.float32)
        _lenS = 128 - jax.random.randint(jax.random.fold_in(_rk, 7), (16,), 0, max(1, 128 // 4) + 1, jnp.int32)
        _lenS2 = 128 - jax.random.randint(jax.random.fold_in(_rk, 8), (16,), 0, max(1, 128 // 4) + 1, jnp.int32)
        _ctx_2048P = jax.random.normal(jax.random.fold_in(_rk, 11), (16, 16, 256), jnp.float32)
        _ctx_2048c = jax.random.dirichlet(jax.random.fold_in(_rk, 511), 0.3 * jnp.ones((16,), jnp.float32), (16, 128))
        _ctx_2048t = jnp.einsum('bsk,bkd->bsd', _ctx_2048c, _ctx_2048P)
        _ctx_2048t = _ctx_2048t * jax.lax.rsqrt(jnp.mean(jnp.square(_ctx_2048t)) + 1e-12) * 0.953939
        ctx_2048 = 4.13588e-05 + 0.999923 * (_ctx_2048t + 0.3 * jax.random.normal(jax.random.fold_in(_rk, 611), (16, 128, 256), jnp.float32))
        return (x, ctx_2048)
    x, ctx_2048 = _rec_inputs()

    def _L0_attn_setup():
        import jax, jax.numpy as jnp
        import numpy as np
        B, S, DIM = (1, 256, 256)
        HEADS, KV_HEADS = (32, 8)
        DH = DIM // HEADS
        G = HEADS // KV_HEADS
        CBLK = 16
        SBLK = 16
        NSEL = 8
        WIN = 64
        SCALE = DH ** (-0.5)
        NEG = -1e+30
        CDIM = CBLK * DH

        def _rope(x, pos):
            d = x.shape[-1]
            inv = 1.0 / 10000.0 ** (jnp.arange(0, d, 2, dtype=jnp.float32) / d)
            ang = pos[:, None] * inv[None, :]
            cos, sin = (jnp.cos(ang), jnp.sin(ang))
            x1, x2 = (x[..., 0::2], x[..., 1::2])
            return jnp.stack([x1 * cos - x2 * sin, x1 * sin + x2 * cos], axis=-1).reshape(x.shape)

        def _forward(x, w_qkv, k_pos, v_pos, k_cw1, k_cb1, k_cw2, k_cb2, v_cw1, v_cb1, v_cw2, v_cb2, mem_ck, mem_cv, w_gate, b_gate, w_out):
            b, n, _ = x.shape
            di, dkv = (HEADS * DH, KV_HEADS * DH)
            qkv = x @ w_qkv
            q = qkv[..., :di].reshape(b, n, KV_HEADS, G, DH).transpose(0, 2, 3, 1, 4)
            k = qkv[..., di:di + dkv].reshape(b, n, KV_HEADS, DH).transpose(0, 2, 1, 3)
            v = qkv[..., di + dkv:].reshape(b, n, KV_HEADS, DH).transpose(0, 2, 1, 3)
            nc = n // CBLK
            kb = k[:, :, :nc * CBLK].reshape(b, KV_HEADS, nc, CBLK, DH) + k_pos[None, :, None]
            vb = v[:, :, :nc * CBLK].reshape(b, KV_HEADS, nc, CBLK, DH) + v_pos[None, :, None]
            ck = jax.nn.relu(kb.reshape(b, KV_HEADS, nc, CDIM) @ k_cw1 + k_cb1) @ k_cw2 + k_cb2
            cv = jax.nn.relu(vb.reshape(b, KV_HEADS, nc, CDIM) @ v_cw1 + v_cb1) @ v_cw2 + v_cb2
            ck = jnp.concatenate([jnp.broadcast_to(mem_ck[None], (b, KV_HEADS, 1, DH)), ck], axis=2)
            cv = jnp.concatenate([jnp.broadcast_to(mem_cv[None], (b, KV_HEADS, 1, DH)), cv], axis=2)
            csim = jnp.einsum('bhgnd,bhjd->bhgnj', q, ck) * SCALE
            ck_last = jnp.concatenate([jnp.array([-1]), (jnp.arange(nc) + 1) * CBLK - 1])
            cmask = ck_last[None, :] < jnp.arange(n)[:, None]
            csim = jnp.where(cmask, csim, NEG)
            c_out = jnp.einsum('bhgnj,bhjd->bhgnd', jax.nn.softmax(csim, -1), cv)
            imp = csim[..., 1:].mean(axis=2)
            imp = jnp.concatenate([jnp.full(imp.shape[:-1] + (1,), -1000.0, imp.dtype), imp], axis=-1)
            imp = jax.nn.softmax(imp, -1)[..., 1:]
            sel_vals, sel_idx = jax.lax.top_k(imp, NSEL)
            fine_gate_mask = sel_vals > 1e-10
            pos = jnp.arange(n, dtype=jnp.float32)
            rq, rk = (_rope(q, pos), _rope(k, pos))
            nf = n // SBLK
            own = jnp.broadcast_to((jnp.arange(n) // SBLK)[None, None, :, None], (b, KV_HEADS, n, 1))
            idx = jnp.concatenate([sel_idx, own], axis=-1)
            kblocks = rk.reshape(b, KV_HEADS, nf, SBLK, DH)
            vblocks = v.reshape(b, KV_HEADS, nf, SBLK, DH)
            bi = jnp.arange(b)[:, None, None, None]
            hi = jnp.arange(KV_HEADS)[None, :, None, None]
            fk = kblocks[bi, hi, idx].reshape(b, KV_HEADS, n, (NSEL + 1) * SBLK, DH)
            fv = vblocks[bi, hi, idx].reshape(b, KV_HEADS, n, (NSEL + 1) * SBLK, DH)
            sel_m = jnp.repeat(fine_gate_mask[..., None], SBLK, -1).reshape(b, KV_HEADS, n, NSEL * SBLK)
            diag_m = (jnp.arange(n) % SBLK)[:, None] >= jnp.arange(SBLK)[None, :]
            fmask = jnp.concatenate([sel_m, jnp.broadcast_to(diag_m[None, None], (b, KV_HEADS, n, SBLK))], axis=-1)
            fsim = jnp.einsum('bhgnd,bhnjd->bhgnj', rq, fk) * SCALE
            fsim = jnp.where(fmask[:, :, None], fsim, NEG)
            f_out = jnp.einsum('bhgnj,bhnjd->bhgnd', jax.nn.softmax(fsim, -1), fv)
            nwin = n // WIN
            qw = rq.reshape(b, KV_HEADS, G, nwin, WIN, DH)
            kw = rk.reshape(b, KV_HEADS, nwin, WIN, DH)
            vw = v.reshape(b, KV_HEADS, nwin, WIN, DH)
            kcat = jnp.concatenate([jnp.concatenate([jnp.zeros_like(kw[:, :, :1]), kw[:, :, :-1]], 2), kw], 3)
            vcat = jnp.concatenate([jnp.concatenate([jnp.zeros_like(vw[:, :, :1]), vw[:, :, :-1]], 2), vw], 3)
            ssim = jnp.einsum('bhgwid,bhwjd->bhgwij', qw, kcat) * SCALE
            i_, j_ = (jnp.arange(WIN), jnp.arange(2 * WIN))
            delta = i_[:, None] - (j_[None, :] - WIN)
            smask = ((delta >= 0) & (delta <= WIN))[None] & ((jnp.arange(nwin) > 0)[:, None, None] | (j_ >= WIN)[None, None, :])
            ssim = jnp.where(smask[None, None, None], ssim, NEG)
            s_out = jnp.einsum('bhgwij,bhwjd->bhgwid', jax.nn.softmax(ssim, -1), vcat)
            s_out = s_out.reshape(b, KV_HEADS, G, n, DH)
            gates = jax.nn.sigmoid(x @ w_gate + b_gate).reshape(b, n, KV_HEADS, G, 3).transpose(0, 2, 3, 1, 4)
            out = gates[..., 0:1] * c_out + gates[..., 1:2] * f_out + gates[..., 2:3] * s_out
            out = out.transpose(0, 3, 1, 2, 4).reshape(b, n, HEADS * DH)
            return out @ w_out
        key = jax.random.key(seed)
        ks = jax.random.split(key, 16)

        def rnd(i, shape, sc=0.02):
            return jax.random.normal(ks[i], shape, dtype=jnp.float32) * sc
        dim_inner, dim_kv = (HEADS * DH, KV_HEADS * DH)
        return {'hidden_states': jax.random.normal(ks[0], (B, S, DIM), dtype=jnp.float32), 'w_qkv': rnd(1, (DIM, dim_inner + 2 * dim_kv)), 'k_pos': rnd(2, (KV_HEADS, CBLK, DH)), 'v_pos': rnd(3, (KV_HEADS, CBLK, DH)), 'k_cw1': rnd(4, (CDIM, CDIM)), 'k_cb1': jnp.zeros((CDIM,), jnp.float32), 'k_cw2': rnd(5, (CDIM, DH)), 'k_cb2': jnp.zeros((DH,), jnp.float32), 'v_cw1': rnd(6, (CDIM, CDIM)), 'v_cb1': jnp.zeros((CDIM,), jnp.float32), 'v_cw2': rnd(7, (CDIM, DH)), 'v_cb2': jnp.zeros((DH,), jnp.float32), 'mem_ck': rnd(8, (KV_HEADS, 1, DH)), 'mem_cv': rnd(9, (KV_HEADS, 1, DH)), 'w_gate': rnd(10, (DIM, 3 * HEADS)), 'b_gate': jnp.tile(jnp.array([-2.0, -2.0, 2.0], jnp.float32), HEADS), 'w_out': rnd(11, (dim_inner, DIM))}
    _L0_attn_all = _L0_attn_setup()
    _L0_attn_in = {k: v for k, v in _L0_attn_all.items() if k in ('w_qkv', 'k_pos', 'v_pos', 'k_cw1', 'k_cb1', 'k_cw2', 'k_cb2', 'v_cw1', 'v_cb1', 'v_cw2', 'v_cb2', 'mem_ck', 'mem_cv', 'w_gate', 'b_gate', 'w_out')}
    del _L0_attn_all

    def _L0_xattn_setup():
        import jax, jax.numpy as jnp
        import numpy as np
        N_HEAD = 8
        key = jax.random.key(seed)
        k1, k2, k3 = jax.random.split(key, 3)
        b, d, m = (4, 128, 256)
        c, n = (128, 256)
        q = jax.random.normal(k1, (b, d, m), dtype=jnp.float32)
        k = jax.random.normal(k2, (d // d * b, d, n), dtype=jnp.float32).reshape(b, d, n)
        v = jax.random.normal(k3, (b, c, n), dtype=jnp.float32)
        return {'q': q, 'k': k, 'v': v}
    _L0_xattn_all = _L0_xattn_setup()
    _L0_xattn_in = {k: v for k, v in _L0_xattn_all.items() if k in ()}
    del _L0_xattn_all

    def _L0_ffn_setup():
        import jax, jax.numpy as jnp
        import numpy as np
        from jax import lax
        H = 256
        E = 64
        K = 8
        I = 64
        SI = 64
        B, S = (1, 128)
        SCALE = 0.02

        def _moe_forward(hidden_states, gate_w, expert_gate_w, expert_up_w, expert_down_w, shared_gate_w, shared_up_w, shared_down_w, shared_expert_gate_w):
            b, s, h = hidden_states.shape
            x = hidden_states.reshape(-1, h)
            T = x.shape[0]
            shared_out = jax.nn.silu(x @ shared_gate_w) * (x @ shared_up_w) @ shared_down_w
            router_logits = x @ gate_w
            probs = jax.nn.softmax(router_logits.astype(jnp.float32), axis=-1)
            topk_w, topk_idx = lax.top_k(probs, K)
            topk_w = topk_w / jnp.sum(topk_w, axis=-1, keepdims=True)
            topk_w = topk_w.astype(x.dtype)
            combine = jnp.zeros((T, E), dtype=x.dtype).at[jnp.arange(T)[:, None], topk_idx].add(topk_w)

            def body(acc, ws):
                gw, uw, dw, c = ws
                hdn = jax.nn.silu(x @ gw) * (x @ uw)
                return (acc + c[:, None] * (hdn @ dw), None)
            expert_out, _ = lax.scan(body, jnp.zeros_like(x), (expert_gate_w, expert_up_w, expert_down_w, combine.T))
            out = expert_out + jax.nn.sigmoid(x @ shared_expert_gate_w) * shared_out
            return out.reshape(b, s, h)
        key = jax.random.key(seed)
        ks = jax.random.split(key, 10)
        return {'hidden_states': jax.random.normal(ks[0], (B, S, H), dtype=jnp.float32), 'gate_w': jax.random.normal(ks[1], (H, E), dtype=jnp.float32) * SCALE, 'expert_gate_w': jax.random.normal(ks[2], (E, H, I), dtype=jnp.float32) * SCALE, 'expert_up_w': jax.random.normal(ks[3], (E, H, I), dtype=jnp.float32) * SCALE, 'expert_down_w': jax.random.normal(ks[4], (E, I, H), dtype=jnp.float32) * SCALE, 'shared_gate_w': jax.random.normal(ks[5], (H, SI), dtype=jnp.float32) * SCALE, 'shared_up_w': jax.random.normal(ks[6], (H, SI), dtype=jnp.float32) * SCALE, 'shared_down_w': jax.random.normal(ks[7], (SI, H), dtype=jnp.float32) * SCALE, 'shared_expert_gate_w': jax.random.normal(ks[8], (H, 1), dtype=jnp.float32) * SCALE}
    _L0_ffn_all = _L0_ffn_setup()
    _L0_ffn_in = {k: v for k, v in _L0_ffn_all.items() if k in ('gate_w', 'expert_gate_w', 'expert_up_w', 'expert_down_w', 'shared_gate_w', 'shared_up_w', 'shared_down_w', 'shared_expert_gate_w')}
    del _L0_ffn_all
    return {'x': x, 'ctx_2048': ctx_2048, 'L0_attn_w_qkv': _L0_attn_in['w_qkv'], 'L0_attn_k_pos': _L0_attn_in['k_pos'], 'L0_attn_v_pos': _L0_attn_in['v_pos'], 'L0_attn_k_cw1': _L0_attn_in['k_cw1'], 'L0_attn_k_cb1': _L0_attn_in['k_cb1'], 'L0_attn_k_cw2': _L0_attn_in['k_cw2'], 'L0_attn_k_cb2': _L0_attn_in['k_cb2'], 'L0_attn_v_cw1': _L0_attn_in['v_cw1'], 'L0_attn_v_cb1': _L0_attn_in['v_cb1'], 'L0_attn_v_cw2': _L0_attn_in['v_cw2'], 'L0_attn_v_cb2': _L0_attn_in['v_cb2'], 'L0_attn_mem_ck': _L0_attn_in['mem_ck'], 'L0_attn_mem_cv': _L0_attn_in['mem_cv'], 'L0_attn_w_gate': _L0_attn_in['w_gate'], 'L0_attn_b_gate': _L0_attn_in['b_gate'], 'L0_attn_w_out': _L0_attn_in['w_out'], 'L0_ffn_gate_w': _L0_ffn_in['gate_w'], 'L0_ffn_expert_gate_w': _L0_ffn_in['expert_gate_w'], 'L0_ffn_expert_up_w': _L0_ffn_in['expert_up_w'], 'L0_ffn_expert_down_w': _L0_ffn_in['expert_down_w'], 'L0_ffn_shared_gate_w': _L0_ffn_in['shared_gate_w'], 'L0_ffn_shared_up_w': _L0_ffn_in['shared_up_w'], 'L0_ffn_shared_down_w': _L0_ffn_in['shared_down_w'], 'L0_ffn_shared_expert_gate_w': _L0_ffn_in['shared_expert_gate_w']}

def reference(x, ctx_2048, L0_attn_w_qkv, L0_attn_k_pos, L0_attn_v_pos, L0_attn_k_cw1, L0_attn_k_cb1, L0_attn_k_cw2, L0_attn_k_cb2, L0_attn_v_cw1, L0_attn_v_cb1, L0_attn_v_cw2, L0_attn_v_cb2, L0_attn_mem_ck, L0_attn_mem_cv, L0_attn_w_gate, L0_attn_b_gate, L0_attn_w_out, L0_ffn_gate_w, L0_ffn_expert_gate_w, L0_ffn_expert_up_w, L0_ffn_expert_down_w, L0_ffn_shared_gate_w, L0_ffn_shared_up_w, L0_ffn_shared_down_w, L0_ffn_shared_expert_gate_w):
    import jax
    import jax.numpy as jnp

    def _L0_attn_ref(hidden_states, w_qkv, k_pos, v_pos, k_cw1, k_cb1, k_cw2, k_cb2, v_cw1, v_cb1, v_cw2, v_cb2, mem_ck, mem_cv, w_gate, b_gate, w_out):
        import jax, jax.numpy as jnp
        import numpy as np
        B, S, DIM = (1, 256, 256)
        HEADS, KV_HEADS = (32, 8)
        DH = DIM // HEADS
        G = HEADS // KV_HEADS
        CBLK = 16
        SBLK = 16
        NSEL = 8
        WIN = 64
        SCALE = DH ** (-0.5)
        NEG = -1e+30
        CDIM = CBLK * DH

        def _rope(x, pos):
            d = x.shape[-1]
            inv = 1.0 / 10000.0 ** (jnp.arange(0, d, 2, dtype=jnp.float32) / d)
            ang = pos[:, None] * inv[None, :]
            cos, sin = (jnp.cos(ang), jnp.sin(ang))
            x1, x2 = (x[..., 0::2], x[..., 1::2])
            return jnp.stack([x1 * cos - x2 * sin, x1 * sin + x2 * cos], axis=-1).reshape(x.shape)

        def _forward(x, w_qkv, k_pos, v_pos, k_cw1, k_cb1, k_cw2, k_cb2, v_cw1, v_cb1, v_cw2, v_cb2, mem_ck, mem_cv, w_gate, b_gate, w_out):
            b, n, _ = x.shape
            di, dkv = (HEADS * DH, KV_HEADS * DH)
            qkv = x @ w_qkv
            q = qkv[..., :di].reshape(b, n, KV_HEADS, G, DH).transpose(0, 2, 3, 1, 4)
            k = qkv[..., di:di + dkv].reshape(b, n, KV_HEADS, DH).transpose(0, 2, 1, 3)
            v = qkv[..., di + dkv:].reshape(b, n, KV_HEADS, DH).transpose(0, 2, 1, 3)
            nc = n // CBLK
            kb = k[:, :, :nc * CBLK].reshape(b, KV_HEADS, nc, CBLK, DH) + k_pos[None, :, None]
            vb = v[:, :, :nc * CBLK].reshape(b, KV_HEADS, nc, CBLK, DH) + v_pos[None, :, None]
            ck = jax.nn.relu(kb.reshape(b, KV_HEADS, nc, CDIM) @ k_cw1 + k_cb1) @ k_cw2 + k_cb2
            cv = jax.nn.relu(vb.reshape(b, KV_HEADS, nc, CDIM) @ v_cw1 + v_cb1) @ v_cw2 + v_cb2
            ck = jnp.concatenate([jnp.broadcast_to(mem_ck[None], (b, KV_HEADS, 1, DH)), ck], axis=2)
            cv = jnp.concatenate([jnp.broadcast_to(mem_cv[None], (b, KV_HEADS, 1, DH)), cv], axis=2)
            csim = jnp.einsum('bhgnd,bhjd->bhgnj', q, ck) * SCALE
            ck_last = jnp.concatenate([jnp.array([-1]), (jnp.arange(nc) + 1) * CBLK - 1])
            cmask = ck_last[None, :] < jnp.arange(n)[:, None]
            csim = jnp.where(cmask, csim, NEG)
            c_out = jnp.einsum('bhgnj,bhjd->bhgnd', jax.nn.softmax(csim, -1), cv)
            imp = csim[..., 1:].mean(axis=2)
            imp = jnp.concatenate([jnp.full(imp.shape[:-1] + (1,), -1000.0, imp.dtype), imp], axis=-1)
            imp = jax.nn.softmax(imp, -1)[..., 1:]
            sel_vals, sel_idx = jax.lax.top_k(imp, NSEL)
            fine_gate_mask = sel_vals > 1e-10
            pos = jnp.arange(n, dtype=jnp.float32)
            rq, rk = (_rope(q, pos), _rope(k, pos))
            nf = n // SBLK
            own = jnp.broadcast_to((jnp.arange(n) // SBLK)[None, None, :, None], (b, KV_HEADS, n, 1))
            idx = jnp.concatenate([sel_idx, own], axis=-1)
            kblocks = rk.reshape(b, KV_HEADS, nf, SBLK, DH)
            vblocks = v.reshape(b, KV_HEADS, nf, SBLK, DH)
            bi = jnp.arange(b)[:, None, None, None]
            hi = jnp.arange(KV_HEADS)[None, :, None, None]
            fk = kblocks[bi, hi, idx].reshape(b, KV_HEADS, n, (NSEL + 1) * SBLK, DH)
            fv = vblocks[bi, hi, idx].reshape(b, KV_HEADS, n, (NSEL + 1) * SBLK, DH)
            sel_m = jnp.repeat(fine_gate_mask[..., None], SBLK, -1).reshape(b, KV_HEADS, n, NSEL * SBLK)
            diag_m = (jnp.arange(n) % SBLK)[:, None] >= jnp.arange(SBLK)[None, :]
            fmask = jnp.concatenate([sel_m, jnp.broadcast_to(diag_m[None, None], (b, KV_HEADS, n, SBLK))], axis=-1)
            fsim = jnp.einsum('bhgnd,bhnjd->bhgnj', rq, fk) * SCALE
            fsim = jnp.where(fmask[:, :, None], fsim, NEG)
            f_out = jnp.einsum('bhgnj,bhnjd->bhgnd', jax.nn.softmax(fsim, -1), fv)
            nwin = n // WIN
            qw = rq.reshape(b, KV_HEADS, G, nwin, WIN, DH)
            kw = rk.reshape(b, KV_HEADS, nwin, WIN, DH)
            vw = v.reshape(b, KV_HEADS, nwin, WIN, DH)
            kcat = jnp.concatenate([jnp.concatenate([jnp.zeros_like(kw[:, :, :1]), kw[:, :, :-1]], 2), kw], 3)
            vcat = jnp.concatenate([jnp.concatenate([jnp.zeros_like(vw[:, :, :1]), vw[:, :, :-1]], 2), vw], 3)
            ssim = jnp.einsum('bhgwid,bhwjd->bhgwij', qw, kcat) * SCALE
            i_, j_ = (jnp.arange(WIN), jnp.arange(2 * WIN))
            delta = i_[:, None] - (j_[None, :] - WIN)
            smask = ((delta >= 0) & (delta <= WIN))[None] & ((jnp.arange(nwin) > 0)[:, None, None] | (j_ >= WIN)[None, None, :])
            ssim = jnp.where(smask[None, None, None], ssim, NEG)
            s_out = jnp.einsum('bhgwij,bhwjd->bhgwid', jax.nn.softmax(ssim, -1), vcat)
            s_out = s_out.reshape(b, KV_HEADS, G, n, DH)
            gates = jax.nn.sigmoid(x @ w_gate + b_gate).reshape(b, n, KV_HEADS, G, 3).transpose(0, 2, 3, 1, 4)
            out = gates[..., 0:1] * c_out + gates[..., 1:2] * f_out + gates[..., 2:3] * s_out
            out = out.transpose(0, 3, 1, 2, 4).reshape(b, n, HEADS * DH)
            return out @ w_out
        return _forward(hidden_states, w_qkv, k_pos, v_pos, k_cw1, k_cb1, k_cw2, k_cb2, v_cw1, v_cb1, v_cw2, v_cb2, mem_ck, mem_cv, w_gate, b_gate, w_out)

    def _L0_xattn_ref(q, k, v):
        import jax, jax.numpy as jnp
        import numpy as np
        N_HEAD = 8
        b, d, m = q.shape
        c = v.shape[1]
        h = N_HEAD
        qh = q.reshape(b * h, d // h, m)
        kh = k.reshape(b * h, d // h, -1)
        vh = v.reshape(b * h, c // h, -1)
        scale = 1.0 / jnp.sqrt(jnp.asarray(d // h, dtype=q.dtype))
        qk = jnp.einsum('bdm,bdn->bmn', qh, kh) * scale
        sm = jax.nn.softmax(qk, axis=-1)
        ret = jnp.einsum('bmn,bcn->bcm', sm, vh)
        return ret.reshape(b, c, m)

    def _L0_ffn_ref(hidden_states, gate_w, expert_gate_w, expert_up_w, expert_down_w, shared_gate_w, shared_up_w, shared_down_w, shared_expert_gate_w):
        import jax, jax.numpy as jnp
        import numpy as np
        from jax import lax
        H = 256
        E = 64
        K = 8
        I = 64
        SI = 64
        B, S = (1, 128)
        SCALE = 0.02

        def _moe_forward(hidden_states, gate_w, expert_gate_w, expert_up_w, expert_down_w, shared_gate_w, shared_up_w, shared_down_w, shared_expert_gate_w):
            b, s, h = hidden_states.shape
            x = hidden_states.reshape(-1, h)
            T = x.shape[0]
            shared_out = jax.nn.silu(x @ shared_gate_w) * (x @ shared_up_w) @ shared_down_w
            router_logits = x @ gate_w
            probs = jax.nn.softmax(router_logits.astype(jnp.float32), axis=-1)
            topk_w, topk_idx = lax.top_k(probs, K)
            topk_w = topk_w / jnp.sum(topk_w, axis=-1, keepdims=True)
            topk_w = topk_w.astype(x.dtype)
            combine = jnp.zeros((T, E), dtype=x.dtype).at[jnp.arange(T)[:, None], topk_idx].add(topk_w)

            def body(acc, ws):
                gw, uw, dw, c = ws
                hdn = jax.nn.silu(x @ gw) * (x @ uw)
                return (acc + c[:, None] * (hdn @ dw), None)
            expert_out, _ = lax.scan(body, jnp.zeros_like(x), (expert_gate_w, expert_up_w, expert_down_w, combine.T))
            out = expert_out + jax.nn.sigmoid(x @ shared_expert_gate_w) * shared_out
            return out.reshape(b, s, h)
        return _moe_forward(hidden_states, gate_w, expert_gate_w, expert_up_w, expert_down_w, shared_gate_w, shared_up_w, shared_down_w, shared_expert_gate_w)
    x = x + _L0_attn_ref(_layernorm(x, axis=-1), L0_attn_w_qkv, L0_attn_k_pos, L0_attn_v_pos, L0_attn_k_cw1, L0_attn_k_cb1, L0_attn_k_cw2, L0_attn_k_cb2, L0_attn_v_cw1, L0_attn_v_cb1, L0_attn_v_cw2, L0_attn_v_cb2, L0_attn_mem_ck, L0_attn_mem_cv, L0_attn_w_gate, L0_attn_b_gate, L0_attn_w_out)
    x = x + _L0_xattn_ref(_layernorm(x, axis=-1), ctx_2048, ctx_2048)
    x = x + _L0_ffn_ref(_layernorm(x, axis=-1), L0_ffn_gate_w, L0_ffn_expert_gate_w, L0_ffn_expert_up_w, L0_ffn_expert_down_w, L0_ffn_shared_gate_w, L0_ffn_shared_up_w, L0_ffn_shared_down_w, L0_ffn_shared_expert_gate_w)
    return x

_drawn_inputs = setup_inputs


def setup_inputs(seed=0):
    import zlib

    import numpy as np

    out = dict(_drawn_inputs(seed))
    spreads = {'L0_attn_k_cb1': (0.0, 2.0),
     'L0_attn_k_cb2': (0.0, 2.0),
     'L0_attn_v_cb1': (0.0, 0.8),
     'L0_attn_v_cb2': (0.0, 0.8)}
    factors = {'L0_attn_k_pos': 45.654,
     'L0_attn_v_pos': 8.0,
     'L0_attn_k_cw1': 27.13,
     'L0_attn_k_cw2': 8.0,
     'L0_attn_v_cw1': 8.0,
     'L0_attn_v_cw2': 8.0,
     'L0_attn_mem_ck': 182.246,
     'L0_attn_mem_cv': 8.0,
     'L0_attn_w_gate': 8.0,
     'L0_ffn_gate_w': 8.0,
     'L0_ffn_expert_gate_w': 8.0,
     'L0_ffn_expert_up_w': 8.0,
     'L0_ffn_expert_down_w': 8.0,
     'L0_ffn_shared_gate_w': 8.0,
     'L0_ffn_shared_up_w': 8.0,
     'L0_ffn_shared_down_w': 8.0,
     'L0_ffn_shared_expert_gate_w': 8.0}
    for name, (base, spread) in spreads.items():
        noise = np.random.default_rng([zlib.crc32(name.encode()), seed]).standard_normal(out[name].shape)
        drawn = base * np.exp(spread * noise) if base else spread * noise
        out[name] = jnp.asarray(drawn.astype(out[name].dtype))
    for name, factor in factors.items():
        out[name] = (out[name] * factor).astype(out[name].dtype)
    return out
```

```python
import concourse.bass as bass
from concourse import mybir
from contextlib import ExitStack

F32 = mybir.dt.float32
BF16 = mybir.dt.bfloat16
ALU = mybir.AluOpType
ACT = mybir.ActivationFunctionType
AX = mybir.AxisListType.X
ds = bass.ds

B, T, D = 16, 128, 256
G, KV, DH = 4, 8, 8
NB, BLK = 8, 16
HD = KV * DH
SCALE = float(DH) ** -0.5
NO_BLOCK = -1000.0 * G / SCALE
QKV = 6 * HD
PROJ = QKV + 3 * G * KV
XH, XC = 8, 16
XSCALE = float(XC) ** -0.5
E, K_TOP, I = 64, 8, 64
PAIRS = E // 2 + 1
CROWS = 2 * PAIRS
PASS = 1024
NT = B * T
EPS = 1e-5
CHAIN_ATTN = 54
CHAIN_ROUTE = 7


class Tally:

    def __init__(self, sem):
        self.sem, self.base, self.i, self.per, self.k = sem, 0, None, 0, 0

    def begin(self, i, per):
        self.i, self.per, self.k = i, per, 0

    def end(self, times, what=""):
        assert self.k == self.per, (what, "increments of one iteration", self.k, "declared", self.per)
        self.base += self.per * times
        self.i, self.k = None, 0

    def add(self, n=1):
        if self.i is None:
            self.base += n
        else:
            self.k += n

    def value(self):
        return self.base if self.i is None else self.i * self.per + (self.base + self.k)


def build(nc, io):
    ctx = ExitStack()
    with ctx:
        def sb(name, shape, dt=F32):
            return ctx.enter_context(nc.sbuf_tensor(name, shape, dt))

        def sem(name):
            return ctx.enter_context(nc.semaphore(name))

        bank = [ctx.enter_context(nc.psum_tensor(f"bank{n}", [128, 512], F32)) for n in range(8)]

        ident = sb("ident", [128, 128])
        identb = sb("identb", [128, 128], BF16)
        causal = sb("causal", [128, 128], BF16)
        window = sb("window", [128, 128], BF16)
        masks = sb("masks", [128, 2, 128])
        rope_cs = sb("rope_cs", [128, 2, DH // 2])
        block_mask = sb("block_mask", [128, NB])
        past_neg = sb("past_neg", [128, NB])
        kv_rows = sb("kv_rows", [128, 2 * KV])
        cv_rows = sb("cv_rows", [128, KV])
        head_rows = sb("head_rows", [128, XH])
        head_sel = sb("head_sel", [XH, XH, 128], BF16)
        gather = sb("gather", [128, 4, 128])
        w_proj = sb("w_proj", [128, 2, PROJ])
        gate_bias = sb("gate_bias", [128, 96])
        w_out = sb("w_out", [128, 2, D])
        pos = sb("pos", [128, 2, HD])
        cb1 = sb("cb1", [128, 2])
        w2k = sb("w2k", [128, 248])
        b2k = sb("b2k", [1, 248])
        ones_row = sb("ones_row", [1, 128])
        w2v = sb("w2v", [128, DH])
        b2v = sb("b2v", [64, DH])
        mem_k = sb("mem_k", [128, 1])
        w_router = sb("w_router", [128, 2, E + 1])
        eps = sb("eps", [128, 1])

        X = sb("X", [128, B, D])
        stats = sb("stats", [128, B, 6])
        mean = sb("mean", [128, B])
        log_var = sb("log_var", [128, B])
        var_eps = sb("var_eps", [128, B])
        newton = sb("newton", [128, B])
        rstd = sb("rstd", [128, B])
        proj = sb("proj", [128, B, PROJ])
        gates = sb("gates", [128, B, 96])
        block_k = sb("block_k", [128, 2 * NT])
        xt_all = block_k[:, :].rearrange("p (c n) -> p c n", c=2)
        ck = sb("ck", [128, B, 2 * 72])
        cv = sb("cv", [72, B, HD])

        arena = sb("arena", [128, 8192])
        head_sel_f = arena[0:XH, 7168:8192].rearrange("p (h n) -> p h n", h=XH)
        w1_diag = arena[:, :].rearrange("p (i n) -> p i n", i=8)
        probs = arena[:, 0:4096].rearrange("p (u n) -> p u n", u=8)

        xn = sb("xn", [128, 2, D])
        xnT = sb("xnT", [128, 2, D])
        kv_pos = sb("kv_pos", [128, 2, 2, HD])
        hid = sb("hid", [128, 1024])
        hidT = sb("hidT", [128, 1024])
        hid_v = sb("hid_v", [128, 1024])
        cv_raw = sb("cv_raw", [72, B, DH])
        mem_diag = sb("mem_diag", [128, 2 * KV])

        block = ctx.enter_context(nc.Block())
        w = {}

        def S(name):
            if name not in w:
                w[name] = sem(name)
            return w[name]

        def pairs_of_batches(engine):
            def run(body):
                body(0)
                with engine.Fori(1, B // 2) as i:
                    body(i)
            return run

        tiny = sb("tiny", [128, 32])
        tiny_used = [0]

        def settle(eng):
            c = tiny_used[0]
            tiny_used[0] += 1
            if eng is nc.vector:
                nc.vector.memset(tiny[:, c:c + 1], 0.0)
            else:
                nc.gpsimd.tensor_tensor(tiny[:, c:c + 1], ident[:, 0:1], ident[:, 0:1], ALU.add)

        def ln_stats_vector(dve, n, ready):
            chain = S(f"ln{n}_stat")
            with dve.Fori(0, B) as i:
                ready(dve, i)
                last = nc.vector.bn_stats(stats[:, ds(i, 1), :].rearrange("p a s -> p (a s)"),
                                          X[:, ds(i, 1), :].rearrange("p a d -> p (a d)"))
                last.then_inc(chain, 1)
            dve.wait_ge(chain, B)
            nc.vector.tensor_tensor(mean[:], stats[:, :, 1], stats[:, :, 4], ALU.add).then_inc(chain, 1)
            nc.vector.tensor_tensor(newton[:], stats[:, :, 1], stats[:, :, 4], ALU.subtract).then_inc(chain, 1)
            nc.vector.tensor_tensor(var_eps[:], stats[:, :, 2], stats[:, :, 5], ALU.add).then_inc(chain, 1)
            dve.wait_ge(chain, B + 3)
            nc.vector.tensor_scalar(mean[:], mean[:], 0.5, None, ALU.mult).then_inc(chain, 1)
            nc.vector.tensor_tensor(newton[:], newton[:], newton[:], ALU.mult).then_inc(chain, 1)
            nc.vector.tensor_scalar(var_eps[:], var_eps[:], 1.0 / D, EPS, ALU.mult, ALU.add).then_inc(chain, 1)
            dve.wait_ge(chain, B + 6)
            nc.vector.scalar_tensor_tensor(var_eps[:], newton[:], 0.25, var_eps[:], ALU.mult, ALU.add)\
                .then_inc(S(f"ln{n}_var"), 1)
            dve.wait_ge(S(f"ln{n}_guess"), 2)
            c2 = S(f"ln{n}_newton")
            nc.vector.tensor_tensor(newton[:], rstd[:], rstd[:], ALU.mult).then_inc(c2, 1)
            dve.wait_ge(c2, 1)
            nc.vector.tensor_tensor(newton[:], newton[:], var_eps[:], ALU.mult).then_inc(c2, 1)
            dve.wait_ge(c2, 2)
            nc.vector.tensor_scalar(newton[:], newton[:], -0.5, 1.5, ALU.mult, ALU.add).then_inc(c2, 1)
            dve.wait_ge(c2, 3)
            nc.vector.tensor_tensor(rstd[:], rstd[:], newton[:], ALU.mult).then_inc(S(f"ln{n}_done"), 1)
            dve.wait_ge(S(f"ln{n}_done"), 1)

        def ln_stats_scalar(act, n):
            act.wait_ge(S(f"ln{n}_var"), 1)
            nc.scalar.activation(log_var[:], var_eps[:], ACT.Ln).then_inc(S(f"ln{n}_guess"), 1)
            act.wait_ge(S(f"ln{n}_guess"), 1)
            nc.scalar.activation(rstd[:], log_var[:], ACT.Exp, scale=-0.5).then_inc(S(f"ln{n}_guess"), 1)

        def normalise(out, b):
            return nc.vector.tensor_scalar(out, X[:, ds(b, 1), :].rearrange("p a d -> p (a d)"),
                                           mean[:, ds(b, 1)],
                                           rstd[:, ds(b, 1)], ALU.subtract, ALU.mult)

        def proj_vector(dve):
            nc.vector.memset(w2k[:], 0.0)
            nc.vector.memset(b2k[:], 0.0)
            nc.vector.memset(ones_row[:], 1.0)
            nc.vector.memset(arena[:], 0.0).then_inc(S("zeroed"), 1)
            dve.wait_ge(S("ld_x"), 32)
            ln_stats_vector(dve, 1, lambda e, i: None)
            dve.wait_ge(S("ld_first"), 64)
            @pairs_of_batches(dve)
            def _(i):
                for p in range(2):
                    b = 2 * i + p
                    dve.wait_ge(S("xT_done"), b)
                    normalise(xn[:, p, :], b).then_inc(S("xn_ready"), 1)
                for p in range(2):
                    b = 2 * i + p
                    dve.wait_ge(S("proj_kept"), b + 1)
                    dve.wait_ge(S("kvT_done"), b)
                    for n in range(2):
                        src = proj[:, ds(b, 1), (4 + n) * HD:(5 + n) * HD].to_broadcast([128, 2, HD])
                        add = pos[:, n:n + 1, :].to_broadcast([128, 2, HD])
                        last = nc.vector.tensor_tensor(kv_pos[:, n, :, :], src, add, ALU.add)
                    last.then_inc(S("kv_pos_ready"), 1)
                    dve.wait_ge(S("kvT_done"), b + 1)
                    for n in range(2):
                        col = n * NT + b * T
                        nc.vector.tensor_copy(block_k[0:64, ds(col, T)], bank[4 + 2 * p + n][0:64, 0:T])
                        last = nc.vector.tensor_copy(block_k[64:128, ds(col, T - 1)],
                                                     bank[4 + 2 * p + n][64:128, 1:T])
                    last.then_inc(S("block_k_ready"), 1)

        def proj_tensor(pe):
            pe.wait_ge(S("ld_first"), 64)

            def transposes(b, p):
                pe.wait_ge(S("xn_ready"), b + 1)
                pe.wait_ge(S("xnT_ready"), b)
                for c in range(2):
                    last = nc.tensor.transpose(bank[p][:, c * 128:c * 128 + 128], xn[:, p, c * 128:c * 128 + 128],
                                               ident[:])
                last.then_inc(S("xT_done"), 1)

            def project(b, p):
                pe.wait_ge(S("xnT_ready"), b + 1)
                pe.wait_ge(S("proj_kept"), b)
                for c in range(2):
                    last = nc.tensor.matmul(bank[2 + p][:, 0:PROJ], xnT[:, p, c * 128:c * 128 + 128],
                                            w_proj[:, c, :], start=c == 0, stop=c == 1)
                last.then_inc(S("proj_done"), 1)

            def kv_transposes(b, p):
                pe.wait_ge(S("kv_pos_ready"), b + 1)
                pe.wait_ge(S("block_k_ready"), b)
                for n in range(2):
                    last = nc.tensor.transpose(bank[4 + 2 * p + n][:, 0:T],
                                               kv_pos[:, n, :, :].rearrange("p a d -> p (a d)"), ident[:])
                last.then_inc(S("kvT_done"), 1)

            @pairs_of_batches(pe)
            def _(i):
                for p in range(2):
                    transposes(2 * i + p, p)
                for p in range(2):
                    project(2 * i + p, p)
                for p in range(2):
                    kv_transposes(2 * i + p, p)

        def proj_scalar(act):
            ln_stats_scalar(act, 1)
            @pairs_of_batches(act)
            def _(i):
                for p in range(2):
                    act.wait_ge(S("xT_done"), 2 * i + p + 1)
                    act.wait_ge(S("proj_done"), 2 * i + p)
                    nc.scalar.copy(xnT[:, p, :], bank[p][:, 0:D]).then_inc(S("xnT_ready"), 1)
                for p in range(2):
                    b = 2 * i + p
                    act.wait_ge(S("proj_done"), b + 1)
                    nc.scalar.copy(proj[:, ds(b, 1), :].rearrange("p a n -> p (a n)"),
                                   bank[2 + p][:, 0:PROJ]).then_inc(S("proj_kept"), 1)

        def comp_tensor(pe):
            pe.wait_ge(S("block_k_ready"), B)
            for n in range(2):
                pe.wait_ge(S("ld_w1k" if n == 0 else "ld_w1v"), 256)
                if n == 1:
                    pe.wait_ge(S("hid_kept"), 2)
                for half in range(2):
                    for i in range(8):
                        lhsT = block_k[:, n * NT + 2 * i:(n + 1) * NT:BLK]
                        last = nc.tensor.matmul(bank[half][:], lhsT, w1_diag[:, i, half * 512:half * 512 + 512],
                                                start=i == 0, stop=i == 7)
                last.then_inc(S("hidden_done"), 1)
                pe.wait_ge(S("hid_kept"), 2 * n + 2)
                if n == 1:
                    pe.wait_ge(S("hidT_kept"), 2)
                for kv in range(KV):
                    last = nc.tensor.transpose(bank[2 + kv // 4][:, kv % 4 * 128:kv % 4 * 128 + 128],
                                               hid[:, kv * 128:kv * 128 + 128], ident[:])
                last.then_inc(S("hidT_done"), 1)
            pe.wait_ge(S("ld_comp"), 11 * 16)
            pe.wait_ge(S("hidT_kept"), 4)
            for g2 in range(2):
                for kv in range(KV):
                    off = 120 - (g2 * HD + kv * DH)
                    o = bank[4 + 2 * g2 + kv // 4][:, kv % 4 * 128:kv % 4 * 128 + 128]
                    nc.tensor.matmul(o, w2k[:, off:off + 128], hidT[:, kv * 128:kv * 128 + 128],
                                     start=True, stop=False)
                    last = nc.tensor.matmul(o, b2k[:, off:off + 128], ones_row[:], start=False, stop=True)
            last.then_inc(S("ck_done"), 1)
            for b in range(B):
                last = nc.tensor.matmul(bank[0][0:64, b * DH:b * DH + DH], hid_v[:, b * 64:b * 64 + 64], w2v[:],
                                        start=True, stop=True)
            last.then_inc(S("cv_done"), 1)

        def comp_scalar(act):
            for n in range(2):
                act.wait_ge(S("hidden_done"), n + 1)
                if n == 1:
                    act.wait_ge(S("hidT_done"), 1)
                for half in range(2):
                    nc.scalar.copy(hid[:, half * 512:half * 512 + 512], bank[half][:]).then_inc(S("hid_kept"), 1)
                act.wait_ge(S("hidT_done"), n + 1)
                if n == 0:
                    act.wait_ge(S("ld_comp"), 11 * 16)
                for half in range(2):
                    if n == 0:
                        o = hidT[:, half * 512:half * 512 + 512]
                        src = bank[2 + half][:]
                    else:
                        o = hid_v[:, :].rearrange("p (b kv c) -> p kv b c", b=B, kv=KV)[:, half * 4:half * 4 + 4]
                        src = bank[2 + half][:].rearrange("p (kv b c) -> p kv b c", kv=4, b=B)
                    nc.scalar.activation(o, src, ACT.Relu, bias=cb1[:, n:n + 1]).then_inc(S("hidT_kept"), 1)
            act.wait_ge(S("gate_sum"), 1)
            nc.scalar.activation(gates[:], gates[:], ACT.Exp, scale=-1.0).then_inc(S("gate_exp"), 1)

        def comp_vector(dve):
            nc.vector.tensor_tensor(gates[:], proj[:, :, QKV:PROJ],
                                    gate_bias[:].rearrange("p (a n) -> p a n", a=1).to_broadcast([128, B, 96]),
                                    ALU.add).then_inc(S("gate_sum"), 1)
            dve.wait_ge(S("ld_comp"), 11 * 16)
            nc.vector.tensor_scalar(mem_diag[:], kv_rows[:], mem_k[:, 0:1], None, ALU.mult).then_inc(S("mem_diag_ok"), 1)
            dve.wait_ge(S("mem_diag_ok"), 1)
            ck5 = ck[:].rearrange("p b (g n) -> p b g n", g=2)
            for g2 in range(2):
                nc.vector.tensor_copy(ck5[:, :, g2, 64:72],
                                      mem_diag[:, g2 * KV:g2 * KV + KV].rearrange("p (a n) -> p a n", a=1)
                                      .to_broadcast([128, B, KV]))
            nc.vector.tensor_copy(cv_raw[64:72, 1:B, :], cv_raw[64:72, 0:1, :].to_broadcast([8, B - 1, DH]))
            dve.wait_ge(S("ck_done"), 1)
            for g2 in range(2):
                for half in range(2):
                    o = ck5[:, :, g2, half * 32:half * 32 + 32].rearrange("p b (kv c) -> p kv b c", kv=4)
                    last = nc.vector.tensor_copy(o, bank[4 + 2 * g2 + half][:]
                                                 .rearrange("p (kv b c) -> p kv b c", kv=4, b=B))
            last.then_inc(S("ck_ready"), 1)
            dve.wait_ge(S("cv_done"), 1)
            nc.vector.tensor_tensor(cv_raw[0:64], bank[0][0:64, 0:128].rearrange("p (b d) -> p b d", b=B),
                                    b2v[:].rearrange("p (a d) -> p a d", a=1).to_broadcast([64, B, DH]),
                                    ALU.add).then_inc(S("cv_raw_ok"), 1)
            dve.wait_ge(S("cv_raw_ok"), 1)
            o = cv[:].rearrange("p b (kv d) -> p b kv d", kv=KV)
            i0 = cv_raw[:].rearrange("p b (a d) -> p b a d", a=1).to_broadcast([72, B, KV, DH])
            i1 = cv_rows[0:72].rearrange("p (a kv c) -> p a kv c", a=1, c=1).to_broadcast([72, B, KV, DH])
            nc.vector.tensor_tensor(o, i0, i1, ALU.mult).then_inc(S("cv_ready"), 1)
            dve.wait_ge(S("gate_exp"), 1)
            nc.vector.tensor_scalar(gates[:], gates[:], 1.0, None, ALU.add).then_inc(S("gate_one"), 1)
            dve.wait_ge(S("gate_one"), 1)
            nc.vector.reciprocal(gates[:], gates[:]).then_inc(S("gates_ready"), 1)
            dve.wait_ge(S("gates_ready"), 1)

        raw = sb("raw", [128, (G + 1) * HD])
        rot = sb("rot", [128, (G + 1) * HD])
        rope_a = sb("rope_a", [128, 40, 4])
        rope_b = sb("rope_b", [128, 40, 4])
        query = [[sb(f"query{br}{p}", [128, 512]) for p in range(2)] for br in range(2)]
        key_diag = [sb(f"key_diag{p}", [128, KV, 128]) for p in range(2)]
        query_b = sb("query_b", [128, 512], BF16)
        key_b = sb("key_b", [128, KV, 128], BF16)
        rawT = sb("rawT", [128, 256])
        csim = sb("csim", [128, G, 72])
        cexp = sb("cexp", [128, G, 72])
        cprob = sb("cprob", [128, G, 72])
        cprobT = sb("cprobT", [72, 512])
        cmax = sb("cmax", [128, G, KV])
        csum = sb("csum", [128, G, KV])
        imp = sb("imp", [128, 72])
        impmax = sb("impmax", [128, KV])
        impe = sb("impe", [128, 72])
        impsum = sb("impsum", [128, KV])
        skip = sb("skip", [128, HD])
        blockmax = sb("blockmax", [128, G, KV, NB])
        farmax = sb("farmax", [128, G, KV])
        finemax = sb("finemax", [128, G, KV, NB])
        nearmax = sb("nearmax", [128, G, KV])
        rows = [sb(f"rows{br}", [128, G, 128]) for br in range(2)]
        value = [sb(f"value{p}", [128, KV, 32]) for p in range(2)]
        pv = sb("pv", [128, 2, 512])
        weight = sb("weight", [128, G, 4])
        part = sb("part", [128, G, 4, DH])
        attn = [sb(f"attn{p}", [128, G, KV, DH]) for p in range(2)]
        attnT = sb("attnT", [128, 256])

        SMAX = [bank[0], bank[1]]
        SCORE = [bank[2], bank[3]]
        PV = [bank[4], bank[5]]
        T0, T1 = bank[6], bank[7]
        BR = [0, 1, 0, 1]
        HALF = [0, 0, 1, 1]

        def halves(engine, half_body, tail, lead=1):
            for b in range(lead):
                half_body(b, b % 2, b > 0, True, None)
            with engine.Fori(0, (B - 1 - lead) // 2) as i:
                half_body(2 * i + lead, 1, True, True, i)
                half_body(2 * i + lead + 1, 0, True, True, i)
            half_body(B - 1, 1, True, False, None)
            tail(B - 1, 1)

        def attn_tensor(pe):
            def qk_transposes(b):
                pe.wait_ge(S("rot_ready"), b + 1)
                for c in range(2):
                    nc.tensor.transpose(T1[:, 128 + c * 128:256 + c * 128], raw[:, c * 128:c * 128 + 128], ident[:])
                nc.tensor.transpose(T1[0:64, 0:128], rot[:, G * HD:(G + 1) * HD], ident[:]).then_inc(S("rawT_done"), 1)
                for g in range(G):
                    last = nc.tensor.transpose(T0[0:64, g * 128:g * 128 + 128], rot[:, g * HD:g * HD + HD], ident[:])
                last.then_inc(S("rqT_done"), 1)

            def block_scores(b):
                pe.wait_ge(S("rawT_ready"), b + 1)
                for c in range(2):
                    last = nc.tensor.matmul(T1[:, c * 144:c * 144 + 144], rawT[:, c * 128:c * 128 + 128],
                                            ck[:, ds(b, 1), :].rearrange("p a n -> p (a n)"), start=True, stop=True)
                last.then_inc(S("csim_done"), 1)

            def max_scores(b, m):
                if m == 0:
                    pe.wait_ge(S("query_b_ready"), b + 1)
                    pe.wait_ge(S("key_b_ready"), b + 1)
                pe.wait_ge(S(f"smax_read{m % 2}"), 6 * b + m // 2)
                g, half = (m // 2, m % 2) if m < 8 else (m - 8, 0)
                kvs, keys = (slice(half * 4, half * 4 + 4), 128) if m < 8 else (slice(0, 8), 64)
                out = SMAX[m % 2][:, :].rearrange("p (h k) -> p h k", k=keys)
                nc.tensor.matmul(out, query_b[:, g * 128:g * 128 + 128], key_b[:, kvs, 0:keys], start=True, stop=False)
                mask = (causal if m < 8 else window)[:, 0:keys].rearrange("p (a k) -> p a k", a=1)
                nc.tensor.matmul(out, identb[:], mask.to_broadcast([128, 512 // keys, keys]), start=False,
                                 stop=True).then_inc(S("smax_done"), 1)

            def row_transposes(b):
                pe.wait_ge(S("query_low_ready"), b + 1)
                if not isinstance(b, int) or b > 0:
                    pe.wait_ge(S("part_ready"), 4 * b - 1)
                pe.wait_ge(S("cout_kept"), b + 1)
                for br in range(2):
                    pe.wait_ge(S(f"rows_ready{br}"), b + 1)
                    for g in range(G):
                        last = nc.tensor.transpose((T0, T1)[br][:, g * 128:g * 128 + 128], rows[br][:, g, :], ident[:])
                    last.then_inc(S(f"rowsT_done{br}"), 1)

            def comp_transposes(b):
                pe.wait_ge(S("cprob_ready"), b + 1)
                if not isinstance(b, int) or b > 1:
                    pe.wait_ge(S("attnT_ready"), b - 1)
                for g in range(G):
                    last = nc.tensor.transpose(T1[0:72, g * 128:g * 128 + 128], cprob[:, g, :], ident[:])
                last.then_inc(S("cprobT_done"), 1)

            def comp_values(b):
                pe.wait_ge(S("cprobT_ready"), b + 1)
                for g in range(G):
                    last = nc.tensor.matmul(T1[:, g * HD:g * HD + HD], cprobT[:, g * 128:g * 128 + 128],
                                            cv[:, ds(b, 1), :].rearrange("p a n -> p (a n)"), start=True, stop=True)
                last.then_inc(S("cout_done"), 1)

            def score(b, p, u):
                gr, kv = u // 4, HALF[u // 4] * 4 + u % 4
                if u == 0:
                    pe.wait_ge(S("rows_kept0"), b + 1)
                    pe.wait_ge(S("rows_kept1"), b + 1)
                pe.wait_ge(S(f"prob_ready{u % 2}"), 8 * b + u // 2)
                nc.tensor.matmul(SCORE[u % 2][:], key_diag[p][:, kv, :], query[BR[gr]][p][:], start=True, stop=False)
                eye = identb[:].rearrange("p (a k) -> p a k", a=1).to_broadcast([128, G, 128])
                nc.tensor.matmul(SCORE[u % 2][:].rearrange("p (g t) -> p g t", g=G), (causal, window)[BR[gr]][:], eye,
                                 start=False, stop=True).then_inc(S("score_done"), 1)

            def values(b, p, gr):
                if gr == 0:
                    pe.wait_ge(S("value_ready"), b + 1)
                for j in range(4):
                    u = gr * 4 + j
                    pe.wait_ge(S(f"prob_ready{u % 2}"), 8 * b + u // 2 + 1)
                pe.wait_ge(S(f"pv_kept{gr % 2}"), 2 * b + gr // 2)
                for j in range(4):
                    u = gr * 4 + j
                    last = nc.tensor.matmul(PV[gr % 2][32 * j:32 * j + 32, :], value[p][:, HALF[gr] * 4 + j, :],
                                            probs[:, u % 8, :], start=True, stop=True)
                last.then_inc(S("pv_done"), 1)

            def pv_transposes(b, gr):
                pe.wait_ge(S(f"pv_kept{gr % 2}"), 2 * b + gr // 2 + 1)
                if gr == 0:
                    pe.wait_ge(S("attn_added"), b)
                    if not isinstance(b, int) or b < B - 1:
                        pe.wait_ge(S("query_low_ready"), b + 2)
                elif gr == 3 and (not isinstance(b, int) or b < B - 2):
                    pe.wait_ge(S("query_low_ready"), b + 3)
                else:
                    pe.wait_ge(S("part_ready"), 4 * b + gr)
                for g in range(G):
                    last = nc.tensor.transpose(T0[:, g * 128:g * 128 + 128], pv[:, gr % 2, g * 128:g * 128 + 128],
                                               ident[:])
                last.then_inc(S("pvT_done"), 1)

            def out_transposes(b, p):
                pe.wait_ge(S("attn_ready"), b + 1)
                if not isinstance(b, int) or b < B - 2:
                    pe.wait_ge(S("csim_kept"), b + 3)
                a = attn[p][:].rearrange("p g kv d -> p (g kv d)")
                for c in range(2):
                    last = nc.tensor.transpose(T1[:, c * 128:c * 128 + 128], a[:, c * 128:c * 128 + 128], ident[:])
                last.then_inc(S("attnT_done"), 1)

            def out_project(b):
                pe.wait_ge(S("attnT_ready"), b + 1)
                pe.wait_ge(S("part_ready"), 4 * b + 4)
                for c in range(2):
                    last = nc.tensor.matmul(T0[:, 0:D], attnT[:, c * 128:c * 128 + 128], w_out[:, c, :],
                                            start=c == 0, stop=c == 1)
                last.then_inc(S("out_done"), 1)

            def half_body(b, p, previous, following, i):
                for u in range(16):
                    score(b, p, u)
                    if u == 1:
                        if previous:
                            values(b - 1, 1 - p, 3)
                        if following:
                            qk_transposes(b + 1)
                    if u == 2 and previous:
                        pv_transposes(b - 1, 3)
                    if u == 3 and following:
                        block_scores(b + 1)
                    if u == 4 and previous:
                        out_transposes(b - 1, 1 - p)
                    if following and 4 <= u < 10:
                        max_scores(b + 1, 2 * (u - 4))
                        max_scores(b + 1, 2 * (u - 4) + 1)
                    if u == 6 and previous:
                        out_project(b - 1)
                    if u in (5, 9, 13):
                        values(b, p, (u - 5) // 4)
                    if u in (7, 11, 15):
                        pv_transposes(b, (u - 7) // 4)
                    if following and u == 11:
                        comp_transposes(b + 1)
                    if following and u == 12:
                        comp_values(b + 1)
                    if following and u == 15:
                        row_transposes(b + 1)

            def tail(b, p):
                values(b, p, 3)
                pv_transposes(b, 3)
                out_transposes(b, p)
                out_project(b)

            pe.wait_ge(S("ld_attn"), 5 * 16)
            pe.wait_ge(S("ld_key_rows"), 32)
            pe.wait_ge(S("attn_zeroed"), 1)
            pe.wait_ge(S("masks_ready"), 1)
            pe.wait_ge(S("ck_ready"), 1)
            pe.wait_ge(S("cv_ready"), 1)
            qk_transposes(0)
            block_scores(0)
            for m in range(12):
                max_scores(0, m)
            comp_transposes(0)
            comp_values(0)
            row_transposes(0)
            halves(pe, half_body, tail)

        def attn_scalar(act):
            def after_qk(b, p):
                act.wait_ge(S("rqT_done"), b + 1)
                nc.scalar.copy(query_b[0:64, :], T0[0:64, :]).then_inc(S("query_b_ready"), 1)
                nc.scalar.copy(query[0][p][0:64, :], T0[0:64, :])
                nc.scalar.copy(query[1][p][0:64, :], T0[0:64, :]).then_inc(S("query_low_ready"), 1)
                act.wait_ge(S("key_diag_ready"), b + 1)
                nc.scalar.copy(rawT[:], T1[:, 128:384]).then_inc(S("rawT_ready"), 1)

            def comp_exp(b):
                act.wait_ge(S("cexp_in"), b + 1)
                nc.scalar.activation(cexp[:], cexp[:], ACT.Exp, scale=SCALE).then_inc(S("cexp_done"), 1)
                act.wait_ge(S("impe_in"), b + 1)
                nc.scalar.activation(impe[:], impe[:], ACT.Exp, scale=SCALE / G).then_inc(S("impe_done"), 1)

            def comp_keep(b):
                act.wait_ge(S("cprobT_done"), b + 1)
                nc.scalar.copy(cprobT[:], T1[0:72, :]).then_inc(S("cprobT_ready"), 1)

            def rows_keep(b, p):
                for br in range(2):
                    act.wait_ge(S(f"rowsT_done{br}"), b + 1)
                    nc.scalar.copy(query[br][p][64:128, :], (T0, T1)[br][64:128, :])\
                        .then_inc(S(f"rows_kept{br}"), 1)

            def softmax(b, u):
                act.wait_ge(S("score_done"), 16 * b + u + 1)
                if not (isinstance(b, int) and b == 0 and u < 8):
                    act.wait_ge(S("pv_done"), 4 * b + u // 4 - 1)
                nc.scalar.activation(probs[:, u % 8, :], SCORE[u % 2][:], ACT.Exp, scale=SCALE)\
                    .then_inc(S(f"prob_ready{u % 2}"), 1)

            def pv_keep(b, gr):
                act.wait_ge(S("pv_done"), 4 * b + gr + 1)
                nc.scalar.copy(pv[:, gr % 2, :], PV[gr % 2][:]).then_inc(S(f"pv_kept{gr % 2}"), 1)

            def out_keep(b):
                act.wait_ge(S("attnT_done"), b + 1)
                nc.scalar.copy(attnT[:], T1[:, 0:256]).then_inc(S("attnT_ready"), 1)

            def half_body(b, p, previous, following, i):
                for u in range(16):
                    softmax(b, u)
                    if u == 1:
                        if previous:
                            pv_keep(b - 1, 3)
                        if following:
                            after_qk(b + 1, 1 - p)
                    if u == 5 and previous:
                        out_keep(b - 1)
                    if u in (6, 10, 14):
                        pv_keep(b, (u - 6) // 4)
                    if following and u == 8:
                        comp_exp(b + 1)
                    if following and u == 11:
                        comp_keep(b + 1)
                    if following and u == 15:
                        rows_keep(b + 1, 1 - p)

            def tail(b, p):
                pv_keep(b, 3)
                out_keep(b)

            act.wait_ge(S("attn_zeroed"), 1)
            after_qk(0, 0)
            comp_exp(0)
            comp_keep(0)
            rows_keep(0, 0)
            halves(act, half_body, tail)

        def attn_vector(dve):
            chain = Tally(S("attn_chain"))

            def link(ins):
                ins.then_inc(chain.sem, 1)
                chain.add(1)
                dve.wait_ge(chain.sem, chain.value())

            def gkc(ap, n):
                return ap.rearrange("p g (kv c) -> p g kv c", c=n)

            def keys(b, p):
                dve.wait_ge(S("rawT_done"), b + 1)
                src = T1[0:64, 0:128].rearrange("p (a k) -> p a k", a=1).to_broadcast([64, KV, 128])
                m = kv_rows[0:64, 0:KV].rearrange("p (kv a) -> p kv a", a=1).to_broadcast([64, KV, 128])
                nc.vector.tensor_tensor(key_diag[p][0:64], src, m, ALU.mult).then_inc(S("key_diag_ready"), 1)

            def comp_softmax(b):
                dve.wait_ge(S("csim_done"), b + 1)
                s = T1[:, 0:288].rearrange("p (g n) -> p g n", g=G)
                for g in range(G):
                    nc.vector.tensor_tensor(csim[:, g, 0:64].rearrange("p (kv c) -> p kv c", c=NB),
                                            s[:, g, 0:64].rearrange("p (kv c) -> p kv c", c=NB),
                                            block_mask[:].rearrange("p (a c) -> p a c", a=1)
                                            .to_broadcast([128, KV, NB]), ALU.add)
                nc.vector.tensor_copy(csim[:, :, 64:72], s[:, :, 64:72]).then_inc(S("csim_kept"), 1)
                dve.wait_ge(S("csim_kept"), b + 1)
                cs, ce = gkc(csim[:, :, 0:64], NB), gkc(cexp[:, :, 0:64], NB)
                link(nc.vector.tensor_reduce(cmax[:], cs, AX, ALU.max))
                link(nc.vector.tensor_tensor(cmax[:], cmax[:], csim[:, :, 64:72], ALU.max))
                mb = cmax[:].rearrange("p g (kv a) -> p g kv a", a=1).to_broadcast([128, G, KV, NB])
                nc.vector.tensor_tensor(ce, cs, mb, ALU.subtract)
                nc.vector.tensor_tensor(cexp[:, :, 64:72], csim[:, :, 64:72], cmax[:], ALU.subtract)\
                    .then_inc(S("cexp_in"), 1)
                link(nc.vector.tensor_reduce(imp[:, 0:64], csim[:, :, 0:64].rearrange("p g n -> p n g"), AX, ALU.add))
                im = imp[:, 0:64].rearrange("p (kv c) -> p kv c", c=NB)
                link(nc.vector.tensor_reduce(impmax[:], im, AX, ALU.max))
                link(nc.vector.tensor_scalar(impmax[:], impmax[:], NO_BLOCK, None, ALU.max))
                nc.vector.tensor_scalar(impe[:, 64:72], impmax[:], -1.0, NO_BLOCK, ALU.mult, ALU.add)
                ib = impmax[:].rearrange("p (kv a) -> p kv a", a=1).to_broadcast([128, KV, NB])
                nc.vector.tensor_tensor(impe[:, 0:64].rearrange("p (kv c) -> p kv c", c=NB), im, ib,
                                        ALU.subtract).then_inc(S("impe_in"), 1)

            def comp_weights(b):
                dve.wait_ge(S("cexp_done"), b + 1)
                ce = gkc(cexp[:, :, 0:64], NB)
                link(nc.vector.tensor_reduce(csum[:], ce, AX, ALU.add))
                link(nc.vector.tensor_tensor(csum[:], csum[:], cexp[:, :, 64:72], ALU.add))
                link(nc.vector.reciprocal(csum[:], csum[:]))
                gt = gates[:, ds(b, 1), 0:32].rearrange("p a (g kv) -> p (a g) kv", g=G)
                link(nc.vector.tensor_tensor(csum[:], csum[:], gt, ALU.mult))
                dve.wait_ge(S("cprobT_done"), b)
                sbc = csum[:].rearrange("p g (kv a) -> p g kv a", a=1).to_broadcast([128, G, KV, NB])
                nc.vector.tensor_tensor(gkc(cprob[:, :, 0:64], NB), ce, sbc, ALU.mult)
                nc.vector.tensor_tensor(cprob[:, :, 64:72], cexp[:, :, 64:72], csum[:], ALU.mult)\
                    .then_inc(S("cprob_ready"), 1)
                dve.wait_ge(S("impe_done"), b + 1)
                ie = impe[:, 0:64].rearrange("p (kv c) -> p kv c", c=NB)
                link(nc.vector.tensor_reduce(impsum[:], ie, AX, ALU.add))
                link(nc.vector.tensor_tensor(impsum[:], impsum[:], impe[:, 64:72], ALU.add))
                link(nc.vector.tensor_scalar(impsum[:], impsum[:], 1e-10, None, ALU.mult))
                th = impsum[:].rearrange("p (kv a) -> p kv a", a=1).to_broadcast([128, KV, NB])
                sk = skip[:].rearrange("p (kv c) -> p kv c", c=NB)
                link(nc.vector.tensor_tensor(sk, ie, th, ALU.is_le))
                pn = past_neg[:].rearrange("p (a c) -> p a c", a=1).to_broadcast([128, KV, NB])
                link(nc.vector.tensor_tensor(sk, sk, pn, ALU.mult))

            def reduce_max(b, m):
                dve.wait_ge(S("smax_done"), 12 * b + m + 1)
                if m < 8:
                    g, half = m // 2, m % 2
                    src = SMAX[m % 2][:].rearrange("p (h c k) -> p h c k", h=4, k=BLK)
                    ins = nc.vector.tensor_reduce(blockmax[:, g, half * 4:half * 4 + 4, :], src, AX, ALU.max)
                else:
                    src = SMAX[m % 2][:].rearrange("p (h k) -> p h k", k=64)
                    ins = nc.vector.tensor_reduce(farmax[:, m - 8, :], src, AX, ALU.max)
                ins.then_inc(S(f"smax_read{m % 2}"), 1)

            def maxima(b):
                for n in range(2):
                    dve.wait_ge(S(f"smax_read{n}"), 6 * b + 6)
                sk = skip[:].rearrange("p (kv c) -> p kv c", c=NB)
                for g in range(G):
                    last = nc.vector.tensor_tensor(finemax[:, g], blockmax[:, g], sk, ALU.add)
                link(last)
                dve.wait_ge(S("rowsT_done0"), b)
                dve.wait_ge(S("rowsT_done1"), b)
                nc.vector.tensor_reduce(rows[0][:, :, 120:128], finemax[:], AX, ALU.max)
                nc.vector.tensor_copy(rows[0][:, :, 64:120].rearrange("p g (kv c) -> p g kv c", c=7),
                                      sk[:, :, 0:7].rearrange("p (a kv) c -> p a kv c", a=1)
                                      .to_broadcast([128, G, KV, 7])).then_inc(S("rows_ready0"), 1)
                link(nc.vector.tensor_reduce(nearmax[:], blockmax[:, :, :, 4:8], AX, ALU.max))
                nc.vector.tensor_tensor(rows[1][:, :, 120:128], nearmax[:], farmax[:], ALU.max)\
                    .then_inc(S("rows_ready1"), 1)

            def comp_out(b, p):
                dve.wait_ge(S("cout_done"), b + 1)
                if not isinstance(b, int) or b > 1:
                    dve.wait_ge(S("attnT_done"), b - 1)
                nc.vector.tensor_copy(attn[p][:].rearrange("p g kv d -> p (g kv d)"), T1[:, 0:256])\
                    .then_inc(S("cout_kept"), 1)

            def add_branch(b, p, gr):
                dve.wait_ge(S("pvT_done"), 4 * b + gr + 1)
                src = T0[:].rearrange("p (g kv c) -> p g kv c", g=G, c=32)
                link(nc.vector.reciprocal(weight[:], src[:, :, :, DH]))
                k0 = 32 + 32 * BR[gr]
                gt = gates[:, ds(b, 1), k0:k0 + 32].rearrange("p a (g kv) -> p (a g) kv", g=G)
                link(nc.vector.tensor_tensor(weight[:], weight[:], gt[:, :, HALF[gr] * 4:HALF[gr] * 4 + 4], ALU.mult))
                wb = weight[:].rearrange("p g (kv a) -> p g kv a", a=1).to_broadcast([128, G, 4, DH])
                nc.vector.tensor_tensor(part[:], src[:, :, :, 0:DH], wb, ALU.mult).then_inc(S("part_ready"), 1)
                dve.wait_ge(S("part_ready"), 4 * b + gr + 1)
                if gr == 0:
                    dve.wait_ge(S("cout_kept"), b + 1)
                a = attn[p][:, :, HALF[gr] * 4:HALF[gr] * 4 + 4, :]
                ins = nc.vector.tensor_tensor(a, a, part[:], ALU.add)
                if gr == 3:
                    ins.then_inc(S("attn_ready"), 1)
                else:
                    link(ins)

            def residual(b):
                dve.wait_ge(S("out_done"), b + 1)
                x = X[:, ds(b, 1), :].rearrange("p a d -> p (a d)")
                nc.vector.tensor_tensor(x, x, T0[:, 0:D], ALU.add).then_inc(S("attn_added"), 1)

            def half_body(b, p, previous, following, i):
                if i is not None and p == 1:
                    chain.begin(i, CHAIN_ATTN)
                for u in range(16):
                    if u == 1 and following:
                        keys(b + 1, 1 - p)
                    if u == 2 and previous:
                        add_branch(b - 1, 1 - p, 3)
                    if u == 3 and following:
                        comp_softmax(b + 1)
                    if following and 4 <= u < 10:
                        reduce_max(b + 1, 2 * (u - 4))
                        reduce_max(b + 1, 2 * (u - 4) + 1)
                    if u == 6 and previous:
                        residual(b - 1)
                    if u in (7, 11, 15):
                        add_branch(b, p, (u - 7) // 4)
                    if following and u == 9:
                        comp_weights(b + 1)
                        maxima(b + 1)
                    if following and u == 12:
                        comp_out(b + 1, 1 - p)
                if i is not None and p == 0:
                    chain.end(7, "CHAIN_ATTN")

            def tail(b, p):
                add_branch(b, p, 3)
                residual(b)

            for br in range(2):
                nc.vector.memset(rows[br][:], 0.0)
            for p in range(2):
                nc.vector.memset(value[p][:], 0.0)
            nc.vector.memset(query_b[64:128], 0.0)
            link(nc.vector.memset(key_b[64:128], 0.0))
            nc.vector.memset(value[0][:, :, DH:DH + 1], 1.0)
            nc.vector.memset(value[1][:, :, DH:DH + 1], 1.0).then_inc(S("attn_zeroed"), 1)
            dve.wait_ge(S("ld_attn"), 5 * 16)
            nc.vector.tensor_copy(identb[:], ident[:])
            nc.vector.tensor_copy(causal[:], masks[:, 0, :])
            nc.vector.tensor_copy(window[:], masks[:, 1, :]).then_inc(S("masks_ready"), 1)
            keys(0, 0)
            comp_softmax(0)
            for m in range(12):
                reduce_max(0, m)
            comp_weights(0)
            maxima(0)
            comp_out(0, 0)
            halves(dve, half_body, tail)

        def attn_pool(pool):
            chain = Tally(S("rope_chain"))

            def link(ins):
                ins.then_inc(chain.sem, 1)
                chain.add(1)
                pool.wait_ge(chain.sem, chain.value())

            def rotate(b):
                pool.wait_ge(S("rqT_done"), b)
                pool.wait_ge(S("rawT_done"), b)
                settle(nc.gpsimd)
                nc.gpsimd.tensor_copy(raw[:], proj[:, ds(b, 1), 0:(G + 1) * HD].rearrange("p a n -> p (a n)"))\
                    .then_inc(S("raw_ready"), 1)
                pool.wait_ge(S("raw_ready"), b + 1)
                x = raw[:].rearrange("p (h d two) -> p h d two", d=4, two=2)
                o = rot[:].rearrange("p (h d two) -> p h d two", d=4, two=2)
                cos = rope_cs[:, 0:1, :].to_broadcast([128, 40, 4])
                sin = rope_cs[:, 1:2, :].to_broadcast([128, 40, 4])
                nc.gpsimd.tensor_tensor(rope_a[:], x[:, :, :, 0], cos, ALU.mult)
                link(nc.gpsimd.tensor_tensor(rope_b[:], x[:, :, :, 1], sin, ALU.mult))
                link(nc.gpsimd.tensor_tensor(o[:, :, :, 0], rope_a[:], rope_b[:], ALU.subtract))
                nc.gpsimd.tensor_tensor(rope_a[:], x[:, :, :, 0], sin, ALU.mult)
                link(nc.gpsimd.tensor_tensor(rope_b[:], x[:, :, :, 1], cos, ALU.mult))
                nc.gpsimd.tensor_tensor(o[:, :, :, 1], rope_a[:], rope_b[:], ALU.add).then_inc(S("rot_ready"), 1)

            def narrow_keys(b, p):
                pool.wait_ge(S("key_diag_ready"), b + 1)
                settle(nc.gpsimd)
                nc.gpsimd.tensor_copy(key_b[0:64], key_diag[p][0:64]).then_inc(S("key_b_ready"), 1)

            def take_values(b, p):
                if not isinstance(b, int) or b > 1:
                    pool.wait_ge(S("pv_done"), 4 * b - 3)
                src = proj[:, ds(b, 1), (G + 1) * HD:QKV].rearrange("p a (kv d) -> p (a kv) d", d=DH)
                settle(nc.gpsimd)
                nc.gpsimd.tensor_copy(value[p][:, :, 0:DH], src).then_inc(S("value_ready"), 1)

            pool.wait_ge(S("attn_zeroed"), 1)
            pool.wait_ge(S("ld_first"), 64)
            pool.wait_ge(S("ld_attn"), 5 * 16)
            pool.wait_ge(S("proj_kept"), B)
            rotate(0)
            narrow_keys(0, 0)

            def half_body(b, p, previous, following, i):
                if i is not None and p == 1:
                    chain.begin(i, 6)
                take_values(b, p)
                if following:
                    rotate(b + 1)
                    narrow_keys(b + 1, 1 - p)
                if i is not None and p == 0:
                    chain.end(7, "rope_chain")

            halves(pool, half_body, lambda b, p: None)

        xq = [arena[:, 4096 + 256 * p:4352 + 256 * p] for p in range(2)]
        old_proj = proj[:].rearrange("p b n -> p (b n)")
        xdiag = [old_proj[:, 2048 * p:2048 * p + 2048].rearrange("p (h n) -> p h n", h=XH) for p in range(2)]
        xq_b = sb("xq_b", [128, D], BF16)
        xdiag_b = old_proj[:, 4096:5120].bitcast(BF16).rearrange("p (h n) -> p h n", h=XH)
        ctx_in = [arena[:, 4608 + 256 * p:4864 + 256 * p] for p in range(2)]
        xvalue = [old_proj[:, 5120 + 512 * p:5632 + 512 * p].rearrange("p (c h x) -> p c h x", c=2, h=XH)
                  for p in range(2)]
        xmax = sb("xmax", [128, 2, XH])
        xshift = [sb(f"xshift{p}", [XH, D], BF16) for p in range(2)]
        xpv = sb("xpv", [128, 512])
        xden = sb("xden", [128, D])
        xout = sb("xout", [128, D])

        def cross_loads(sp):
            with sp.Fori(0, (B - 2) // 2) as i:
                for p in range(2):
                    b = 2 * i + p
                    sp.wait_ge(S("xdiag_ready"), b + 1)
                    sp.wait_ge(S("ctxT_done"), b + 1)
                    sp.dma_start(ctx_in[p], io["ctx_2048"][ds(b + 2, 1)].rearrange("a t d -> (a t) d"))\
                        .then_inc(S(f"ld_ctx{p}"), 16)

        def ctx_loaded(eng, b, p):
            eng.wait_ge(S(f"ld_ctx{p}"), 8 * (b - p) + 16)

        def cross_tensor(pe):
            def ctx_transposes(b, p):
                ctx_loaded(pe, b, p)
                for c in range(2):
                    last = nc.tensor.transpose(T0[:, c * 128:c * 128 + 128], ctx_in[p][:, c * 128:c * 128 + 128],
                                               ident[:])
                last.then_inc(S("ctxT_done"), 1)

            def max_scores(b, m):
                if m == 0:
                    pe.wait_ge(S("xq_b_ready"), b + 1)
                    pe.wait_ge(S("xdiag_b_ready"), b + 1)
                pe.wait_ge(S(f"xmax_read{m % 2}"), 4 * b + m // 2)
                hs = 2 * (m % 4)
                nc.tensor.matmul(SMAX[m % 2][:].rearrange("p (h n) -> p h n", h=2),
                                 xq_b[:, m // 4 * 128:m // 4 * 128 + 128], xdiag_b[:, hs:hs + 2, :],
                                 start=True, stop=True).then_inc(S("xmax_scored"), 1)

            def shift_transposes(b):
                pe.wait_ge(S("xvalue_ready"), b + 1)
                pe.wait_ge(S("xmax_read0"), 4 * b + 4)
                pe.wait_ge(S("xmax_read1"), 4 * b + 4)
                for c in range(2):
                    last = nc.tensor.transpose(T0[0:XH, c * 128:c * 128 + 128], xmax[:, c, :], ident[:])
                last.then_inc(S("xmaxT_done"), 1)

            def score(b, p, h):
                if h == 0:
                    pe.wait_ge(S("xshift_ready"), b + 1)
                    pe.wait_ge(S("xdiag_ready"), b + 1)
                pe.wait_ge(S(f"xprob_ready{h % 2}"), 4 * b + h // 2)
                out = SCORE[h % 2]
                for c in range(2):
                    o = out[:, c * D:c * D + D]
                    nc.tensor.matmul(o, head_sel[:, h, :], xshift[p][:], start=True, stop=False)
                    last = nc.tensor.matmul(o, xdiag[p][:, h, c * 128:c * 128 + 128], xq[p], start=False, stop=True)
                last.then_inc(S("xscore_done"), 1)

            def values(b, p, gr):
                pe.wait_ge(S("xprob_ready0"), 4 * b + 2 * gr + 2)
                pe.wait_ge(S("xprob_ready1"), 4 * b + 2 * gr + 2)
                pe.wait_ge(S(f"xpv_kept{gr}"), b)
                for c in range(2):
                    for j in range(4):
                        last = nc.tensor.matmul(PV[gr][32 * j:32 * j + 32, 0:D], xvalue[p][:, c, gr * 4 + j, :],
                                                probs[:, gr * 4 + j, c * D:c * D + D], start=c == 0, stop=c == 1)
                last.then_inc(S("xpv_done"), 1)

            def gather_rows(b):
                pe.wait_ge(S("xpv_kept1"), b + 1)
                pe.wait_ge(S("xadded"), b)
                for n in range(2):
                    for gr in range(2):
                        last = nc.tensor.matmul(T1[:, n * D:n * D + D], gather[:, 2 * n + gr, :],
                                                xpv[:, gr * D:gr * D + D], start=gr == 0, stop=gr == 1)
                last.then_inc(S("xgathered"), 1)

            def half_body(b, p, previous, following, i):
                for h in range(XH):
                    score(b, p, h)
                    if h == 1 and previous:
                        values(b - 1, 1 - p, 1)
                    if h == 3 and previous:
                        gather_rows(b - 1)
                    if h == 5:
                        values(b, p, 0)
                    if following:
                        if h == 1:
                            ctx_transposes(b + 1, 1 - p)
                        if 2 <= h < 6:
                            max_scores(b + 1, 2 * (h - 2))
                            max_scores(b + 1, 2 * (h - 2) + 1)
                        if h == 7:
                            shift_transposes(b + 1)

            def tail(b, p):
                values(b, p, 1)
                gather_rows(b)

            pe.wait_ge(S("cross_zeroed"), 1)
            pe.wait_ge(S("ld_cross"), 48)
            pe.wait_ge(S("attn_added"), B)
            ctx_transposes(0, 0)
            for m in range(8):
                max_scores(0, m)
            shift_transposes(0)
            halves(pe, half_body, tail, 3)

        def cross_scalar(act):
            def prepare(b, p):
                act.wait_ge(S("xq_ready"), b + 1)
                nc.scalar.copy(xq_b[:], xq[p]).then_inc(S("xq_b_ready"), 1)
                act.wait_ge(S("xdiag_ready"), b + 1)
                nc.scalar.copy(xdiag_b, xdiag[p]).then_inc(S("xdiag_b_ready"), 1)

            def keep_values(b, p):
                act.wait_ge(S("ctxT_done"), b + 1)
                nc.scalar.copy(xvalue[p][:, :, :, 0:XC],
                               T0[:, 0:256].rearrange("p (c h x) -> p c h x", c=2, h=XH)).then_inc(S("xvalue_ready"), 1)

            def keep_shift(b, p):
                act.wait_ge(S("xmaxT_done"), b + 1)
                nc.scalar.mul(xshift[p][:], T0[0:XH, 0:D], -1.0).then_inc(S("xshift_ready"), 1)

            def softmax(b, h):
                act.wait_ge(S("xscore_done"), 8 * b + h + 1)
                if not (isinstance(b, int) and b == 0):
                    act.wait_ge(S("xpv_done"), 2 * b - 1 + h // 4)
                nc.scalar.activation(probs[:, h, :], SCORE[h % 2][:], ACT.Exp, scale=XSCALE)\
                    .then_inc(S(f"xprob_ready{h % 2}"), 1)

            def pv_keep(b, gr):
                act.wait_ge(S("xpv_done"), 2 * b + gr + 1)
                act.wait_ge(S("xgathered"), b)
                nc.scalar.copy(xpv[:, gr * D:gr * D + D], PV[gr][:, 0:D]).then_inc(S(f"xpv_kept{gr}"), 1)

            def half_body(b, p, previous, following, i):
                for h in range(XH):
                    softmax(b, h)
                    if h == 0 and following:
                        prepare(b + 1, 1 - p)
                    if h == 2 and previous:
                        pv_keep(b - 1, 1)
                    if h == 2 and following:
                        keep_values(b + 1, 1 - p)
                    if h == 6:
                        pv_keep(b, 0)
                    if h == 7 and following:
                        keep_shift(b + 1, 1 - p)

            act.wait_ge(S("cross_zeroed"), 1)
            ln_stats_scalar(act, 2)
            prepare(0, 0)
            keep_values(0, 0)
            keep_shift(0, 0)
            halves(act, half_body, lambda b, p: pv_keep(b, 1), 3)

        def cross_vector(dve):
            def query_(b, p):
                if not isinstance(b, int) or b > 1:
                    dve.wait_ge(S("xscore_done"), 8 * b - 8)
                normalise(xq[p], b).then_inc(S("xq_ready"), 1)

            def reduce_max(b, m):
                dve.wait_ge(S("xmax_scored"), 8 * b + m + 1)
                if m == 0:
                    dve.wait_ge(S("xmaxT_done"), b)
                hs = 2 * (m % 4)
                nc.vector.tensor_reduce(xmax[:, m // 4, hs:hs + 2], SMAX[m % 2][:].rearrange("p (h n) -> p h n", h=2),
                                        AX, ALU.max).then_inc(S(f"xmax_read{m % 2}"), 1)

            def residual(b):
                dve.wait_ge(S("xgathered"), b + 1)
                nc.vector.reciprocal(xden[:], T1[:, D:2 * D]).then_inc(S("xden_ready"), 1)
                dve.wait_ge(S("xden_ready"), b + 1)
                nc.vector.tensor_tensor(xout[:], T1[:, 0:D], xden[:], ALU.mult).then_inc(S("xadded"), 1)
                dve.wait_ge(S("xadded"), b + 1)
                x = X[:, ds(b, 1), :].rearrange("p a d -> p (a d)")
                nc.vector.tensor_tensor(x, x, xout[:], ALU.add).then_inc(S("xdone"), 1)

            def half_body(b, p, previous, following, i):
                for h in range(XH):
                    if h == 0 and following:
                        query_(b + 1, 1 - p)
                    if following and 2 <= h < 6:
                        reduce_max(b + 1, 2 * (h - 2))
                        reduce_max(b + 1, 2 * (h - 2) + 1)
                    if h == 4 and previous:
                        residual(b - 1)

            dve.wait_ge(S("attn_added"), B)
            for p in range(2):
                last = nc.vector.memset(xvalue[p], 0.0)
            last.then_inc(S("xvalue_zero"), 1)
            dve.wait_ge(S("xvalue_zero"), 1)
            dve.wait_ge(S("ld_cross"), 48)
            nc.vector.tensor_copy(head_sel[:], head_sel_f)
            nc.vector.memset(xvalue[0][:, :, :, XC:XC + 1], 1.0)
            nc.vector.memset(xvalue[1][:, :, :, XC:XC + 1], 1.0).then_inc(S("cross_zeroed"), 1)
            ln_stats_vector(dve, 2, lambda e, i: None)
            query_(0, 0)
            for m in range(8):
                reduce_max(0, m)
            halves(dve, half_body, lambda b, p: residual(b), 3)

        def cross_pool(pool):
            def spread(b, p):
                ctx_loaded(pool, b, p)
                if not isinstance(b, int) or b > 1:
                    pool.wait_ge(S("xscore_done"), 8 * b - 8)
                src = ctx_in[p].rearrange("p (a n) -> p a n", a=1).to_broadcast([128, XH, D])
                m = head_rows[:].rearrange("p (h a) -> p h a", a=1).to_broadcast([128, XH, D])
                nc.gpsimd.tensor_tensor(xdiag[p], src, m, ALU.mult).then_inc(S("xdiag_ready"), 1)

            def half_body(b, p, previous, following, i):
                if following:
                    spread(b + 1, 1 - p)

            pool.wait_ge(S("ld_cross"), 48)
            pool.wait_ge(S("attn_added"), B)
            spread(0, 0)
            halves(pool, half_body, lambda b, p: None, 3)

        logits = sb("logits", [128, E + 1])
        top = sb("top", [128, 8])
        left = sb("left", [128, E])
        chosen = sb("chosen", [128, E])
        route_e = sb("route_e", [128, E + 1])
        route_n = sb("route_n", [128, 1])
        route_s = sb("route_s", [128, 1])
        combine = [sb(f"combine{p}", [128, CROWS]) for p in range(2)]
        combineT = sb("combineT", [CROWS, 2, 128])
        w_up = [old_proj[:, 6144 + 512 * p:6656 + 512 * p].rearrange("p (c s m) -> p c s m", c=2, s=2)
                for p in range(2)]
        w_down = [old_proj[:, 7168 + 256 * p:7424 + 256 * p] for p in range(2)]
        comb = [xdiag[p][:, 0:4, :].rearrange("p h n -> p (h n)") for p in range(2)]
        act_g = [arena[:, 5120 + 512 * n:5632 + 512 * n] for n in range(2)]
        act_u = [arena[:, 6144 + 512 * n:6656 + 512 * n] for n in range(2)]
        hT = [arena[:, 7168 + 512 * n:7680 + 512 * n] for n in range(2)]
        scratch = nc.dram_tensor("combine_scratch", [CROWS, NT], F32, kind="Internal").ap()
        GATE = [bank[0], bank[1]]
        UP = [bank[2], bank[3]]
        OUT = [bank[4 + n] for n in range(4)]
        NPASS = NT // PASS

        def moe_loads(sp):
            with sp.Fori(0, B // 2) as i:
                for p in range(2):
                    b = 2 * i + p
                    sp.wait_ge(S("combineT_ready"), b + 1)
                    sp.dma_start(scratch[:, ds(b * T, T)], combineT[:, p, :]).then_inc(S("combine_out"), 16)
            sp.wait_ge(S("combine_out"), 16 * B)

            def pair(j, n, p, first):
                if not first:
                    sp.wait_ge(S("down_done"), 2 * n - 2)
                sp.dma_start(w_up[p], io["w_up"][ds(j, 1)].rearrange("a p n -> (a p) n")
                             .rearrange("p (c s m) -> p c s m", c=2, s=2)).then_inc(S(f"ld_pair{p}"), 16)
                sp.dma_start(w_down[p], io["w_down"][ds(j, 1)].rearrange("a p n -> (a p) n"))\
                    .then_inc(S(f"ld_pair{p}"), 16)

            def rows_(j, t0, p):
                for r in range(2):
                    sp.dma_start(comb[p][64 * r:64 * r + 64, :],
                                 scratch[ds(2 * j + r, 1), t0:t0 + PASS].to_broadcast([64, PASS]))\
                        .then_inc(S(f"ld_pair{p}"), 16)

            def store(ps):
                sp.wait_ge(S("final_ready"), ps + 1)
                sp.dma_start(io["out"].rearrange("b t d -> t b d")[:, 8 * ps:8 * ps + 8, :],
                             X[:, 8 * ps:8 * ps + 8, :]).then_inc(S("stored"), 16)

            for ps in range(NPASS):
                n0 = ps * PAIRS
                for j in range(2):
                    pair(j, n0 + j, (n0 + j) % 2, n0 + j < 2)
                    rows_(j, ps * PASS, (n0 + j) % 2)
                if ps:
                    store(ps - 1)
                with sp.Fori(1, (PAIRS - 1) // 2) as i:
                    for h in range(2):
                        pair(2 * i + h, n0 + 2 * i + h, (n0 + h) % 2, False)
                        rows_(2 * i + h, ps * PASS, (n0 + h) % 2)
                pair(PAIRS - 1, n0 + PAIRS - 1, (n0 + PAIRS - 1) % 2, False)
                rows_(PAIRS - 1, ps * PASS, (n0 + PAIRS - 1) % 2)
            store(NPASS - 1)
            sp.wait_ge(S("stored"), 16 * NPASS)

        def moe_tensor(pe):
            pe.wait_ge(S("ld_router"), 16)

            def transposes(b, p):
                pe.wait_ge(S("xn3_ready"), b + 1)
                pe.wait_ge(S("xn3T_ready"), b)
                for c in range(2):
                    last = nc.tensor.transpose(bank[p][:, c * 128:c * 128 + 128], xn[:, p, c * 128:c * 128 + 128],
                                               ident[:])
                last.then_inc(S("x3T_done"), 1)

            def route(b, p):
                pe.wait_ge(S("xn3T_ready"), b + 1)
                pe.wait_ge(S("logits_kept"), b)
                for c in range(2):
                    last = nc.tensor.matmul(bank[2 + p][:, 0:E + 1], xnT[:, p, c * 128:c * 128 + 128],
                                            w_router[:, c, :], start=c == 0, stop=c == 1)
                last.then_inc(S("logits_done"), 1)

            def combine_transpose(b, p):
                pe.wait_ge(S("combine_ready"), b + 1)
                pe.wait_ge(S("combineT_ready"), b)
                nc.tensor.transpose(bank[4 + p][0:CROWS, 0:128], combine[p][:], ident[:])\
                    .then_inc(S("combineT_done"), 1)

            @pairs_of_batches(pe)
            def _(i):
                for p in range(2):
                    transposes(2 * i + p, p)
                for p in range(2):
                    route(2 * i + p, p)
                for p in range(2):
                    combine_transpose(2 * i + p, p)

            def up(n, use, p, t0, h):
                if h == 0:
                    pe.wait_ge(S(f"ld_pair{p}"), 64 * use + 64)
                pe.wait_ge(S(f"gated{h}"), n)
                pe.wait_ge(S(f"upped{h}"), n)
                t = t0 + 512 * h
                for s, out in enumerate((GATE[h], UP[h])):
                    for c in range(2):
                        last = nc.tensor.matmul(out[:], w_up[p][:, c, s, :], xt_all[:, c, t:t + 512],
                                                start=c == 0, stop=c == 1)
                    last.then_inc(S(("gate_done", "up_done")[s]), 1)

            def down(n, p, h):
                pe.wait_ge(S(f"hT_ready{h}"), n + 1)
                for q in range(4):
                    k = 4 * h + q
                    last = nc.tensor.matmul(OUT[k // 2][:, k % 2 * D:k % 2 * D + D], hT[h][:, q * 128:q * 128 + 128],
                                            w_down[p], start=False, stop=True, skip_group_check=True)
                last.then_inc(S("down_done"), 1)

            pe.wait_ge(S("xn3T_ready"), B)
            pe.wait_ge(S("combineT_ready"), B)
            pe.wait_ge(S("xt_all_ready"), B)
            for ps in range(NPASS):
                n0, t0 = ps * PAIRS, ps * PASS
                up(n0, n0 // 2, n0 % 2, t0, 0)
                if ps:
                    pe.wait_ge(S("final_ready"), ps)
                for k in range(4):
                    nc.tensor.matmul(OUT[k][:], zero_b[:], zero_b4[:], start=True, stop=True, skip_group_check=True)
                def two_pairs(i):
                    for hh in range(2):
                        n, p = n0 + 2 * i + hh, (n0 + hh) % 2
                        up(n, None, p, t0, 1)
                        down(n, p, 0)
                        up(n + 1, (n0 + hh + 1) // 2 + i, 1 - p, t0, 0)
                        down(n, p, 1)

                if ps == 0:
                    two_pairs(0)
                with pe.Fori(1 if ps == 0 else 0, (PAIRS - 1) // 2) as i:
                    two_pairs(i)
                n, p = n0 + PAIRS - 1, (n0 + PAIRS - 1) % 2
                up(n, None, p, t0, 1)
                down(n, p, 0)
                down(n, p, 1)

        zero_b = sb("zero_b", [128, 128], BF16)
        zero_b4 = sb("zero_b4", [128, 512], BF16)

        def moe_scalar(act):
            ln_stats_scalar(act, 3)
            @pairs_of_batches(act)
            def _(i):
                for p in range(2):
                    b = 2 * i + p
                    act.wait_ge(S("x3T_done"), b + 1)
                    act.wait_ge(S("logits_done"), b)
                    act.wait_ge(S("xt_all_ready"), 2 * i)
                    nc.scalar.copy(xnT[:, p, :], bank[p][:, 0:D]).then_inc(S("xn3T_ready"), 1)
                for p in range(2):
                    b = 2 * i + p
                    act.wait_ge(S("logits_done"), b + 1)
                    act.wait_ge(S("combine_ready"), b)
                    nc.scalar.copy(logits[:], bank[2 + p][:, 0:E + 1]).then_inc(S("logits_kept"), 1)
                    act.wait_ge(S("route_max"), b + 1)
                    nc.scalar.activation(route_e[:, 0:E], logits[:, 0:E], ACT.Exp, bias=route_n[:, 0:1])
                    nc.scalar.activation(route_e[:, E:E + 1], logits[:, E:E + 1], ACT.Exp, scale=-1.0)\
                        .then_inc(S("route_exp"), 1)
                    act.wait_ge(S("combineT_done"), b + 1)
                    if p == 0:
                        act.wait_ge(S("combine_out"), 16 * b)
                    nc.scalar.copy(combineT[:, p, :], bank[4 + p][0:CROWS, 0:128]).then_inc(S("combineT_ready"), 1)

            def gate(n, h):
                act.wait_ge(S("gate_done"), 2 * n + h + 1)
                act.wait_ge(S(f"upped{h}"), n)
                nc.scalar.activation(act_g[h], GATE[h][:], ACT.Silu).then_inc(S(f"gated{h}"), 1)

            for h in range(2):
                gate(0, h)
            with act.Fori(1, NPASS * PAIRS) as n:
                for h in range(2):
                    gate(n, h)

        def moe_vector(dve):
            nc.vector.memset(zero_b[:], 0.0)
            nc.vector.memset(zero_b4[:], 0.0)
            for p in range(2):
                last = nc.vector.memset(combine[p][:], 0.0)
            last.then_inc(S("moe_zeroed"), 1)
            dve.wait_ge(S("xdone"), B)
            ln_stats_vector(dve, 3, lambda e, i: None)
            chain = Tally(S("route_chain"))

            def link(ins):
                ins.then_inc(chain.sem, 1)
                chain.add(1)
                dve.wait_ge(chain.sem, chain.value())

            @pairs_of_batches(dve)
            def _(i):
                chain.begin(i, 2 * CHAIN_ROUTE)
                for p in range(2):
                    b = 2 * i + p
                    dve.wait_ge(S("x3T_done"), b)
                    normalise(xn[:, p, :], b).then_inc(S("xn3_ready"), 1)
                for p in range(2):
                    b = 2 * i + p
                    dve.wait_ge(S("logits_kept"), b + 1)
                    settle(nc.vector)
                    link(nc.vector.max(top[:], logits[:, 0:E]))
                    nc.vector.tensor_scalar(route_n[:], top[:, 0:1], -1.0, None, ALU.mult).then_inc(S("route_max"), 1)
                    link(nc.vector.match_replace(left[:], top[:], logits[:, 0:E], -3.0e38))
                    link(nc.vector.tensor_tensor(chosen[:], logits[:, 0:E], left[:], ALU.not_equal))
                    dve.wait_ge(S("route_exp"), b + 1)
                    link(nc.vector.tensor_tensor(chosen[:], chosen[:], route_e[:, 0:E], ALU.mult))
                    link(nc.vector.tensor_reduce(route_s[:], chosen[:], AX, ALU.add))
                    link(nc.vector.reciprocal(route_s[:], route_s[:]))
                    dve.wait_ge(S("combineT_done"), b)
                    nc.vector.tensor_scalar(combine[p][:, 0:E], chosen[:], route_s[:, 0:1], None, ALU.mult)
                    link(nc.vector.tensor_scalar(route_e[:, E:E + 1], route_e[:, E:E + 1], 1.0, None, ALU.add))
                    nc.vector.reciprocal(combine[p][:, E:E + 1], route_e[:, E:E + 1]).then_inc(S("combine_ready"), 1)
            chain.end(B // 2, "CHAIN_ROUTE x 2")

            def gated(n, h):
                dve.wait_ge(S(f"gated{h}"), n + 1)
                dve.wait_ge(S("up_done"), 2 * n + h + 1)
                dve.wait_ge(S(f"hT_ready{h}"), n)
                nc.vector.tensor_tensor(act_u[h], act_g[h], UP[h][:], ALU.mult).then_inc(S(f"upped{h}"), 1)

            for ps in range(NPASS):
                if ps == 0:
                    for h in range(2):
                        gated(0, h)
                with dve.Fori(1 if ps == 0 else 0, PAIRS) as j:
                    for h in range(2):
                        gated(j + ps * PAIRS, h)
                dve.wait_ge(S("down_done"), 2 * PAIRS * (ps + 1))
                for k in range(4):
                    x = X[:, 8 * ps + 2 * k:8 * ps + 2 * k + 2, :].rearrange("p b d -> p (b d)")
                    last = nc.vector.tensor_tensor(x, x, OUT[k][:], ALU.add)
                last.then_inc(S("final_ready"), 1)

        def moe_pool(pool):
            @pairs_of_batches(pool)
            def _(i):
                for p in range(2):
                    b = 2 * i + p
                    pool.wait_ge(S("xn3T_ready"), b + 1)
                    settle(nc.gpsimd)
                    nc.gpsimd.tensor_copy(xt_all[:, :, ds(b * T, T)],
                                          xnT[:, p, :].rearrange("p (c t) -> p c t", c=2)).then_inc(S("xt_all_ready"), 1)

            def weigh(i):
                for p in range(2):
                    pool.wait_ge(S(f"ld_pair{p}"), 64 * i + 64)
                    for h in range(2):
                        pool.wait_ge(S(f"upped{h}"), 2 * i + p + 1)
                        pool.wait_ge(S("down_done"), 2 * (2 * i + p))
                        nc.gpsimd.tensor_tensor(hT[h], act_u[h], comb[p][:, 512 * h:512 * h + 512], ALU.mult)\
                            .then_inc(S(f"hT_ready{h}"), 1)

            weigh(0)
            with pool.Fori(1, NPASS * PAIRS // 2) as i:
                weigh(i)


        @block.gpsimd
        def _(pool):
            attn_pool(pool)
            cross_pool(pool)
            moe_pool(pool)

        @block.vector
        def _(dve):
            proj_vector(dve)
            comp_vector(dve)
            attn_vector(dve)
            cross_vector(dve)
            moe_vector(dve)

        @block.scalar
        def _(act):
            proj_scalar(act)
            comp_scalar(act)
            attn_scalar(act)
            cross_scalar(act)
            moe_scalar(act)

        @block.tensor
        def _(pe):
            proj_tensor(pe)
            comp_tensor(pe)
            attn_tensor(pe)
            cross_tensor(pe)
            moe_tensor(pe)

        @block.sync
        def _(sp):
            def load(dst, src, s):
                sp.dma_start(dst, src).then_inc(S(s), 16)

            xv = io["x"].rearrange("b t d -> t b d")
            load(ident[:], io["c_ident"], "ld_first")
            for c in range(2):
                load(X[:, 8 * c:8 * c + 8, :], xv[:, 8 * c:8 * c + 8, :], "ld_x")
            load(w_proj[:], io["w_proj"].rearrange("(c p) n -> p c n", p=128), "ld_first")
            load(pos[:], io["pos"], "ld_first")
            load(gate_bias[:], io["gate_bias"].partition_broadcast(128), "ld_first")
            for n, name in enumerate(("L0_attn_k_cb1", "L0_attn_v_cb1")):
                load(cb1[:, n:n + 1], io[name].rearrange("(p a) -> p a", a=1), "ld_comp")
            sp.wait_ge(S("zeroed"), 1)
            load(w2k[:, 120:128], io["L0_attn_k_cw2"], "ld_comp")
            load(b2k[:, 120:128], io["L0_attn_k_cb2"].rearrange("(a d) -> a d", a=1), "ld_comp")
            load(w2v[:], io["L0_attn_v_cw2"], "ld_comp")
            load(b2v[:], io["L0_attn_v_cb2"].partition_broadcast(64), "ld_comp")
            for g in range(2):
                load(mem_k[64 * g:64 * g + 64, :], io["L0_attn_mem_ck"].rearrange("h a d -> (h d) a"), "ld_comp")
            load(cv_raw[64:72, 0, :], io["L0_attn_mem_cv"].rearrange("h a d -> (h a) d"), "ld_comp")
            load(kv_rows[:], io["c_kv_rows"], "ld_comp")
            load(cv_rows[:], io["c_cv_rows"], "ld_comp")

            def load_w1(name, s):
                src = io[name].rearrange("(i r d) n -> r d i n", r=2, d=DH)
                for r in range(2):
                    for kv in range(KV):
                        p0 = r * HD + kv * DH
                        load(w1_diag[p0:p0 + DH, :, kv * 128:kv * 128 + 128], src[r], s)

            load_w1("L0_attn_k_cw1", "ld_w1k")
            for dst, name in ((masks, "c_masks"), (rope_cs, "c_rope"), (block_mask, "c_block_mask"), (past_neg, "c_past_neg")):
                load(dst[:], io[name], "ld_attn")
            load(w_out[:], io["w_out"].rearrange("(c p) n -> p c n", p=128), "ld_attn")
            load(head_rows[:], io["c_head_rows"], "ld_cross")
            load(gather[:], io["c_gather"], "ld_cross")
            load(w_router[:], io["w_router"].rearrange("(c p) n -> p c n", p=128), "ld_router")
            sp.wait_ge(S("hidden_done"), 1)
            load_w1("L0_attn_v_cw1", "ld_w1v")
            for p in range(2):
                load(key_diag[p][64:128, :, :], io["c_key_rows"], "ld_key_rows")
            sp.wait_ge(S("hidden_done"), 2)
            for i in range(2):
                load(ctx_in[i], io["ctx_2048"][i], f"ld_ctx{i}")
            load(head_sel_f, io["c_head_sel"], "ld_cross")
            cross_loads(sp)
            moe_loads(sp)



def constants():
    import numpy as np

    f4, neg = np.float32, -1e30
    t = np.arange(T)
    past = (np.arange(NB)[None] + 1) * BLK - 1 < t[:, None]
    ahead = t[None] > t[:, None]
    inv = f4(1.0) / f4(10000.0) ** (np.arange(0, DH, 2, dtype=f4) / f4(DH))
    ang = t.astype(f4)[:, None] * inv[None]
    key_rows = np.zeros((64, KV, T), f4)
    for kv in range(KV):
        for c in range(NB - 1):
            key_rows[kv * 7 + c, kv, c * BLK:c * BLK + BLK] = 1.0
        key_rows[56 + kv, kv] = -1.0
    kv_rows = np.zeros((128, 2 * KV), f4)
    kv_rows[np.arange(128), np.arange(128) // DH] = 1.0
    cv_rows = np.zeros((128, KV), f4)
    cv_rows[np.arange(64), np.arange(64) // NB] = 1.0
    cv_rows[64 + np.arange(KV), np.arange(KV)] = 1.0
    head_rows = np.zeros((128, XH), f4)
    head_rows[t, t // XC] = 1.0
    head_sel = np.zeros((XH, XH, 128), f4)
    head_sel[np.arange(XH), np.arange(XH)] = 1.0
    gather = np.zeros((128, 4, 128), f4)
    for h in range(XH):
        for c in range(XC):
            gather[h % 4 * 32 + c, h // 4, h * XC + c] = 1.0
            gather[h % 4 * 32 + XC, 2 + h // 4, h * XC + c] = 1.0
    return {
        "c_ident": np.eye(128, dtype=f4),
        "c_masks": np.stack([np.where(ahead, neg, 0.0),
                             np.where(ahead | (t[:, None] - t[None] > 64), neg, 0.0)], 1).astype(f4),
        "c_rope": np.stack([np.cos(ang), np.sin(ang)], 1).astype(f4),
        "c_block_mask": np.where(past, 0.0, neg).astype(f4), "c_past_neg": np.where(past, neg, 0.0).astype(f4),
        "c_kv_rows": kv_rows, "c_cv_rows": cv_rows, "c_head_rows": head_rows,
        "c_head_sel": head_sel, "c_gather": gather, "c_key_rows": key_rows,
    }


def layouts(a):
    import numpy as np

    q = a["L0_attn_w_qkv"][:, :G * HD].reshape(D, KV, G, DH).transpose(0, 2, 1, 3).reshape(D, G * HD)
    gate = a["L0_attn_w_gate"].reshape(D, KV, G, 3).transpose(0, 3, 2, 1).reshape(D, 96)
    none = np.zeros((1, D, I), np.float32)
    up = [np.concatenate([a[f"L0_ffn_expert_{s}_w"], a[f"L0_ffn_shared_{s}_w"][None], none]) for s in ("gate", "up")]
    up = np.stack(up).reshape(2, PAIRS, 2, 2, 128, I)
    down = np.concatenate([a["L0_ffn_expert_down_w"], a["L0_ffn_shared_down_w"][None], none.reshape(1, I, D)])
    pos = [np.tile(a[n].transpose(1, 0, 2).reshape(BLK, HD), (NB, 1)) for n in ("L0_attn_k_pos", "L0_attn_v_pos")]
    return {
        "w_proj": np.concatenate([q, a["L0_attn_w_qkv"][:, G * HD:], gate], 1),
        "gate_bias": a["L0_attn_b_gate"].reshape(KV, G, 3).transpose(2, 1, 0).reshape(96),
        "w_out": a["L0_attn_w_out"].reshape(KV, G, DH, D).transpose(1, 0, 2, 3).reshape(D, D),
        "pos": np.stack(pos, 1),
        "w_router": np.concatenate([a["L0_ffn_gate_w"], a["L0_ffn_shared_expert_gate_w"]], 1),
        "w_up": up.transpose(1, 4, 3, 0, 2, 5).reshape(PAIRS, 128, 512),
        "w_down": down.reshape(PAIRS, 128, D),
    }


PLAIN = ["x", "ctx_2048", "L0_attn_k_cw1", "L0_attn_k_cb1", "L0_attn_k_cw2", "L0_attn_k_cb2", "L0_attn_v_cw1",
         "L0_attn_v_cb1", "L0_attn_v_cw2", "L0_attn_v_cb2", "L0_attn_mem_ck", "L0_attn_mem_cv"]


def kernel(**inputs):
    import numpy as np
    import concourse.bacc as bacc
    from concourse.bass_utils import run_bass_kernel_spmd

    a = {k: np.asarray(v) for k, v in inputs.items()}
    sent = {n: a[n] for n in PLAIN} | layouts(a) | constants()
    nc = bacc.Bacc("TRN2", target_bir_lowering=False, num_devices=1)
    arrays, io = {}, {}
    for name, v in sent.items():
        v = np.ascontiguousarray(v)
        arrays[f"in_{name}"] = v
        io[name] = nc.dram_tensor(f"in_{name}", v.shape, mybir.dt.from_np(v.dtype), kind="ExternalInput").ap()
    io["out"] = nc.dram_tensor("out_0", (B, T, D), F32, kind="ExternalOutput").ap()
    build(nc, io)
    r = run_bass_kernel_spmd(nc, [arrays], core_ids=[0])
    return r.results[0]["out_0"]
```

```python
import concourse.bass as bass
from concourse import mybir
from contextlib import ExitStack

F32 = mybir.dt.float32
BF16 = mybir.dt.bfloat16
F32R = mybir.dt.float32r
ALU = mybir.AluOpType
ACT = mybir.ActivationFunctionType
AX = mybir.AxisListType.X
ds = bass.ds

B, T, D = 16, 128, 256
G, KV, DH = 4, 8, 8
NB, BLK = 8, 16
HD = KV * DH
SCALE = float(DH) ** -0.5
NO_BLOCK = -1000.0 * G / SCALE
QKV = 6 * HD
PROJ = QKV + 3 * G * KV
XH, XC = 8, 16
XSCALE = float(XC) ** -0.5
E, K_TOP, I = 64, 8, 64
PAIRS = E // 2 + 1
CROWS = 2 * PAIRS
PASS = 1024
NT = B * T
EPS = 1e-5
CHAIN_ATTN = 56
CHAIN_ROUTE = 7


class Tally:

    def __init__(self, sem):
        self.sem, self.base, self.i, self.per, self.k = sem, 0, None, 0, 0

    def begin(self, i, per):
        self.i, self.per, self.k = i, per, 0

    def end(self, times, what=""):
        assert self.k == self.per, (what, "increments of one iteration", self.k, "declared", self.per)
        self.base += self.per * times
        self.i, self.k = None, 0

    def add(self, n=1):
        if self.i is None:
            self.base += n
        else:
            self.k += n

    def value(self):
        return self.base if self.i is None else self.i * self.per + (self.base + self.k)


def build(nc, io):
    ctx = ExitStack()
    with ctx:
        place = [ctx]

        def sb(name, shape, dt=F32):
            return place[0].enter_context(nc.sbuf_tensor(name, shape, dt))

        def phase_memory():
            if place[0] is not ctx:
                place[0].close()
            place[0] = ExitStack()

        def sem(name):
            return ctx.enter_context(nc.semaphore(name))

        bank = [ctx.enter_context(nc.psum_tensor(f"bank{n}", [128, 512], F32)) for n in range(8)]

        ident = sb("ident", [128, 128])
        identb = sb("identb", [128, 128], BF16)
        causal = sb("causal", [128, 128], BF16)
        window = sb("window", [128, 128], BF16)
        masks = sb("masks", [128, 2, 128])
        rope_cs = sb("rope_cs", [128, 2, DH // 2])
        block_mask = sb("block_mask", [128, NB])
        past_neg = sb("past_neg", [128, NB])
        kv_rows = sb("kv_rows", [128, 2 * KV])
        cv_rows = sb("cv_rows", [128, KV])
        head_rows = sb("head_rows", [128, XH])
        head_sel = sb("head_sel", [XH, XH, 128], BF16)
        gather = sb("gather", [128, 4, 128])
        w_proj = sb("w_proj", [128, 2, PROJ])
        gate_bias = sb("gate_bias", [128, 96])
        w_out = sb("w_out", [128, 2, D])
        pos = sb("pos", [128, 2, HD])
        cb1 = sb("cb1", [128, 2])
        w2k = sb("w2k", [128, 248])
        b2k = sb("b2k", [1, 248])
        ones_row = sb("ones_row", [1, 128])
        w2v = sb("w2v", [128, DH])
        b2v = sb("b2v", [64, DH])
        mem_k = sb("mem_k", [128, 1])
        w_router = sb("w_router", [128, 2, E + 1])
        eps = sb("eps", [128, 1])

        X = sb("X", [128, B, D])
        stats = sb("stats", [128, B, 6])
        mean = sb("mean", [128, B])
        log_var = sb("log_var", [128, B])
        var_eps = sb("var_eps", [128, B])
        newton = sb("newton", [128, B])
        rstd = sb("rstd", [128, B])
        proj = sb("proj", [128, B, PROJ])
        gates = sb("gates", [128, B, 96])
        ck = sb("ck", [128, B, 2 * 72])
        cv = sb("cv", [72, B, HD])

        xn = sb("xn", [128, 2, D])
        xnT = sb("xnT", [128, 2, D])
        tiny = sb("tiny", [128, 32])
        tiny_used = [0]

        phase_memory()
        block_k = sb("block_k", [128, 2 * NT])
        w1_diag = sb("w1_diag", [128, 8, 1024])
        kv_pos = sb("kv_pos", [128, 2, 2, HD])
        hid = sb("hid", [128, 1024])
        hidT = sb("hidT", [128, 1024])
        hid_v = sb("hid_v", [128, 1024])
        cv_raw = sb("cv_raw", [72, B, DH])
        mem_diag = sb("mem_diag", [128, 2 * KV])

        w = {}

        def S(name):
            if name not in w:
                w[name] = sem(name)
            return w[name]

        def pairs_of_batches(engine):
            def run(body):
                body(0)
                with engine.Fori(1, B // 2) as i:
                    body(i)
            return run

        def settle(eng):
            c = tiny_used[0]
            tiny_used[0] += 1
            if eng is nc.vector:
                nc.vector.memset(tiny[:, c:c + 1], 0.0)
            else:
                nc.gpsimd.tensor_tensor(tiny[:, c:c + 1], ident[:, 0:1], ident[:, 0:1], ALU.add)

        def ln_stats_vector(dve, n):
            chain, past = S("ln_stat"), (n - 1) * (B + 6)
            with dve.Fori(0, B) as i:
                last = nc.vector.bn_stats(stats[:, ds(i, 1), :].rearrange("p a s -> p (a s)"),
                                          X[:, ds(i, 1), :].rearrange("p a d -> p (a d)"))
                last.then_inc(chain, 1)
            dve.wait_ge(chain, past + B)
            nc.vector.tensor_tensor(mean[:], stats[:, :, 1], stats[:, :, 4], ALU.add).then_inc(chain, 1)
            nc.vector.tensor_tensor(newton[:], stats[:, :, 1], stats[:, :, 4], ALU.subtract).then_inc(chain, 1)
            nc.vector.tensor_tensor(var_eps[:], stats[:, :, 2], stats[:, :, 5], ALU.add).then_inc(chain, 1)
            dve.wait_ge(chain, past + B + 3)
            nc.vector.tensor_scalar(mean[:], mean[:], 0.5, None, ALU.mult).then_inc(chain, 1)
            nc.vector.tensor_tensor(newton[:], newton[:], newton[:], ALU.mult).then_inc(chain, 1)
            nc.vector.tensor_scalar(var_eps[:], var_eps[:], 1.0 / D, EPS, ALU.mult, ALU.add).then_inc(chain, 1)
            dve.wait_ge(chain, past + B + 6)
            nc.vector.scalar_tensor_tensor(var_eps[:], newton[:], 0.25, var_eps[:], ALU.mult, ALU.add)\
                .then_inc(S("ln_var"), 1)
            dve.wait_ge(S("ln_guess"), 2 * n)
            c2, past = S("ln_newton"), (n - 1) * 3
            nc.vector.tensor_tensor(newton[:], rstd[:], rstd[:], ALU.mult).then_inc(c2, 1)
            dve.wait_ge(c2, past + 1)
            nc.vector.tensor_tensor(newton[:], newton[:], var_eps[:], ALU.mult).then_inc(c2, 1)
            dve.wait_ge(c2, past + 2)
            nc.vector.tensor_scalar(newton[:], newton[:], -0.5, 1.5, ALU.mult, ALU.add).then_inc(c2, 1)
            dve.wait_ge(c2, past + 3)
            nc.vector.tensor_tensor(rstd[:], rstd[:], newton[:], ALU.mult).then_inc(S("ln_done"), 1)
            dve.wait_ge(S("ln_done"), n)

        def ln_stats_scalar(act, n):
            act.wait_ge(S("ln_var"), n)
            nc.scalar.activation(log_var[:], var_eps[:], ACT.Ln).then_inc(S("ln_guess"), 1)
            act.wait_ge(S("ln_guess"), 2 * n - 1)
            nc.scalar.activation(rstd[:], log_var[:], ACT.Exp, scale=-0.5).then_inc(S("ln_guess"), 1)

        def normalise(out, b):
            return nc.vector.tensor_scalar(out, X[:, ds(b, 1), :].rearrange("p a d -> p (a d)"),
                                           mean[:, ds(b, 1)],
                                           rstd[:, ds(b, 1)], ALU.subtract, ALU.mult)

        def proj_vector(dve):
            nc.vector.memset(w2k[:], 0.0)
            nc.vector.memset(b2k[:], 0.0)
            nc.vector.memset(ones_row[:], 1.0)
            nc.vector.memset(w1_diag[:], 0.0).then_inc(S("zeroed"), 1)
            dve.wait_ge(S("ld_x"), 32)
            ln_stats_vector(dve, 1)
            dve.wait_ge(S("ld_first"), 64)
            @pairs_of_batches(dve)
            def _(i):
                for p in range(2):
                    b = 2 * i + p
                    dve.wait_ge(S("xT_done"), b)
                    normalise(xn[:, p, :], b).then_inc(S("xn_ready"), 1)
                for p in range(2):
                    b = 2 * i + p
                    dve.wait_ge(S("proj_kept"), b + 1)
                    dve.wait_ge(S("kvT_done"), b)
                    for n in range(2):
                        src = proj[:, ds(b, 1), (4 + n) * HD:(5 + n) * HD].to_broadcast([128, 2, HD])
                        add = pos[:, n:n + 1, :].to_broadcast([128, 2, HD])
                        last = nc.vector.tensor_tensor(kv_pos[:, n, :, :], src, add, ALU.add)
                    last.then_inc(S("kv_pos_ready"), 1)
                    dve.wait_ge(S("kvT_done"), b + 1)
                    for n in range(2):
                        col = n * NT + b * T
                        nc.vector.tensor_copy(block_k[0:64, ds(col, T)], bank[4 + 2 * p + n][0:64, 0:T])
                        last = nc.vector.tensor_copy(block_k[64:128, ds(col, T - 1)],
                                                     bank[4 + 2 * p + n][64:128, 1:T])
                    last.then_inc(S("block_k_ready"), 1)

        def proj_tensor(pe):
            pe.wait_ge(S("ld_first"), 64)

            def transposes(b, p):
                pe.wait_ge(S("xn_ready"), b + 1)
                pe.wait_ge(S("xnT_ready"), b)
                for c in range(2):
                    last = nc.tensor.transpose(bank[p][:, c * 128:c * 128 + 128], xn[:, p, c * 128:c * 128 + 128],
                                               ident[:])
                last.then_inc(S("xT_done"), 1)

            def project(b, p):
                pe.wait_ge(S("xnT_ready"), b + 1)
                pe.wait_ge(S("proj_kept"), b)
                for c in range(2):
                    last = nc.tensor.matmul(bank[2 + p][:, 0:PROJ], xnT[:, p, c * 128:c * 128 + 128],
                                            w_proj[:, c, :], start=c == 0, stop=c == 1)
                last.then_inc(S("proj_done"), 1)

            def kv_transposes(b, p):
                pe.wait_ge(S("kv_pos_ready"), b + 1)
                pe.wait_ge(S("block_k_ready"), b)
                for n in range(2):
                    last = nc.tensor.transpose(bank[4 + 2 * p + n][:, 0:T],
                                               kv_pos[:, n, :, :].rearrange("p a d -> p (a d)"), ident[:])
                last.then_inc(S("kvT_done"), 1)

            @pairs_of_batches(pe)
            def _(i):
                for p in range(2):
                    transposes(2 * i + p, p)
                for p in range(2):
                    project(2 * i + p, p)
                for p in range(2):
                    kv_transposes(2 * i + p, p)

        def proj_scalar(act):
            ln_stats_scalar(act, 1)
            @pairs_of_batches(act)
            def _(i):
                for p in range(2):
                    act.wait_ge(S("xT_done"), 2 * i + p + 1)
                    act.wait_ge(S("proj_done"), 2 * i + p)
                    nc.scalar.copy(xnT[:, p, :], bank[p][:, 0:D]).then_inc(S("xnT_ready"), 1)
                for p in range(2):
                    b = 2 * i + p
                    act.wait_ge(S("proj_done"), b + 1)
                    nc.scalar.copy(proj[:, ds(b, 1), :].rearrange("p a n -> p (a n)"),
                                   bank[2 + p][:, 0:PROJ]).then_inc(S("proj_kept"), 1)

        def comp_tensor(pe):
            pe.wait_ge(S("block_k_ready"), B)
            for n in range(2):
                pe.wait_ge(S("ld_w1k" if n == 0 else "ld_w1v"), 256)
                if n == 1:
                    pe.wait_ge(S("hid_kept"), 2)
                for half in range(2):
                    for i in range(8):
                        lhsT = block_k[:, n * NT + 2 * i:(n + 1) * NT:BLK]
                        last = nc.tensor.matmul(bank[half][:], lhsT, w1_diag[:, i, half * 512:half * 512 + 512],
                                                start=i == 0, stop=i == 7)
                last.then_inc(S("hidden_done"), 1)
                pe.wait_ge(S("hid_kept"), 2 * n + 2)
                if n == 1:
                    pe.wait_ge(S("hidT_kept"), 2)
                for kv in range(KV):
                    last = nc.tensor.transpose(bank[2 + kv // 4][:, kv % 4 * 128:kv % 4 * 128 + 128],
                                               hid[:, kv * 128:kv * 128 + 128], ident[:])
                last.then_inc(S("hidT_done"), 1)
            pe.wait_ge(S("ld_comp"), 11 * 16)
            pe.wait_ge(S("hidT_kept"), 4)
            for g2 in range(2):
                for kv in range(KV):
                    off = 120 - (g2 * HD + kv * DH)
                    o = bank[4 + 2 * g2 + kv // 4][:, kv % 4 * 128:kv % 4 * 128 + 128]
                    nc.tensor.matmul(o, w2k[:, off:off + 128], hidT[:, kv * 128:kv * 128 + 128],
                                     start=True, stop=False)
                    last = nc.tensor.matmul(o, b2k[:, off:off + 128], ones_row[:], start=False, stop=True)
            last.then_inc(S("ck_done"), 1)
            for b in range(B):
                last = nc.tensor.matmul(bank[0][0:64, b * DH:b * DH + DH], hid_v[:, b * 64:b * 64 + 64], w2v[:],
                                        start=True, stop=True)
            last.then_inc(S("cv_done"), 1)

        def comp_scalar(act):
            for n in range(2):
                act.wait_ge(S("hidden_done"), n + 1)
                if n == 1:
                    act.wait_ge(S("hidT_done"), 1)
                for half in range(2):
                    nc.scalar.copy(hid[:, half * 512:half * 512 + 512], bank[half][:]).then_inc(S("hid_kept"), 1)
                act.wait_ge(S("hidT_done"), n + 1)
                if n == 0:
                    act.wait_ge(S("ld_comp"), 11 * 16)
                for half in range(2):
                    if n == 0:
                        o = hidT[:, half * 512:half * 512 + 512]
                        src = bank[2 + half][:]
                    else:
                        o = hid_v[:, :].rearrange("p (b kv c) -> p kv b c", b=B, kv=KV)[:, half * 4:half * 4 + 4]
                        src = bank[2 + half][:].rearrange("p (kv b c) -> p kv b c", kv=4, b=B)
                    nc.scalar.activation(o, src, ACT.Relu, bias=cb1[:, n:n + 1]).then_inc(S("hidT_kept"), 1)
            act.wait_ge(S("gate_sum"), 1)
            nc.scalar.activation(gates[:], gates[:], ACT.Exp, scale=-1.0).then_inc(S("gate_exp"), 1)

        def comp_vector(dve):
            nc.vector.tensor_tensor(gates[:], proj[:, :, QKV:PROJ],
                                    gate_bias[:].rearrange("p (a n) -> p a n", a=1).to_broadcast([128, B, 96]),
                                    ALU.add).then_inc(S("gate_sum"), 1)
            dve.wait_ge(S("ld_comp"), 11 * 16)
            nc.vector.tensor_scalar(mem_diag[:], kv_rows[:], mem_k[:, 0:1], None, ALU.mult).then_inc(S("mem_diag_ok"), 1)
            dve.wait_ge(S("mem_diag_ok"), 1)
            ck5 = ck[:].rearrange("p b (g n) -> p b g n", g=2)
            for g2 in range(2):
                nc.vector.tensor_copy(ck5[:, :, g2, 64:72],
                                      mem_diag[:, g2 * KV:g2 * KV + KV].rearrange("p (a n) -> p a n", a=1)
                                      .to_broadcast([128, B, KV]))
            nc.vector.tensor_copy(cv_raw[64:72, 1:B, :], cv_raw[64:72, 0:1, :].to_broadcast([8, B - 1, DH]))
            dve.wait_ge(S("ck_done"), 1)
            for g2 in range(2):
                for half in range(2):
                    o = ck5[:, :, g2, half * 32:half * 32 + 32].rearrange("p b (kv c) -> p kv b c", kv=4)
                    last = nc.vector.tensor_copy(o, bank[4 + 2 * g2 + half][:]
                                                 .rearrange("p (kv b c) -> p kv b c", kv=4, b=B))
            last.then_inc(S("ck_ready"), 1)
            dve.wait_ge(S("cv_done"), 1)
            nc.vector.tensor_tensor(cv_raw[0:64], bank[0][0:64, 0:128].rearrange("p (b d) -> p b d", b=B),
                                    b2v[:].rearrange("p (a d) -> p a d", a=1).to_broadcast([64, B, DH]),
                                    ALU.add).then_inc(S("cv_raw_ok"), 1)
            dve.wait_ge(S("cv_raw_ok"), 1)
            o = cv[:].rearrange("p b (kv d) -> p b kv d", kv=KV)
            i0 = cv_raw[:].rearrange("p b (a d) -> p b a d", a=1).to_broadcast([72, B, KV, DH])
            i1 = cv_rows[0:72].rearrange("p (a kv c) -> p a kv c", a=1, c=1).to_broadcast([72, B, KV, DH])
            nc.vector.tensor_tensor(o, i0, i1, ALU.mult).then_inc(S("cv_ready"), 1)
            dve.wait_ge(S("gate_exp"), 1)
            nc.vector.tensor_scalar(gates[:], gates[:], 1.0, None, ALU.add).then_inc(S("gate_one"), 1)
            dve.wait_ge(S("gate_one"), 1)
            nc.vector.reciprocal(gates[:], gates[:]).then_inc(S("gates_ready"), 1)
            dve.wait_ge(S("gates_ready"), 1)

        phase_memory()
        probs = sb("probs", [128, 8, 512])
        raw = sb("raw", [128, (G + 1) * HD])
        rot = sb("rot", [128, (G + 1) * 2 * HD])
        rope_a = sb("rope_a", [128, 40, 4])
        rope_b = sb("rope_b", [128, 40, 4])
        query = [[sb(f"query{br}{p}", [128, 512], F32R) for p in range(2)] for br in range(2)]
        query_rest = [sb(f"query_rest{p}", [128, 512], F32R) for p in range(2)]
        key_diag = [sb(f"key_diag{p}", [128, KV, 128], F32R) for p in range(2)]
        key_rest = [sb(f"key_rest{p}", [128, KV, 128], F32R) for p in range(2)]
        key_parts = sb("key_parts", [128, 128], F32R)
        key_high = sb("key_high", [64, 128], F32R)
        part_rows = sb("part_rows", [128, KV])
        query_b = sb("query_b", [128, 512], BF16)
        key_b = sb("key_b", [128, KV, 128], BF16)
        rawT = sb("rawT", [128, 256])
        csim = sb("csim", [128, G, 72])
        cexp = sb("cexp", [128, G, 72])
        cprob = sb("cprob", [128, G, 72])
        cprobT = sb("cprobT", [72, 512])
        cmax = sb("cmax", [128, G, KV])
        csum = sb("csum", [128, G, KV])
        imp = sb("imp", [128, 72])
        impmax = sb("impmax", [128, KV])
        impe = sb("impe", [128, 72])
        impsum = sb("impsum", [128, KV])
        skip = sb("skip", [128, HD])
        blockmax = sb("blockmax", [128, G, KV, NB])
        farmax = sb("farmax", [128, G, KV])
        finemax = sb("finemax", [128, G, KV, NB])
        nearmax = sb("nearmax", [128, G, KV])
        rows = [sb(f"rows{br}", [128, G, 128]) for br in range(2)]
        value = [sb(f"value{p}", [128, KV, 32]) for p in range(2)]
        pv = sb("pv", [128, 2, 512])
        weight = sb("weight", [128, G, 4])
        part = sb("part", [128, G, 4, DH])
        attn = [sb(f"attn{p}", [128, G, KV, DH]) for p in range(2)]
        attnT = sb("attnT", [128, 256])

        SMAX = [bank[0], bank[1]]
        SCORE = [bank[2], bank[3]]
        PV = [bank[4], bank[5]]
        T0, T1 = bank[6], bank[7]
        BR = [0, 1, 0, 1]
        HALF = [0, 0, 1, 1]

        COMP_AT, ROWS_AT = 11, 14

        def halves(engine, half_body, tail, lead=1):
            for b in range(lead):
                half_body(b, b % 2, b > 0, True, None)
            with engine.Fori(0, (B - 1 - lead) // 2) as i:
                half_body(2 * i + lead, 1, True, True, i)
                half_body(2 * i + lead + 1, 0, True, True, i)
            half_body(B - 1, 1, True, False, None)
            tail(B - 1, 1)

        key_rows = probs[64:128, 0:2, :].rearrange("p a (kv k) -> p (a kv) k", k=128)

        def attn_tensor(pe):
            def qk_transposes(b):
                pe.wait_ge(S("rot_ready"), b + 1)
                if not isinstance(b, int) or b > 1:
                    pe.wait_ge(S("part_ready"), 4 * b - 5)
                for c in range(2):
                    nc.tensor.transpose(T1[:, 128 + c * 128:256 + c * 128], raw[:, c * 128:c * 128 + 128], ident[:])
                nc.tensor.transpose(T1[:, 0:128], rot[:, G * 128:(G + 1) * 128], ident[:]).then_inc(S("rawT_done"), 1)
                for g in range(G):
                    last = nc.tensor.transpose(T0[:, g * 128:g * 128 + 128], rot[:, g * 128:g * 128 + 128], ident[:])
                last.then_inc(S("rqT_done"), 1)

            def block_scores(b):
                pe.wait_ge(S("rawT_ready"), b + 1)
                for c in range(2):
                    last = nc.tensor.matmul(T1[:, c * 144:c * 144 + 144], rawT[:, c * 128:c * 128 + 128],
                                            ck[:, ds(b, 1), :].rearrange("p a n -> p (a n)"), start=True, stop=True)
                last.then_inc(S("csim_done"), 1)

            def max_scores(b, m):
                if m == 0:
                    pe.wait_ge(S("query_b_ready"), b + 1)
                    pe.wait_ge(S("key_b_ready"), b + 1)
                pe.wait_ge(S(f"smax_read{m % 2}"), 6 * b + m // 2)
                g, half = (m // 2, m % 2) if m < 8 else (m - 8, 0)
                kvs, keys = (slice(half * 4, half * 4 + 4), 128) if m < 8 else (slice(0, 8), 64)
                out = SMAX[m % 2][:, :].rearrange("p (h k) -> p h k", k=keys)
                nc.tensor.matmul(out, query_b[:, g * 128:g * 128 + 128], key_b[:, kvs, 0:keys], start=True, stop=False)
                mask = (causal if m < 8 else window)[:, 0:keys].rearrange("p (a k) -> p a k", a=1)
                nc.tensor.matmul(out, identb[:], mask.to_broadcast([128, 512 // keys, keys]), start=False,
                                 stop=True).then_inc(S("smax_done"), 1)

            def row_transposes(b):
                pe.wait_ge(S("query_rest_ready"), b + 1)
                if not isinstance(b, int) or b > 0:
                    pe.wait_ge(S("part_ready"), 4 * b - 2)
                pe.wait_ge(S("cout_kept"), b + 1)
                for br in range(2):
                    pe.wait_ge(S(f"rows_ready{br}"), b + 1)
                    for g in range(G):
                        last = nc.tensor.transpose((T0, T1)[br][:, g * 128:g * 128 + 128], rows[br][:, g, :], ident[:])
                    last.then_inc(S(f"rowsT_done{br}"), 1)

            def comp_transposes(b):
                pe.wait_ge(S("cprob_ready"), b + 1)
                if not isinstance(b, int) or b > 1:
                    pe.wait_ge(S("attnT_ready"), b - 1)
                for g in range(G):
                    last = nc.tensor.transpose(T1[0:72, g * 128:g * 128 + 128], cprob[:, g, :], ident[:])
                last.then_inc(S("cprobT_done"), 1)

            def comp_values(b):
                pe.wait_ge(S("cprobT_ready"), b + 1)
                for g in range(G):
                    last = nc.tensor.matmul(T1[:, g * HD:g * HD + HD], cprobT[:, g * 128:g * 128 + 128],
                                            cv[:, ds(b, 1), :].rearrange("p a n -> p (a n)"), start=True, stop=True)
                last.then_inc(S("cout_done"), 1)

            def score(b, p, u):
                gr, kv = u // 4, HALF[u // 4] * 4 + u % 4
                if u == 0:
                    pe.wait_ge(S("rows_kept0"), b + 1)
                    pe.wait_ge(S("rows_kept1"), b + 1)
                    pe.wait_ge(S("query_rest_ready"), b + 1)
                    pe.wait_ge(S("key_rest_ready"), b + 1)
                pe.wait_ge(S(f"prob_ready{u % 2}"), 8 * b + u // 2)
                nc.tensor.matmul(SCORE[u % 2][:], key_diag[p][:, kv, :], query[BR[gr]][p][:], start=True, stop=False)
                nc.tensor.matmul(SCORE[u % 2][:], key_rest[p][:, kv, :], query_rest[p][:], start=False, stop=False)
                eye = identb[:].rearrange("p (a k) -> p a k", a=1).to_broadcast([128, G, 128])
                nc.tensor.matmul(SCORE[u % 2][:].rearrange("p (g t) -> p g t", g=G), (causal, window)[BR[gr]][:], eye,
                                 start=False, stop=True).then_inc(S("score_done"), 1)

            def values(b, p, gr):
                if gr == 0:
                    pe.wait_ge(S("value_ready"), b + 1)
                for j in range(4):
                    u = gr * 4 + j
                    pe.wait_ge(S(f"prob_ready{u % 2}"), 8 * b + u // 2 + 1)
                pe.wait_ge(S(f"pv_kept{gr % 2}"), 2 * b + gr // 2)
                for j in range(4):
                    u = gr * 4 + j
                    last = nc.tensor.matmul(PV[gr % 2][32 * j:32 * j + 32, :], value[p][:, HALF[gr] * 4 + j, :],
                                            probs[:, u % 8, :], start=True, stop=True)
                last.then_inc(S("pv_done"), 1)

            def pv_transposes(b, gr):
                pe.wait_ge(S(f"pv_kept{gr % 2}"), 2 * b + gr // 2 + 1)
                if gr == 0:
                    pe.wait_ge(S("attn_added"), b)
                    if not isinstance(b, int) or b < B - 1:
                        pe.wait_ge(S("query_rest_ready"), b + 2)
                elif gr == 2 and (not isinstance(b, int) or b < B - 1):
                    pe.wait_ge(S("rows_kept0"), b + 2)
                elif gr == 3 and (not isinstance(b, int) or b < B - 2):
                    pe.wait_ge(S("query_rest_ready"), b + 3)
                else:
                    pe.wait_ge(S("part_ready"), 4 * b + gr)
                for g in range(G):
                    last = nc.tensor.transpose(T0[:, g * 128:g * 128 + 128], pv[:, gr % 2, g * 128:g * 128 + 128],
                                               ident[:])
                last.then_inc(S("pvT_done"), 1)

            def out_transposes(b, p):
                pe.wait_ge(S("attn_ready"), b + 1)
                if not isinstance(b, int) or b < B - 2:
                    pe.wait_ge(S("csim_kept"), b + 3)
                a = attn[p][:].rearrange("p g kv d -> p (g kv d)")
                for c in range(2):
                    last = nc.tensor.transpose(T1[:, c * 128:c * 128 + 128], a[:, c * 128:c * 128 + 128], ident[:])
                last.then_inc(S("attnT_done"), 1)

            def out_project(b):
                pe.wait_ge(S("attnT_ready"), b + 1)
                pe.wait_ge(S("part_ready"), 4 * b + 4)
                for c in range(2):
                    last = nc.tensor.matmul(T0[:, 0:D], attnT[:, c * 128:c * 128 + 128], w_out[:, c, :],
                                            start=c == 0, stop=c == 1)
                last.then_inc(S("out_done"), 1)

            def half_body(b, p, previous, following, i):
                for u in range(16):
                    score(b, p, u)
                    if u == 1:
                        if previous:
                            values(b - 1, 1 - p, 3)
                        if following:
                            qk_transposes(b + 1)
                    if u == 2 and previous:
                        pv_transposes(b - 1, 3)
                    if u == 3 and following:
                        block_scores(b + 1)
                    if u == 4 and previous:
                        out_transposes(b - 1, 1 - p)
                    if following and 4 <= u < 10:
                        max_scores(b + 1, 2 * (u - 4))
                        max_scores(b + 1, 2 * (u - 4) + 1)
                    if u == 6 and previous:
                        out_project(b - 1)
                    if u in (5, 9, 13):
                        values(b, p, (u - 5) // 4)
                    if following and u == ROWS_AT:
                        row_transposes(b + 1)
                    if u in (7, 11, 15):
                        pv_transposes(b, (u - 7) // 4)
                    if following and u == COMP_AT:
                        comp_transposes(b + 1)
                    if following and u == COMP_AT + 1:
                        comp_values(b + 1)

            def tail(b, p):
                values(b, p, 3)
                pv_transposes(b, 3)
                out_transposes(b, p)
                out_project(b)

            pe.wait_ge(S("ld_attn"), 5 * 16)
            pe.wait_ge(S("attn_zeroed"), 1)
            pe.wait_ge(S("masks_ready"), 1)
            pe.wait_ge(S("ck_ready"), 1)
            pe.wait_ge(S("cv_ready"), 1)
            qk_transposes(0)
            block_scores(0)
            for m in range(12):
                max_scores(0, m)
            comp_transposes(0)
            comp_values(0)
            row_transposes(0)
            halves(pe, half_body, tail)

        def attn_scalar(act):
            def after_qk(b, p):
                act.wait_ge(S("rqT_done"), b + 1)
                nc.scalar.copy(query_b[0:64, :], T0[0:64, :]).then_inc(S("query_b_ready"), 1)
                nc.scalar.copy(query_rest[p][:], T0[:]).then_inc(S("query_high_ready"), 1)
                act.wait_ge(S("key_parts_ready"), b + 1)
                nc.scalar.copy(rawT[:], T1[:, 128:384]).then_inc(S("rawT_ready"), 1)
                act.wait_ge(S("query_high_ready"), b + 1)
                for br in range(2):
                    nc.scalar.copy(query[br][p][0:64, :], query_rest[p][0:64, :])

            def comp_exp(b):
                act.wait_ge(S("cexp_in"), b + 1)
                nc.scalar.activation(cexp[:], cexp[:], ACT.Exp, scale=SCALE).then_inc(S("cexp_done"), 1)
                act.wait_ge(S("impe_in"), b + 1)
                nc.scalar.activation(impe[:], impe[:], ACT.Exp, scale=SCALE / G).then_inc(S("impe_done"), 1)

            def comp_keep(b):
                act.wait_ge(S("cprobT_done"), b + 1)
                nc.scalar.copy(cprobT[:], T1[0:72, :]).then_inc(S("cprobT_ready"), 1)

            def rows_keep(b, p):
                for br in range(2):
                    act.wait_ge(S(f"rowsT_done{br}"), b + 1)
                    nc.scalar.copy(query[br][p][64:128, :], (T0, T1)[br][64:128, :])\
                        .then_inc(S(f"rows_kept{br}"), 1)

            def softmax(b, u):
                act.wait_ge(S("score_done"), 16 * b + u + 1)
                if not (isinstance(b, int) and b == 0 and u < 8):
                    act.wait_ge(S("pv_done"), 4 * b + u // 4 - 1)
                nc.scalar.activation(probs[:, u % 8, :], SCORE[u % 2][:], ACT.Exp, scale=SCALE)\
                    .then_inc(S(f"prob_ready{u % 2}"), 1)

            def pv_keep(b, gr):
                act.wait_ge(S("pv_done"), 4 * b + gr + 1)
                nc.scalar.copy(pv[:, gr % 2, :], PV[gr % 2][:]).then_inc(S(f"pv_kept{gr % 2}"), 1)

            def out_keep(b):
                act.wait_ge(S("attnT_done"), b + 1)
                nc.scalar.copy(attnT[:], T1[:, 0:256]).then_inc(S("attnT_ready"), 1)

            def half_body(b, p, previous, following, i):
                for u in range(16):
                    softmax(b, u)
                    if u == 1:
                        if previous:
                            pv_keep(b - 1, 3)
                        if following:
                            after_qk(b + 1, 1 - p)
                    if u == 5 and previous:
                        out_keep(b - 1)
                    if u in (6, 10, 14):
                        pv_keep(b, (u - 6) // 4)
                    if following and u == 8:
                        comp_exp(b + 1)
                    if following and u == COMP_AT:
                        comp_keep(b + 1)
                    if following and u == ROWS_AT:
                        rows_keep(b + 1, 1 - p)

            def tail(b, p):
                pv_keep(b, 3)
                out_keep(b)

            act.wait_ge(S("attn_zeroed"), 1)
            after_qk(0, 0)
            comp_exp(0)
            comp_keep(0)
            rows_keep(0, 0)
            halves(act, half_body, tail)

        def attn_vector(dve):
            chain = Tally(S("attn_chain"))

            def link(ins):
                ins.then_inc(chain.sem, 1)
                chain.add(1)
                dve.wait_ge(chain.sem, chain.value())

            def gkc(ap, n):
                return ap.rearrange("p g (kv c) -> p g kv c", c=n)

            def keys(b, p):
                dve.wait_ge(S("rawT_done"), b + 1)
                nc.vector.tensor_copy(key_parts[64:128], T1[64:128, 0:128])
                link(nc.vector.tensor_copy(key_high[:], T1[0:64, 0:128]))
                nc.vector.tensor_tensor(key_parts[0:64], T1[0:64, 0:128], key_high[:], ALU.subtract)\
                    .then_inc(S("key_parts_ready"), 1)
                src = key_high[:].rearrange("p (a k) -> p a k", a=1).to_broadcast([64, KV, 128])
                m = kv_rows[0:64, 0:KV].rearrange("p (kv a) -> p kv a", a=1).to_broadcast([64, KV, 128])
                nc.vector.tensor_tensor(key_diag[p][0:64], src, m, ALU.mult).then_inc(S("key_diag_ready"), 1)
                dve.wait_ge(S("query_high_ready"), b + 1)
                nc.vector.tensor_tensor(query_rest[p][64:128], T0[64:128, :], query_rest[p][64:128], ALU.subtract)\
                    .then_inc(S("query_rest_ready"), 1)
                dve.wait_ge(S("key_parts_ready"), b + 1)
                src = key_parts[:].rearrange("p (a k) -> p a k", a=1).to_broadcast([128, KV, 128])
                m = part_rows[:].rearrange("p (kv a) -> p kv a", a=1).to_broadcast([128, KV, 128])
                nc.vector.tensor_tensor(key_rest[p][:], src, m, ALU.mult).then_inc(S("key_rest_ready"), 1)

            def comp_softmax(b):
                dve.wait_ge(S("csim_done"), b + 1)
                s = T1[:, 0:288].rearrange("p (g n) -> p g n", g=G)
                for g in range(G):
                    nc.vector.tensor_tensor(csim[:, g, 0:64].rearrange("p (kv c) -> p kv c", c=NB),
                                            s[:, g, 0:64].rearrange("p (kv c) -> p kv c", c=NB),
                                            block_mask[:].rearrange("p (a c) -> p a c", a=1)
                                            .to_broadcast([128, KV, NB]), ALU.add)
                nc.vector.tensor_copy(csim[:, :, 64:72], s[:, :, 64:72]).then_inc(S("csim_kept"), 1)
                dve.wait_ge(S("csim_kept"), b + 1)
                cs, ce = gkc(csim[:, :, 0:64], NB), gkc(cexp[:, :, 0:64], NB)
                link(nc.vector.tensor_reduce(cmax[:], cs, AX, ALU.max))
                link(nc.vector.tensor_tensor(cmax[:], cmax[:], csim[:, :, 64:72], ALU.max))
                mb = cmax[:].rearrange("p g (kv a) -> p g kv a", a=1).to_broadcast([128, G, KV, NB])
                nc.vector.tensor_tensor(ce, cs, mb, ALU.subtract)
                nc.vector.tensor_tensor(cexp[:, :, 64:72], csim[:, :, 64:72], cmax[:], ALU.subtract)\
                    .then_inc(S("cexp_in"), 1)
                link(nc.vector.tensor_reduce(imp[:, 0:64], csim[:, :, 0:64].rearrange("p g n -> p n g"), AX, ALU.add))
                im = imp[:, 0:64].rearrange("p (kv c) -> p kv c", c=NB)
                link(nc.vector.tensor_reduce(impmax[:], im, AX, ALU.max))
                link(nc.vector.tensor_scalar(impmax[:], impmax[:], NO_BLOCK, None, ALU.max))
                nc.vector.tensor_scalar(impe[:, 64:72], impmax[:], -1.0, NO_BLOCK, ALU.mult, ALU.add)
                ib = impmax[:].rearrange("p (kv a) -> p kv a", a=1).to_broadcast([128, KV, NB])
                nc.vector.tensor_tensor(impe[:, 0:64].rearrange("p (kv c) -> p kv c", c=NB), im, ib,
                                        ALU.subtract).then_inc(S("impe_in"), 1)

            def comp_weights(b):
                dve.wait_ge(S("cexp_done"), b + 1)
                ce = gkc(cexp[:, :, 0:64], NB)
                link(nc.vector.tensor_reduce(csum[:], ce, AX, ALU.add))
                link(nc.vector.tensor_tensor(csum[:], csum[:], cexp[:, :, 64:72], ALU.add))
                link(nc.vector.reciprocal(csum[:], csum[:]))
                gt = gates[:, ds(b, 1), 0:32].rearrange("p a (g kv) -> p (a g) kv", g=G)
                link(nc.vector.tensor_tensor(csum[:], csum[:], gt, ALU.mult))
                dve.wait_ge(S("cprobT_done"), b)
                sbc = csum[:].rearrange("p g (kv a) -> p g kv a", a=1).to_broadcast([128, G, KV, NB])
                nc.vector.tensor_tensor(gkc(cprob[:, :, 0:64], NB), ce, sbc, ALU.mult)
                nc.vector.tensor_tensor(cprob[:, :, 64:72], cexp[:, :, 64:72], csum[:], ALU.mult)\
                    .then_inc(S("cprob_ready"), 1)
                dve.wait_ge(S("impe_done"), b + 1)
                ie = impe[:, 0:64].rearrange("p (kv c) -> p kv c", c=NB)
                link(nc.vector.tensor_reduce(impsum[:], ie, AX, ALU.add))
                link(nc.vector.tensor_tensor(impsum[:], impsum[:], impe[:, 64:72], ALU.add))
                link(nc.vector.tensor_scalar(impsum[:], impsum[:], 1e-10, None, ALU.mult))
                th = impsum[:].rearrange("p (kv a) -> p kv a", a=1).to_broadcast([128, KV, NB])
                sk = skip[:].rearrange("p (kv c) -> p kv c", c=NB)
                link(nc.vector.tensor_tensor(sk, ie, th, ALU.is_le))
                pn = past_neg[:].rearrange("p (a c) -> p a c", a=1).to_broadcast([128, KV, NB])
                link(nc.vector.tensor_tensor(sk, sk, pn, ALU.mult))

            def reduce_max(b, m):
                dve.wait_ge(S("smax_done"), 12 * b + m + 1)
                if m < 8:
                    g, half = m // 2, m % 2
                    src = SMAX[m % 2][:].rearrange("p (h c k) -> p h c k", h=4, k=BLK)
                    ins = nc.vector.tensor_reduce(blockmax[:, g, half * 4:half * 4 + 4, :], src, AX, ALU.max)
                else:
                    src = SMAX[m % 2][:].rearrange("p (h k) -> p h k", k=64)
                    ins = nc.vector.tensor_reduce(farmax[:, m - 8, :], src, AX, ALU.max)
                ins.then_inc(S(f"smax_read{m % 2}"), 1)

            def maxima(b):
                for n in range(2):
                    dve.wait_ge(S(f"smax_read{n}"), 6 * b + 6)
                sk = skip[:].rearrange("p (kv c) -> p kv c", c=NB)
                for g in range(G):
                    last = nc.vector.tensor_tensor(finemax[:, g], blockmax[:, g], sk, ALU.add)
                link(last)
                dve.wait_ge(S("rowsT_done0"), b)
                dve.wait_ge(S("rowsT_done1"), b)
                nc.vector.tensor_reduce(rows[0][:, :, 120:128], finemax[:], AX, ALU.max)
                nc.vector.tensor_copy(rows[0][:, :, 64:120].rearrange("p g (kv c) -> p g kv c", c=7),
                                      sk[:, :, 0:7].rearrange("p (a kv) c -> p a kv c", a=1)
                                      .to_broadcast([128, G, KV, 7])).then_inc(S("rows_ready0"), 1)
                link(nc.vector.tensor_reduce(nearmax[:], blockmax[:, :, :, 4:8], AX, ALU.max))
                nc.vector.tensor_tensor(rows[1][:, :, 120:128], nearmax[:], farmax[:], ALU.max)\
                    .then_inc(S("rows_ready1"), 1)

            def comp_out(b, p):
                dve.wait_ge(S("cout_done"), b + 1)
                if not isinstance(b, int) or b > 1:
                    dve.wait_ge(S("attnT_done"), b - 1)
                nc.vector.tensor_copy(attn[p][:].rearrange("p g kv d -> p (g kv d)"), T1[:, 0:256])\
                    .then_inc(S("cout_kept"), 1)

            def add_branch(b, p, gr):
                dve.wait_ge(S("pvT_done"), 4 * b + gr + 1)
                src = T0[:].rearrange("p (g kv c) -> p g kv c", g=G, c=32)
                link(nc.vector.reciprocal(weight[:], src[:, :, :, DH]))
                k0 = 32 + 32 * BR[gr]
                gt = gates[:, ds(b, 1), k0:k0 + 32].rearrange("p a (g kv) -> p (a g) kv", g=G)
                link(nc.vector.tensor_tensor(weight[:], weight[:], gt[:, :, HALF[gr] * 4:HALF[gr] * 4 + 4], ALU.mult))
                wb = weight[:].rearrange("p g (kv a) -> p g kv a", a=1).to_broadcast([128, G, 4, DH])
                nc.vector.tensor_tensor(part[:], src[:, :, :, 0:DH], wb, ALU.mult).then_inc(S("part_ready"), 1)
                dve.wait_ge(S("part_ready"), 4 * b + gr + 1)
                if gr == 0:
                    dve.wait_ge(S("cout_kept"), b + 1)
                a = attn[p][:, :, HALF[gr] * 4:HALF[gr] * 4 + 4, :]
                ins = nc.vector.tensor_tensor(a, a, part[:], ALU.add)
                if gr == 3:
                    ins.then_inc(S("attn_ready"), 1)
                else:
                    link(ins)

            def residual(b):
                dve.wait_ge(S("out_done"), b + 1)
                x = X[:, ds(b, 1), :].rearrange("p a d -> p (a d)")
                nc.vector.tensor_tensor(x, x, T0[:, 0:D], ALU.add).then_inc(S("attn_added"), 1)

            def half_body(b, p, previous, following, i):
                if i is not None and p == 1:
                    chain.begin(i, CHAIN_ATTN)
                for u in range(16):
                    if u == 1 and following:
                        keys(b + 1, 1 - p)
                    if u == 2 and previous:
                        add_branch(b - 1, 1 - p, 3)
                    if u == 3 and following:
                        comp_softmax(b + 1)
                    if following and 4 <= u < 10:
                        reduce_max(b + 1, 2 * (u - 4))
                        reduce_max(b + 1, 2 * (u - 4) + 1)
                    if u == 6 and previous:
                        residual(b - 1)
                    if u in (7, 11, 15):
                        add_branch(b, p, (u - 7) // 4)
                    if following and u == 9:
                        comp_weights(b + 1)
                        maxima(b + 1)
                    if following and u == COMP_AT + 1:
                        comp_out(b + 1, 1 - p)
                if i is not None and p == 0:
                    chain.end(7, "CHAIN_ATTN")

            def tail(b, p):
                add_branch(b, p, 3)
                residual(b)

            for br in range(2):
                nc.vector.memset(rows[br][:], 0.0)
            for p in range(2):
                nc.vector.memset(value[p][:], 0.0)
            nc.vector.memset(query_b[64:128], 0.0)
            link(nc.vector.memset(key_b[64:128], 0.0))
            nc.vector.memset(value[0][:, :, DH:DH + 1], 1.0)
            nc.vector.memset(value[1][:, :, DH:DH + 1], 1.0).then_inc(S("attn_zeroed"), 1)
            dve.wait_ge(S("ld_attn"), 5 * 16)
            nc.vector.tensor_copy(identb[:], ident[:])
            nc.vector.tensor_copy(causal[:], masks[:, 0, :])
            nc.vector.tensor_copy(window[:], masks[:, 1, :]).then_inc(S("masks_ready"), 1)
            nc.vector.tensor_tensor(part_rows[:], kv_rows[:, 0:KV], kv_rows[:, KV:2 * KV], ALU.add)\
                .then_inc(S("part_rows_ready"), 1)
            dve.wait_ge(S("ld_key_rows"), 16)
            for p in range(2):
                nc.vector.tensor_copy(key_diag[p][64:128], key_rows)
            dve.wait_ge(S("part_rows_ready"), 1)
            keys(0, 0)
            comp_softmax(0)
            for m in range(12):
                reduce_max(0, m)
            comp_weights(0)
            maxima(0)
            comp_out(0, 0)
            halves(dve, half_body, tail)

        def attn_pool(pool):
            chain = Tally(S("rope_chain"))

            def link(ins):
                ins.then_inc(chain.sem, 1)
                chain.add(1)
                pool.wait_ge(chain.sem, chain.value())

            def rotate(b):
                pool.wait_ge(S("rqT_done"), b)
                pool.wait_ge(S("rawT_done"), b)
                settle(nc.gpsimd)
                nc.gpsimd.tensor_copy(raw[:], proj[:, ds(b, 1), 0:(G + 1) * HD].rearrange("p a n -> p (a n)"))\
                    .then_inc(S("raw_ready"), 1)
                pool.wait_ge(S("raw_ready"), b + 1)
                x = raw[:].rearrange("p (h d two) -> p h d two", d=4, two=2)
                o = rot[:].rearrange("p (g r h two) -> p g r h two", g=G + 1, r=2, two=2)

                def grouped(ap):
                    return ap.rearrange("p (g h) d -> p g (h d)", g=G + 1)
                cos = rope_cs[:, 0:1, :].to_broadcast([128, 40, 4])
                sin = rope_cs[:, 1:2, :].to_broadcast([128, 40, 4])
                nc.gpsimd.tensor_tensor(rope_a[:], x[:, :, :, 0], cos, ALU.mult)
                link(nc.gpsimd.tensor_tensor(rope_b[:], x[:, :, :, 1], sin, ALU.mult))
                link(nc.gpsimd.tensor_tensor(o[:, :, 0, :, 0], grouped(rope_a[:]), grouped(rope_b[:]), ALU.subtract))
                nc.gpsimd.tensor_tensor(rope_a[:], x[:, :, :, 0], sin, ALU.mult)
                link(nc.gpsimd.tensor_tensor(rope_b[:], x[:, :, :, 1], cos, ALU.mult))
                link(nc.gpsimd.tensor_tensor(o[:, :, 0, :, 1], grouped(rope_a[:]), grouped(rope_b[:]), ALU.add))
                twice = rot[:].rearrange("p (g r n) -> p g r n", g=G + 1, r=2)
                settle(nc.gpsimd)
                nc.gpsimd.tensor_copy(twice[:, :, 1, :], twice[:, :, 0, :]).then_inc(S("rot_ready"), 1)

            def narrow_keys(b, p):
                pool.wait_ge(S("key_diag_ready"), b + 1)
                settle(nc.gpsimd)
                nc.gpsimd.tensor_copy(key_b[0:64], key_diag[p][0:64]).then_inc(S("key_b_ready"), 1)

            def take_values(b, p):
                if not isinstance(b, int) or b > 1:
                    pool.wait_ge(S("pv_done"), 4 * b - 3)
                src = proj[:, ds(b, 1), (G + 1) * HD:QKV].rearrange("p a (kv d) -> p (a kv) d", d=DH)
                settle(nc.gpsimd)
                nc.gpsimd.tensor_copy(value[p][:, :, 0:DH], src).then_inc(S("value_ready"), 1)

            pool.wait_ge(S("attn_zeroed"), 1)
            pool.wait_ge(S("ld_first"), 64)
            pool.wait_ge(S("ld_attn"), 5 * 16)
            pool.wait_ge(S("proj_kept"), B)
            rotate(0)
            narrow_keys(0, 0)

            def half_body(b, p, previous, following, i):
                if i is not None and p == 1:
                    chain.begin(i, 8)
                take_values(b, p)
                if following:
                    rotate(b + 1)
                    narrow_keys(b + 1, 1 - p)
                if i is not None and p == 0:
                    chain.end(7, "rope_chain")

            halves(pool, half_body, lambda b, p: None)

        phase_memory()
        probs4 = sb("probs4", [128, 8, 512])
        head_sel_f = sb("head_sel_f", [XH, XH, 128])
        xq = [sb(f"xq{p}", [128, D]) for p in range(2)]
        xdiag = [sb(f"xdiag{p}", [128, XH, D]) for p in range(2)]
        xq_b = sb("xq_b", [128, D], BF16)
        xdiag_b = sb("xdiag_b", [128, XH, D], BF16)
        ctx_in = [sb(f"ctx_in{p}", [128, D]) for p in range(2)]
        xvalue = [sb(f"xvalue{p}", [128, 2, XH, 32]) for p in range(2)]
        xmax = sb("xmax", [128, 2, XH])
        xshift = [sb(f"xshift{p}", [XH, D], BF16) for p in range(2)]
        xpv = sb("xpv", [128, 512])
        xden = sb("xden", [128, D])
        xout = sb("xout", [128, D])

        def cross_loads(sp):
            with sp.Fori(0, (B - 2) // 2) as i:
                for p in range(2):
                    b = 2 * i + p
                    sp.wait_ge(S("xdiag_ready"), b + 1)
                    sp.wait_ge(S("ctxT_done"), b + 1)
                    sp.dma_start(ctx_in[p][:], io["ctx_2048"][ds(b + 2, 1)].rearrange("a t d -> (a t) d"))\
                        .then_inc(S(f"ld_ctx{p}"), 16)

        def ctx_loaded(eng, b, p):
            eng.wait_ge(S(f"ld_ctx{p}"), 8 * (b - p) + 16)

        def cross_tensor(pe):
            def ctx_transposes(b, p):
                ctx_loaded(pe, b, p)
                for c in range(2):
                    last = nc.tensor.transpose(T0[:, c * 128:c * 128 + 128], ctx_in[p][:, c * 128:c * 128 + 128],
                                               ident[:])
                last.then_inc(S("ctxT_done"), 1)

            def max_scores(b, m):
                if m == 0:
                    pe.wait_ge(S("xq_b_ready"), b + 1)
                    pe.wait_ge(S("xdiag_b_ready"), b + 1)
                pe.wait_ge(S(f"xmax_read{m % 2}"), 4 * b + m // 2)
                hs = 2 * (m % 4)
                nc.tensor.matmul(SMAX[m % 2][:].rearrange("p (h n) -> p h n", h=2),
                                 xq_b[:, m // 4 * 128:m // 4 * 128 + 128], xdiag_b[:, hs:hs + 2, :],
                                 start=True, stop=True).then_inc(S("xmax_scored"), 1)

            def shift_transposes(b):
                pe.wait_ge(S("xvalue_ready"), b + 1)
                pe.wait_ge(S("xmax_read0"), 4 * b + 4)
                pe.wait_ge(S("xmax_read1"), 4 * b + 4)
                for c in range(2):
                    last = nc.tensor.transpose(T0[0:XH, c * 128:c * 128 + 128], xmax[:, c, :], ident[:])
                last.then_inc(S("xmaxT_done"), 1)

            def score(b, p, h):
                if h == 0:
                    pe.wait_ge(S("xshift_ready"), b + 1)
                    pe.wait_ge(S("xdiag_ready"), b + 1)
                pe.wait_ge(S(f"xprob_ready{h % 2}"), 4 * b + h // 2)
                out = SCORE[h % 2]
                for c in range(2):
                    o = out[:, c * D:c * D + D]
                    nc.tensor.matmul(o, head_sel[:, h, :], xshift[p][:], start=True, stop=False)
                    last = nc.tensor.matmul(o, xdiag[p][:, h, c * 128:c * 128 + 128], xq[p][:], start=False, stop=True)
                last.then_inc(S("xscore_done"), 1)

            def values(b, p, gr):
                pe.wait_ge(S("xprob_ready0"), 4 * b + 2 * gr + 2)
                pe.wait_ge(S("xprob_ready1"), 4 * b + 2 * gr + 2)
                pe.wait_ge(S(f"xpv_kept{gr}"), b)
                for c in range(2):
                    for j in range(4):
                        last = nc.tensor.matmul(PV[gr][32 * j:32 * j + 32, 0:D], xvalue[p][:, c, gr * 4 + j, :],
                                                probs4[:, gr * 4 + j, c * D:c * D + D], start=c == 0, stop=c == 1)
                last.then_inc(S("xpv_done"), 1)

            def gather_rows(b):
                pe.wait_ge(S("xpv_kept1"), b + 1)
                pe.wait_ge(S("xadded"), b)
                for n in range(2):
                    for gr in range(2):
                        last = nc.tensor.matmul(T1[:, n * D:n * D + D], gather[:, 2 * n + gr, :],
                                                xpv[:, gr * D:gr * D + D], start=gr == 0, stop=gr == 1)
                last.then_inc(S("xgathered"), 1)

            def half_body(b, p, previous, following, i):
                for h in range(XH):
                    score(b, p, h)
                    if h == 1 and previous:
                        values(b - 1, 1 - p, 1)
                    if h == 3 and previous:
                        gather_rows(b - 1)
                    if h == 5:
                        values(b, p, 0)
                    if following:
                        if h == 1:
                            ctx_transposes(b + 1, 1 - p)
                        if 2 <= h < 6:
                            max_scores(b + 1, 2 * (h - 2))
                            max_scores(b + 1, 2 * (h - 2) + 1)
                        if h == 7:
                            shift_transposes(b + 1)

            def tail(b, p):
                values(b, p, 1)
                gather_rows(b)

            pe.wait_ge(S("cross_zeroed"), 1)
            pe.wait_ge(S("ld_cross"), 48)
            pe.wait_ge(S("attn_added"), B)
            ctx_transposes(0, 0)
            for m in range(8):
                max_scores(0, m)
            shift_transposes(0)
            halves(pe, half_body, tail, 3)

        def cross_scalar(act):
            def prepare(b, p):
                act.wait_ge(S("xq_ready"), b + 1)
                nc.scalar.copy(xq_b[:], xq[p][:]).then_inc(S("xq_b_ready"), 1)
                act.wait_ge(S("xdiag_ready"), b + 1)
                nc.scalar.copy(xdiag_b[:], xdiag[p][:]).then_inc(S("xdiag_b_ready"), 1)

            def keep_values(b, p):
                act.wait_ge(S("ctxT_done"), b + 1)
                nc.scalar.copy(xvalue[p][:, :, :, 0:XC],
                               T0[:, 0:256].rearrange("p (c h x) -> p c h x", c=2, h=XH)).then_inc(S("xvalue_ready"), 1)

            def keep_shift(b, p):
                act.wait_ge(S("xmaxT_done"), b + 1)
                nc.scalar.mul(xshift[p][:], T0[0:XH, 0:D], -1.0).then_inc(S("xshift_ready"), 1)

            def softmax(b, h):
                act.wait_ge(S("xscore_done"), 8 * b + h + 1)
                if not (isinstance(b, int) and b == 0):
                    act.wait_ge(S("xpv_done"), 2 * b - 1 + h // 4)
                nc.scalar.activation(probs4[:, h, :], SCORE[h % 2][:], ACT.Exp, scale=XSCALE)\
                    .then_inc(S(f"xprob_ready{h % 2}"), 1)

            def pv_keep(b, gr):
                act.wait_ge(S("xpv_done"), 2 * b + gr + 1)
                act.wait_ge(S("xgathered"), b)
                nc.scalar.copy(xpv[:, gr * D:gr * D + D], PV[gr][:, 0:D]).then_inc(S(f"xpv_kept{gr}"), 1)

            def half_body(b, p, previous, following, i):
                for h in range(XH):
                    softmax(b, h)
                    if h == 0 and following:
                        prepare(b + 1, 1 - p)
                    if h == 2 and previous:
                        pv_keep(b - 1, 1)
                    if h == 2 and following:
                        keep_values(b + 1, 1 - p)
                    if h == 6:
                        pv_keep(b, 0)
                    if h == 7 and following:
                        keep_shift(b + 1, 1 - p)

            act.wait_ge(S("cross_zeroed"), 1)
            ln_stats_scalar(act, 2)
            prepare(0, 0)
            keep_values(0, 0)
            keep_shift(0, 0)
            halves(act, half_body, lambda b, p: pv_keep(b, 1), 3)

        def cross_vector(dve):
            def query_(b, p):
                if not isinstance(b, int) or b > 1:
                    dve.wait_ge(S("xscore_done"), 8 * b - 8)
                normalise(xq[p][:], b).then_inc(S("xq_ready"), 1)

            def reduce_max(b, m):
                dve.wait_ge(S("xmax_scored"), 8 * b + m + 1)
                if m == 0:
                    dve.wait_ge(S("xmaxT_done"), b)
                hs = 2 * (m % 4)
                nc.vector.tensor_reduce(xmax[:, m // 4, hs:hs + 2], SMAX[m % 2][:].rearrange("p (h n) -> p h n", h=2),
                                        AX, ALU.max).then_inc(S(f"xmax_read{m % 2}"), 1)

            def residual(b):
                dve.wait_ge(S("xgathered"), b + 1)
                nc.vector.reciprocal(xden[:], T1[:, D:2 * D]).then_inc(S("xden_ready"), 1)
                dve.wait_ge(S("xden_ready"), b + 1)
                nc.vector.tensor_tensor(xout[:], T1[:, 0:D], xden[:], ALU.mult).then_inc(S("xadded"), 1)
                dve.wait_ge(S("xadded"), b + 1)
                x = X[:, ds(b, 1), :].rearrange("p a d -> p (a d)")
                nc.vector.tensor_tensor(x, x, xout[:], ALU.add).then_inc(S("xdone"), 1)

            def half_body(b, p, previous, following, i):
                for h in range(XH):
                    if h == 0 and following:
                        query_(b + 1, 1 - p)
                    if following and 2 <= h < 6:
                        reduce_max(b + 1, 2 * (h - 2))
                        reduce_max(b + 1, 2 * (h - 2) + 1)
                    if h == 4 and previous:
                        residual(b - 1)

            dve.wait_ge(S("attn_added"), B)
            for p in range(2):
                last = nc.vector.memset(xvalue[p][:], 0.0)
            last.then_inc(S("xvalue_zero"), 1)
            dve.wait_ge(S("xvalue_zero"), 1)
            dve.wait_ge(S("ld_cross"), 48)
            nc.vector.tensor_copy(head_sel[:], head_sel_f[:])
            nc.vector.memset(xvalue[0][:, :, :, XC:XC + 1], 1.0)
            nc.vector.memset(xvalue[1][:, :, :, XC:XC + 1], 1.0).then_inc(S("cross_zeroed"), 1)
            ln_stats_vector(dve, 2)
            query_(0, 0)
            for m in range(8):
                reduce_max(0, m)
            halves(dve, half_body, lambda b, p: residual(b), 3)

        def cross_pool(pool):
            def spread(b, p):
                ctx_loaded(pool, b, p)
                if not isinstance(b, int) or b > 1:
                    pool.wait_ge(S("xscore_done"), 8 * b - 8)
                src = ctx_in[p][:].rearrange("p (a n) -> p a n", a=1).to_broadcast([128, XH, D])
                m = head_rows[:].rearrange("p (h a) -> p h a", a=1).to_broadcast([128, XH, D])
                nc.gpsimd.tensor_tensor(xdiag[p][:], src, m, ALU.mult).then_inc(S("xdiag_ready"), 1)

            def half_body(b, p, previous, following, i):
                if following:
                    spread(b + 1, 1 - p)

            pool.wait_ge(S("ld_cross"), 48)
            pool.wait_ge(S("attn_added"), B)
            spread(0, 0)
            halves(pool, half_body, lambda b, p: None, 3)

        phase_memory()
        logits = sb("logits", [128, E + 1])
        top = sb("top", [128, 8])
        left = sb("left", [128, E])
        chosen = sb("chosen", [128, E])
        route_e = sb("route_e", [128, E + 1])
        route_n = sb("route_n", [128, 1])
        route_s = sb("route_s", [128, 1])
        combine = [sb(f"combine{p}", [128, CROWS]) for p in range(2)]
        combineT = sb("combineT", [CROWS, 2, 128])
        x_hi = sb("x_hi", [128, 2, NT], F32R)
        x_lo = sb("x_lo", [128, 2, NT], F32R)
        up_in = [sb(f"up_in{p}", [128, 2, 2, 128]) for p in range(2)]
        up_hi = [sb(f"up_hi{p}", [128, 2, 2, 128], F32R) for p in range(2)]
        up_lo = [sb(f"up_lo{p}", [128, 2, 2, 128], F32R) for p in range(2)]
        down_in = [sb(f"down_in{p}", [128, D]) for p in range(2)]
        down_hi = [sb(f"down_hi{p}", [128, D], F32R) for p in range(2)]
        down_lo = [sb(f"down_lo{p}", [128, D], F32R) for p in range(2)]
        comb = [sb(f"comb{p}", [128, PASS]) for p in range(2)]
        act_g = [sb(f"act_g{h}", [128, 512]) for h in range(2)]
        act_u = [sb(f"act_u{h}", [128, 512]) for h in range(2)]
        hidden = [sb(f"hidden{h}", [128, 512]) for h in range(2)]
        h_hi = [sb(f"h_hi{h}", [128, 512], F32R) for h in range(2)]
        h_lo = [sb(f"h_lo{h}", [128, 512], F32R) for h in range(2)]
        zero_b = sb("zero_b", [128, 128], BF16)
        zero_b4 = sb("zero_b4", [128, 512], BF16)
        scratch = nc.dram_tensor("combine_scratch", [CROWS, NT], F32, kind="Internal").ap()
        GATE = [bank[0], bank[1]]
        UP = [bank[2], bank[3]]
        OUT = [bank[4 + n] for n in range(4)]
        NPASS = NT // PASS
        LAST = NPASS * PAIRS - 1
        assert NPASS == 2 and PAIRS % 2 == 1

        def moe_loads(sp):
            with sp.Fori(0, B // 2) as i:
                for p in range(2):
                    b = 2 * i + p
                    sp.wait_ge(S("combineT_ready"), b + 1)
                    sp.dma_start(scratch[:, ds(b * T, T)], combineT[:, p, :]).then_inc(S("combine_out"), 16)
            sp.wait_ge(S("combine_out"), 16 * B)
            sp.wait_ge(S("xdone"), B)

            def loads(n, j, p, t0):
                later = not isinstance(n, int) or n > 1
                if later:
                    sp.wait_ge(S("up_split"), n - 1)
                sp.dma_start(up_in[p][:], io["w_up"][ds(j, 1)].rearrange("a p n -> (a p) n")
                             .rearrange("p (c s m) -> p c s m", c=2, s=2)).then_inc(S(f"ld_up{p}"), 16)
                if later:
                    sp.wait_ge(S("weighed1"), n - 1)
                for r in range(2):
                    sp.dma_start(comb[p][64 * r:64 * r + 64, :],
                                 scratch[ds(2 * j + r, 1), t0:t0 + PASS].to_broadcast([64, PASS]))\
                        .then_inc(S(f"ld_comb{p}"), 16)
                if later:
                    sp.wait_ge(S("down_split"), n - 1)
                sp.dma_start(down_in[p][:], io["w_down"][ds(j, 1)].rearrange("a p n -> (a p) n"))\
                    .then_inc(S(f"ld_down{p}"), 16)

            def store(ps):
                sp.wait_ge(S("final_ready"), ps + 1)
                sp.dma_start(io["out"].rearrange("b t d -> t b d")[:, 8 * ps:8 * ps + 8, :],
                             X[:, 8 * ps:8 * ps + 8, :]).then_inc(S("stored"), 16)

            for ps in range(NPASS):
                n0, first = ps * PAIRS, 3
                for j in range(first):
                    loads(n0 + j, j, (n0 + j) % 2, ps * PASS)
                if ps:
                    store(ps - 1)
                with sp.Fori(0, (PAIRS - first) // 2) as i:
                    for h in range(2):
                        j = 2 * i + first + h
                        loads(j + n0, j, (n0 + first + h) % 2, ps * PASS)
            store(NPASS - 1)
            sp.wait_ge(S("stored"), 16 * NPASS)

        def moe_tensor(pe):
            pe.wait_ge(S("ld_router"), 16)

            def transposes(b, p):
                pe.wait_ge(S("xn3_ready"), b + 1)
                pe.wait_ge(S("xn3T_ready"), b)
                for c in range(2):
                    last = nc.tensor.transpose(bank[p][:, c * 128:c * 128 + 128], xn[:, p, c * 128:c * 128 + 128],
                                               ident[:])
                last.then_inc(S("x3T_done"), 1)

            def route(b, p):
                pe.wait_ge(S("xn3T_ready"), b + 1)
                pe.wait_ge(S("logits_kept"), b)
                for c in range(2):
                    last = nc.tensor.matmul(bank[2 + p][:, 0:E + 1], xnT[:, p, c * 128:c * 128 + 128],
                                            w_router[:, c, :], start=c == 0, stop=c == 1)
                last.then_inc(S("logits_done"), 1)

            def combine_transpose(b, p):
                pe.wait_ge(S("combine_ready"), b + 1)
                pe.wait_ge(S("combineT_ready"), b)
                nc.tensor.transpose(bank[4 + p][0:CROWS, 0:128], combine[p][:], ident[:])\
                    .then_inc(S("combineT_done"), 1)

            @pairs_of_batches(pe)
            def _(i):
                for p in range(2):
                    transposes(2 * i + p, p)
                for p in range(2):
                    route(2 * i + p, p)
                for p in range(2):
                    combine_transpose(2 * i + p, p)

            def up(n, p, t0, h):
                if h == 0:
                    pe.wait_ge(S("up_split"), n + 1)
                pe.wait_ge(S(f"gated{h}"), n)
                pe.wait_ge(S(f"upped{h}"), n)
                t = t0 + 512 * h
                for s, out in enumerate((GATE[h], UP[h])):
                    for k in range(6):
                        c, (wp, xp) = k // 3, ((up_hi, x_hi), (up_hi, x_lo), (up_lo, x_hi))[k % 3]
                        last = nc.tensor.matmul(out[:], wp[p][:, c, s, :], xp[:, c, t:t + 512],
                                                start=k == 0, stop=k == 5)
                    last.then_inc(S(("gate_done", "up_done")[s]), 1)

            def down(n, p, h):
                if h == 0:
                    pe.wait_ge(S("down_split"), n + 1)
                pe.wait_ge(S(f"h_ready{h}"), n + 1)
                for q in range(4):
                    k = 4 * h + q
                    for hp, wp in ((h_hi, down_hi), (h_hi, down_lo), (h_lo, down_hi)):
                        last = nc.tensor.matmul(OUT[k // 2][:, k % 2 * D:k % 2 * D + D],
                                                hp[h][:, q * 128:q * 128 + 128], wp[p][:],
                                                start=False, stop=True, skip_group_check=True)
                last.then_inc(S("down_done"), 1)

            def start_sums():
                for k in range(4):
                    nc.tensor.matmul(OUT[k][:], zero_b[:], zero_b4[:], start=True, stop=True, skip_group_check=True)

            def slot(n, p, t0):
                for h in range(2):
                    up(n, p, t0, h)
                    down(n - 1, 1 - p, h)

            pe.wait_ge(S("xn3T_ready"), B)
            pe.wait_ge(S("combineT_ready"), B)
            pe.wait_ge(S("x_lo_ready"), B)
            start_sums()
            up(0, 0, 0, 0)
            up(0, 0, 0, 1)
            slot(1, 1, 0)
            slot(2, 0, 0)
            with pe.Fori(1, (PAIRS - 1) // 2) as i:
                slot(2 * i + 1, 1, 0)
                slot(2 * i + 2, 0, 0)
            slot(PAIRS, 1, PASS)
            pe.wait_ge(S("final_ready"), 1)
            start_sums()
            with pe.Fori(0, (PAIRS - 1) // 2) as i:
                slot(2 * i + PAIRS + 1, 0, PASS)
                slot(2 * i + PAIRS + 2, 1, PASS)
            down(LAST, 1, 0)
            down(LAST, 1, 1)

        def all_pairs(engine, body, middle=None):
            for n in range(3):
                body(n, n % 2)
            with engine.Fori(1, (PAIRS - 1) // 2) as i:
                body(2 * i + 1, 1)
                body(2 * i + 2, 0)
            body(PAIRS, 1)
            if middle:
                middle()
            with engine.Fori(0, (PAIRS - 3) // 2) as i:
                body(2 * i + PAIRS + 1, 0)
                body(2 * i + PAIRS + 2, 1)
            body(LAST - 1, 0)
            body(LAST, 1)

        def moe_scalar(act):
            ln_stats_scalar(act, 3)

            @pairs_of_batches(act)
            def _(i):
                for p in range(2):
                    b = 2 * i + p
                    act.wait_ge(S("x3T_done"), b + 1)
                    act.wait_ge(S("logits_done"), b)
                    act.wait_ge(S("x_lo_ready"), 2 * i)
                    nc.scalar.copy(x_hi[:, :, ds(b * T, T)], bank[p][:, 0:D].rearrange("p (c t) -> p c t", c=2))\
                        .then_inc(S("x_hi_ready"), 1)
                    nc.scalar.copy(xnT[:, p, :], bank[p][:, 0:D]).then_inc(S("xn3T_ready"), 1)
                for p in range(2):
                    b = 2 * i + p
                    act.wait_ge(S("logits_done"), b + 1)
                    act.wait_ge(S("combine_ready"), b)
                    nc.scalar.copy(logits[:], bank[2 + p][:, 0:E + 1]).then_inc(S("logits_kept"), 1)
                    act.wait_ge(S("route_max"), b + 1)
                    nc.scalar.activation(route_e[:, 0:E], logits[:, 0:E], ACT.Exp, bias=route_n[:, 0:1])
                    nc.scalar.activation(route_e[:, E:E + 1], logits[:, E:E + 1], ACT.Exp, scale=-1.0)\
                        .then_inc(S("route_exp"), 1)
                    act.wait_ge(S("combineT_done"), b + 1)
                    if p == 0:
                        act.wait_ge(S("combine_out"), 16 * b)
                    nc.scalar.copy(combineT[:, p, :], bank[4 + p][0:CROWS, 0:128]).then_inc(S("combineT_ready"), 1)

            def gate(n, h):
                act.wait_ge(S("gate_done"), 2 * n + h + 1)
                act.wait_ge(S(f"upped{h}"), n)
                nc.scalar.activation(act_g[h][:], GATE[h][:], ACT.Silu).then_inc(S(f"gated{h}"), 1)

            def hidden_high(n, h):
                act.wait_ge(S(f"weighed{h}"), n + 1)
                if not isinstance(n, int) or n:
                    act.wait_ge(S("down_done"), 2 * n - 1 + h)
                nc.scalar.copy(h_hi[h][:], hidden[h][:]).then_inc(S(f"h_hi_ready{h}"), 1)

            def up_high(n, p):
                act.wait_ge(S(f"ld_up{p}"), 8 * (n - p) + 16)
                if not isinstance(n, int) or n > 1:
                    act.wait_ge(S("up_done"), 2 * n - 2)
                nc.scalar.copy(up_hi[p][:], up_in[p][:]).then_inc(S("up_hi_ready"), 1)

            def down_high(n, p):
                act.wait_ge(S(f"ld_down{p}"), 8 * (n - p) + 16)
                if not isinstance(n, int) or n > 1:
                    act.wait_ge(S("down_done"), 2 * n - 2)
                nc.scalar.copy(down_hi[p][:], down_in[p][:]).then_inc(S("down_hi_ready"), 1)

            def pair(n, p):
                gate(n, 0)
                if not isinstance(n, int) or n:
                    hidden_high(n - 1, 1)
                if not isinstance(n, int) or n < LAST:
                    up_high(n + 1, 1 - p)
                gate(n, 1)
                hidden_high(n, 0)
                down_high(n, p)

            up_high(0, 0)
            all_pairs(act, pair)
            hidden_high(LAST, 1)

        def moe_vector(dve):
            dve.wait_ge(S("xdone"), B)
            nc.vector.memset(zero_b[:], 0.0)
            nc.vector.memset(zero_b4[:], 0.0)
            for p in range(2):
                last = nc.vector.memset(combine[p][:], 0.0)
            last.then_inc(S("moe_zeroed"), 1)
            ln_stats_vector(dve, 3)
            chain = Tally(S("route_chain"))

            def link(ins):
                ins.then_inc(chain.sem, 1)
                chain.add(1)
                dve.wait_ge(chain.sem, chain.value())

            @pairs_of_batches(dve)
            def _(i):
                chain.begin(i, 2 * CHAIN_ROUTE)
                for p in range(2):
                    b = 2 * i + p
                    dve.wait_ge(S("x3T_done"), b)
                    normalise(xn[:, p, :], b).then_inc(S("xn3_ready"), 1)
                for p in range(2):
                    b = 2 * i + p
                    dve.wait_ge(S("xn3T_ready"), b + 1)
                    dve.wait_ge(S("x_hi_ready"), b + 1)
                    nc.vector.tensor_tensor(x_lo[:, :, ds(b * T, T)], xnT[:, p, :].rearrange("p (c t) -> p c t", c=2),
                                            x_hi[:, :, ds(b * T, T)], ALU.subtract).then_inc(S("x_lo_ready"), 1)
                for p in range(2):
                    b = 2 * i + p
                    dve.wait_ge(S("logits_kept"), b + 1)
                    settle(nc.vector)
                    link(nc.vector.max(top[:], logits[:, 0:E]))
                    nc.vector.tensor_scalar(route_n[:], top[:, 0:1], -1.0, None, ALU.mult).then_inc(S("route_max"), 1)
                    link(nc.vector.match_replace(left[:], top[:], logits[:, 0:E], -3.0e38))
                    link(nc.vector.tensor_tensor(chosen[:], logits[:, 0:E], left[:], ALU.not_equal))
                    dve.wait_ge(S("route_exp"), b + 1)
                    link(nc.vector.tensor_tensor(chosen[:], chosen[:], route_e[:, 0:E], ALU.mult))
                    link(nc.vector.tensor_reduce(route_s[:], chosen[:], AX, ALU.add))
                    link(nc.vector.reciprocal(route_s[:], route_s[:]))
                    dve.wait_ge(S("combineT_done"), b)
                    nc.vector.tensor_scalar(combine[p][:, 0:E], chosen[:], route_s[:, 0:1], None, ALU.mult)
                    link(nc.vector.tensor_scalar(route_e[:, E:E + 1], route_e[:, E:E + 1], 1.0, None, ALU.add))
                    nc.vector.reciprocal(combine[p][:, E:E + 1], route_e[:, E:E + 1]).then_inc(S("combine_ready"), 1)
            chain.end(B // 2, "CHAIN_ROUTE x 2")

            def gated(n, h):
                dve.wait_ge(S(f"gated{h}"), n + 1)
                dve.wait_ge(S("up_done"), 2 * n + h + 1)
                dve.wait_ge(S(f"weighed{h}"), n)
                nc.vector.tensor_tensor(act_u[h][:], act_g[h][:], UP[h][:], ALU.mult).then_inc(S(f"upped{h}"), 1)

            def hidden_low(n, h):
                dve.wait_ge(S(f"h_hi_ready{h}"), n + 1)
                nc.vector.tensor_tensor(h_lo[h][:], hidden[h][:], h_hi[h][:], ALU.subtract)\
                    .then_inc(S(f"h_ready{h}"), 1)

            def pair(n, p):
                gated(n, 0)
                if not isinstance(n, int) or n:
                    hidden_low(n - 1, 1)
                gated(n, 1)
                hidden_low(n, 0)

            def final(ps):
                dve.wait_ge(S("down_done"), 2 * PAIRS * (ps + 1))
                for k in range(4):
                    x = X[:, 8 * ps + 2 * k:8 * ps + 2 * k + 2, :].rearrange("p b d -> p (b d)")
                    last = nc.vector.tensor_tensor(x, x, OUT[k][:], ALU.add)
                last.then_inc(S("final_ready"), 1)

            all_pairs(dve, pair, lambda: final(0))
            hidden_low(LAST, 1)
            final(1)

        def moe_pool(pool):
            def weigh(n, p, h):
                if h == 0:
                    pool.wait_ge(S(f"ld_comb{p}"), 16 * (n - p) + 32)
                pool.wait_ge(S(f"upped{h}"), n + 1)
                pool.wait_ge(S(f"h_ready{h}"), n)
                nc.gpsimd.tensor_tensor(hidden[h][:], act_u[h][:], comb[p][:, 512 * h:512 * h + 512], ALU.mult)\
                    .then_inc(S(f"weighed{h}"), 1)

            def up_low(n, p):
                pool.wait_ge(S("up_hi_ready"), n + 1)
                nc.gpsimd.tensor_tensor(up_lo[p][:], up_in[p][:], up_hi[p][:], ALU.subtract)\
                    .then_inc(S("up_split"), 1)

            def down_low(n, p):
                pool.wait_ge(S("down_hi_ready"), n + 1)
                nc.gpsimd.tensor_tensor(down_lo[p][:], down_in[p][:], down_hi[p][:], ALU.subtract)\
                    .then_inc(S("down_split"), 1)

            def pair(n, p):
                weigh(n, p, 0)
                if not isinstance(n, int) or n < LAST:
                    up_low(n + 1, 1 - p)
                weigh(n, p, 1)
                down_low(n, p)

            up_low(0, 0)
            all_pairs(pool, pair)

        place[0].close()
        block = ctx.enter_context(nc.Block())

        @block.gpsimd
        def _(pool):
            attn_pool(pool)
            cross_pool(pool)
            moe_pool(pool)

        @block.vector
        def _(dve):
            proj_vector(dve)
            comp_vector(dve)
            attn_vector(dve)
            cross_vector(dve)
            moe_vector(dve)

        @block.scalar
        def _(act):
            proj_scalar(act)
            comp_scalar(act)
            attn_scalar(act)
            cross_scalar(act)
            moe_scalar(act)

        @block.tensor
        def _(pe):
            proj_tensor(pe)
            comp_tensor(pe)
            attn_tensor(pe)
            cross_tensor(pe)
            moe_tensor(pe)

        @block.sync
        def _(sp):
            def load(dst, src, s):
                sp.dma_start(dst, src).then_inc(S(s), 16)

            xv = io["x"].rearrange("b t d -> t b d")
            load(ident[:], io["c_ident"], "ld_first")
            for c in range(2):
                load(X[:, 8 * c:8 * c + 8, :], xv[:, 8 * c:8 * c + 8, :], "ld_x")
            load(w_proj[:], io["w_proj"].rearrange("(c p) n -> p c n", p=128), "ld_first")
            load(pos[:], io["pos"], "ld_first")
            load(gate_bias[:], io["gate_bias"].partition_broadcast(128), "ld_first")
            for n, name in enumerate(("L0_attn_k_cb1", "L0_attn_v_cb1")):
                load(cb1[:, n:n + 1], io[name].rearrange("(p a) -> p a", a=1), "ld_comp")
            sp.wait_ge(S("zeroed"), 1)
            load(w2k[:, 120:128], io["L0_attn_k_cw2"], "ld_comp")
            load(b2k[:, 120:128], io["L0_attn_k_cb2"].rearrange("(a d) -> a d", a=1), "ld_comp")
            load(w2v[:], io["L0_attn_v_cw2"], "ld_comp")
            load(b2v[:], io["L0_attn_v_cb2"].partition_broadcast(64), "ld_comp")
            for g in range(2):
                load(mem_k[64 * g:64 * g + 64, :], io["L0_attn_mem_ck"].rearrange("h a d -> (h d) a"), "ld_comp")
            load(cv_raw[64:72, 0, :], io["L0_attn_mem_cv"].rearrange("h a d -> (h a) d"), "ld_comp")
            load(kv_rows[:], io["c_kv_rows"], "ld_comp")
            load(cv_rows[:], io["c_cv_rows"], "ld_comp")

            def load_w1(name, s):
                src = io[name].rearrange("(i r d) n -> r d i n", r=2, d=DH)
                for r in range(2):
                    for kv in range(KV):
                        p0 = r * HD + kv * DH
                        load(w1_diag[p0:p0 + DH, :, kv * 128:kv * 128 + 128], src[r], s)

            load_w1("L0_attn_k_cw1", "ld_w1k")
            for dst, name in ((masks, "c_masks"), (rope_cs, "c_rope"), (block_mask, "c_block_mask"), (past_neg, "c_past_neg")):
                load(dst[:], io[name], "ld_attn")
            load(w_out[:], io["w_out"].rearrange("(c p) n -> p c n", p=128), "ld_attn")
            load(head_rows[:], io["c_head_rows"], "ld_cross")
            load(gather[:], io["c_gather"], "ld_cross")
            load(w_router[:], io["w_router"].rearrange("(c p) n -> p c n", p=128), "ld_router")
            sp.wait_ge(S("hidden_done"), 1)
            load_w1("L0_attn_v_cw1", "ld_w1v")
            sp.wait_ge(S("cv_ready"), 1)
            load(key_rows, io["c_key_rows"], "ld_key_rows")
            sp.wait_ge(S("attn_added"), B)
            for i in range(2):
                load(ctx_in[i][:], io["ctx_2048"][i], f"ld_ctx{i}")
            load(head_sel_f[:], io["c_head_sel"], "ld_cross")
            cross_loads(sp)
            moe_loads(sp)



def constants():
    import numpy as np

    f4, neg = np.float32, -1e30
    t = np.arange(T)
    past = (np.arange(NB)[None] + 1) * BLK - 1 < t[:, None]
    ahead = t[None] > t[:, None]
    inv = f4(1.0) / f4(10000.0) ** (np.arange(0, DH, 2, dtype=f4) / f4(DH))
    ang = t.astype(f4)[:, None] * inv[None]
    key_rows = np.zeros((64, KV, T), f4)
    for kv in range(KV):
        for c in range(NB - 1):
            key_rows[kv * 7 + c, kv, c * BLK:c * BLK + BLK] = 1.0
        key_rows[56 + kv, kv] = -1.0
    kv_rows = np.zeros((128, 2 * KV), f4)
    kv_rows[np.arange(128), np.arange(128) // DH] = 1.0
    cv_rows = np.zeros((128, KV), f4)
    cv_rows[np.arange(64), np.arange(64) // NB] = 1.0
    cv_rows[64 + np.arange(KV), np.arange(KV)] = 1.0
    head_rows = np.zeros((128, XH), f4)
    head_rows[t, t // XC] = 1.0
    head_sel = np.zeros((XH, XH, 128), f4)
    head_sel[np.arange(XH), np.arange(XH)] = 1.0
    gather = np.zeros((128, 4, 128), f4)
    for h in range(XH):
        for c in range(XC):
            gather[h % 4 * 32 + c, h // 4, h * XC + c] = 1.0
            gather[h % 4 * 32 + XC, 2 + h // 4, h * XC + c] = 1.0
    return {
        "c_ident": np.eye(128, dtype=f4),
        "c_masks": np.stack([np.where(ahead, neg, 0.0),
                             np.where(ahead | (t[:, None] - t[None] > 64), neg, 0.0)], 1).astype(f4),
        "c_rope": np.stack([np.cos(ang), np.sin(ang)], 1).astype(f4),
        "c_block_mask": np.where(past, 0.0, neg).astype(f4), "c_past_neg": np.where(past, neg, 0.0).astype(f4),
        "c_kv_rows": kv_rows, "c_cv_rows": cv_rows, "c_head_rows": head_rows,
        "c_head_sel": head_sel, "c_gather": gather, "c_key_rows": key_rows,
    }


def layouts(a):
    import numpy as np

    q = a["L0_attn_w_qkv"][:, :G * HD].reshape(D, KV, G, DH).transpose(0, 2, 1, 3).reshape(D, G * HD)
    gate = a["L0_attn_w_gate"].reshape(D, KV, G, 3).transpose(0, 3, 2, 1).reshape(D, 96)
    none = np.zeros((1, D, I), np.float32)
    up = [np.concatenate([a[f"L0_ffn_expert_{s}_w"], a[f"L0_ffn_shared_{s}_w"][None], none]) for s in ("gate", "up")]
    up = np.stack(up).reshape(2, PAIRS, 2, 2, 128, I)
    down = np.concatenate([a["L0_ffn_expert_down_w"], a["L0_ffn_shared_down_w"][None], none.reshape(1, I, D)])
    pos = [np.tile(a[n].transpose(1, 0, 2).reshape(BLK, HD), (NB, 1)) for n in ("L0_attn_k_pos", "L0_attn_v_pos")]
    return {
        "w_proj": np.concatenate([q, a["L0_attn_w_qkv"][:, G * HD:], gate], 1),
        "gate_bias": a["L0_attn_b_gate"].reshape(KV, G, 3).transpose(2, 1, 0).reshape(96),
        "w_out": a["L0_attn_w_out"].reshape(KV, G, DH, D).transpose(1, 0, 2, 3).reshape(D, D),
        "pos": np.stack(pos, 1),
        "w_router": np.concatenate([a["L0_ffn_gate_w"], a["L0_ffn_shared_expert_gate_w"]], 1),
        "w_up": up.transpose(1, 4, 3, 0, 2, 5).reshape(PAIRS, 128, 512),
        "w_down": down.reshape(PAIRS, 128, D),
    }


PLAIN = ["x", "ctx_2048", "L0_attn_k_cw1", "L0_attn_k_cb1", "L0_attn_k_cw2", "L0_attn_k_cb2", "L0_attn_v_cw1",
         "L0_attn_v_cb1", "L0_attn_v_cw2", "L0_attn_v_cb2", "L0_attn_mem_ck", "L0_attn_mem_cv"]


def kernel(**inputs):
    import numpy as np
    import concourse.bacc as bacc
    from concourse.bass_utils import run_bass_kernel_spmd

    a = {k: np.asarray(v) for k, v in inputs.items()}
    sent = {n: a[n] for n in PLAIN} | layouts(a) | constants()
    nc = bacc.Bacc("TRN2", target_bir_lowering=False, num_devices=1)
    arrays, io = {}, {}
    for name, v in sent.items():
        v = np.ascontiguousarray(v)
        arrays[f"in_{name}"] = v
        io[name] = nc.dram_tensor(f"in_{name}", v.shape, mybir.dt.from_np(v.dtype), kind="ExternalInput").ap()
    io["out"] = nc.dram_tensor("out_0", (B, T, D), F32, kind="ExternalOutput").ap()
    build(nc, io)
    r = run_bass_kernel_spmd(nc, [arrays], core_ids=[0])
    return r.results[0]["out_0"]
```

```python
import concourse.bass as bass
from concourse import mybir
from contextlib import ExitStack

F32 = mybir.dt.float32
BF16 = mybir.dt.bfloat16
F32R = mybir.dt.float32r
ALU = mybir.AluOpType
ACT = mybir.ActivationFunctionType
AX = mybir.AxisListType.X
ds = bass.ds

B, T, D = 16, 128, 256
G, KV, DH = 4, 8, 8
NB, BLK = 8, 16
HD = KV * DH
SCALE = float(DH) ** -0.5
NO_BLOCK = -1000.0 * G / SCALE
QKV = 6 * HD
PROJ = QKV + 3 * G * KV
XH, XC = 8, 16
XSCALE = float(XC) ** -0.5
E, K_TOP, I = 64, 8, 64
PAIRS = E // 2 + 1
CROWS = 2 * PAIRS
PASS = 1024
NT = B * T
EPS = 1e-5
CHAIN_ATTN = 56
ROUTED = 4
CHAIN_ROUTE = 7


class Tally:

    def __init__(self, sem):
        self.sem, self.base, self.i, self.per, self.k = sem, 0, None, 0, 0

    def begin(self, i, per):
        self.i, self.per, self.k = i, per, 0

    def end(self, times, what=""):
        assert self.k == self.per, (what, "increments of one iteration", self.k, "declared", self.per)
        self.base += self.per * times
        self.i, self.k = None, 0

    def add(self, n=1):
        if self.i is None:
            self.base += n
        else:
            self.k += n

    def value(self):
        return self.base if self.i is None else self.i * self.per + (self.base + self.k)


def build(nc, io):
    ctx = ExitStack()
    with ctx:
        place = [ctx]

        def sb(name, shape, dt=F32):
            return place[0].enter_context(nc.sbuf_tensor(name, shape, dt))

        def phase_memory():
            if place[0] is not ctx:
                place[0].close()
            place[0] = ExitStack()

        def sem(name):
            return ctx.enter_context(nc.semaphore(name))

        bank = [ctx.enter_context(nc.psum_tensor(f"bank{n}", [128, 512], F32)) for n in range(8)]

        ident = sb("ident", [128, 128])
        identb = sb("identb", [128, 128], BF16)
        causal = sb("causal", [128, 128], BF16)
        window = sb("window", [128, 128], BF16)
        masks = sb("masks", [128, 2, 128])
        rope_cs = sb("rope_cs", [128, 2, DH // 2])
        block_mask = sb("block_mask", [128, NB])
        past_neg = sb("past_neg", [128, NB])
        kv_rows = sb("kv_rows", [128, 2 * KV])
        cv_rows = sb("cv_rows", [128, KV])
        head_rows = sb("head_rows", [128, XH])
        head_sel = sb("head_sel", [XH, XH, 128], BF16)
        gather = sb("gather", [128, 4, 128])
        w_proj = sb("w_proj", [128, 2, PROJ])
        gate_bias = sb("gate_bias", [128, 96])
        w_out = sb("w_out", [128, 2, D])
        pos = sb("pos", [128, 2, HD])
        cb1 = sb("cb1", [128, 2])
        w2k = sb("w2k", [128, 248])
        b2k = sb("b2k", [1, 248])
        ones_row = sb("ones_row", [1, 128])
        w2v = sb("w2v", [128, DH])
        b2v = sb("b2v", [64, DH])
        mem_k = sb("mem_k", [128, 1])
        w_router = sb("w_router", [128, 2, E + 1])
        eps = sb("eps", [128, 1])

        X = sb("X", [128, B, D])
        stats = sb("stats", [128, B, 6])
        mean = sb("mean", [128, B])
        log_var = sb("log_var", [128, B])
        var_eps = sb("var_eps", [128, B])
        newton = sb("newton", [128, B])
        rstd = sb("rstd", [128, B])
        proj = sb("proj", [128, B, PROJ])
        gates = sb("gates", [128, B, 96])
        ck = sb("ck", [128, B, 2 * 72])
        cv = sb("cv", [72, B, HD])

        xn = sb("xn", [128, 2, D])
        xnT = sb("xnT", [128, 2, D])
        tiny = sb("tiny", [128, 64])
        tiny_used = [0]

        phase_memory()
        block_k = sb("block_k", [128, 2 * NT])
        w1_diag = sb("w1_diag", [128, 8, 1024])
        kv_pos = sb("kv_pos", [128, 2, 2, 2, HD])
        hid = sb("hid", [128, 1024])
        hidT = sb("hidT", [128, 1024])
        hid_v = sb("hid_v", [128, 1024])
        cv_raw = sb("cv_raw", [72, B, DH])
        mem_diag = sb("mem_diag", [128, 2 * KV])

        w = {}

        def S(name):
            if name not in w:
                w[name] = sem(name)
            return w[name]

        def later(i, least=1):
            return not isinstance(i, int) or i >= least

        def overlapped(engine, steps, front, back):
            front(0)
            front(1)
            back(0)
            with engine.Fori(1, steps - 1) as i:
                front(i + 1)
                back(i)
            back(steps - 1)

        def settle(eng):
            c = tiny_used[0]
            tiny_used[0] += 1
            if eng is nc.vector:
                nc.vector.memset(tiny[:, c:c + 1], 0.0)
            else:
                nc.gpsimd.tensor_tensor(tiny[:, c:c + 1], ident[:, 0:1], ident[:, 0:1], ALU.add)

        def batch_stats(b):
            nc.vector.bn_stats(stats[:, ds(b, 1), :].rearrange("p a s -> p (a s)"),
                               X[:, ds(b, 1), :].rearrange("p a d -> p (a d)")).then_inc(S("ln_stat"), 1)

        def ln_stats_vector(dve, n):
            chain, past = S("ln_stat"), (n - 1) * (B + 6)
            dve.wait_ge(chain, past + B)
            nc.vector.tensor_tensor(mean[:], stats[:, :, 1], stats[:, :, 4], ALU.add).then_inc(chain, 1)
            nc.vector.tensor_tensor(newton[:], stats[:, :, 1], stats[:, :, 4], ALU.subtract).then_inc(chain, 1)
            nc.vector.tensor_tensor(var_eps[:], stats[:, :, 2], stats[:, :, 5], ALU.add).then_inc(chain, 1)
            dve.wait_ge(chain, past + B + 3)
            nc.vector.tensor_scalar(mean[:], mean[:], 0.5, None, ALU.mult).then_inc(chain, 1)
            nc.vector.tensor_tensor(newton[:], newton[:], newton[:], ALU.mult).then_inc(chain, 1)
            nc.vector.tensor_scalar(var_eps[:], var_eps[:], 1.0 / D, EPS, ALU.mult, ALU.add).then_inc(chain, 1)
            dve.wait_ge(chain, past + B + 6)
            nc.vector.scalar_tensor_tensor(var_eps[:], newton[:], 0.25, var_eps[:], ALU.mult, ALU.add)\
                .then_inc(S("ln_var"), 1)
            dve.wait_ge(S("ln_guess"), 2 * n)
            c2, past = S("ln_newton"), (n - 1) * 3
            nc.vector.tensor_tensor(newton[:], rstd[:], rstd[:], ALU.mult).then_inc(c2, 1)
            dve.wait_ge(c2, past + 1)
            nc.vector.tensor_tensor(newton[:], newton[:], var_eps[:], ALU.mult).then_inc(c2, 1)
            dve.wait_ge(c2, past + 2)
            nc.vector.tensor_scalar(newton[:], newton[:], -0.5, 1.5, ALU.mult, ALU.add).then_inc(c2, 1)
            dve.wait_ge(c2, past + 3)
            nc.vector.tensor_tensor(rstd[:], rstd[:], newton[:], ALU.mult).then_inc(S("ln_done"), 1)
            dve.wait_ge(S("ln_done"), n)

        def ln_stats_scalar(act, n):
            act.wait_ge(S("ln_var"), n)
            nc.scalar.activation(log_var[:], var_eps[:], ACT.Ln).then_inc(S("ln_guess"), 1)
            act.wait_ge(S("ln_guess"), 2 * n - 1)
            nc.scalar.activation(rstd[:], log_var[:], ACT.Exp, scale=-0.5).then_inc(S("ln_guess"), 1)

        def normalise(out, b):
            return nc.vector.tensor_scalar(out, X[:, ds(b, 1), :].rearrange("p a d -> p (a d)"),
                                           mean[:, ds(b, 1)],
                                           rstd[:, ds(b, 1)], ALU.subtract, ALU.mult)

        def proj_vector(dve):
            nc.vector.memset(w2k[:], 0.0)
            nc.vector.memset(b2k[:], 0.0)
            nc.vector.memset(ones_row[:], 1.0)
            nc.vector.memset(w1_diag[:], 0.0).then_inc(S("zeroed"), 1)
            dve.wait_ge(S("ld_x"), 32)
            with dve.Fori(0, B // 4) as i:
                for p in range(4):
                    batch_stats(4 * i + p)
            ln_stats_vector(dve, 1)
            dve.wait_ge(S("ld_first"), 64)

            def front(i):
                for p in range(2):
                    b = 2 * i + p
                    dve.wait_ge(S("xT_done"), b)
                    normalise(xn[:, p, :], b).then_inc(S("xn_ready"), 1)

            def back(i):
                for p in range(2):
                    b = 2 * i + p
                    dve.wait_ge(S("proj_kept"), b + 1)
                    if later(i):
                        dve.wait_ge(S("kvT_done"), b - 1)
                    for n in range(2):
                        src = proj[:, ds(b, 1), (4 + n) * HD:(5 + n) * HD].to_broadcast([128, 2, HD])
                        add = pos[:, n:n + 1, :].to_broadcast([128, 2, HD])
                        last = nc.vector.tensor_tensor(kv_pos[:, p, n, :, :], src, add, ALU.add)
                    last.then_inc(S("kv_pos_ready"), 1)
                for p in range(2):
                    b = 2 * i + p
                    dve.wait_ge(S("kvT_done"), b + 1)
                    pair_columns(nc.vector.tensor_copy, b, p, 0).then_inc(S("block_k_ready"), 1)

            overlapped(dve, B // 2, front, back)

        def pair_columns(copy, b, p, n):
            col = n * NT + b * T
            copy(block_k[0:64, ds(col, T)], bank[4 + 2 * p + n][0:64, 0:T])
            return copy(block_k[64:128, ds(col, T - 1)], bank[4 + 2 * p + n][64:128, 1:T])

        def proj_tensor(pe):
            pe.wait_ge(S("ld_first"), 64)

            def transposes(b, p):
                pe.wait_ge(S("xn_ready"), b + 1)
                pe.wait_ge(S("xnT_ready"), b)
                for c in range(2):
                    last = nc.tensor.transpose(bank[p][:, c * 128:c * 128 + 128], xn[:, p, c * 128:c * 128 + 128],
                                               ident[:])
                last.then_inc(S("xT_done"), 1)

            def project(b, p):
                pe.wait_ge(S("xnT_ready"), b + 1)
                pe.wait_ge(S("proj_kept"), b)
                for c in range(2):
                    last = nc.tensor.matmul(bank[2 + p][:, 0:PROJ], xnT[:, p, c * 128:c * 128 + 128],
                                            w_proj[:, c, :], start=c == 0, stop=c == 1)
                last.then_inc(S("proj_done"), 1)

            def kv_transposes(b, p):
                pe.wait_ge(S("kv_pos_ready"), b + 1)
                if later(b, 2):
                    pe.wait_ge(S("block_k_ready"), b - 1)
                    pe.wait_ge(S("block_v_ready"), b - 1)
                for n in range(2):
                    last = nc.tensor.transpose(bank[4 + 2 * p + n][:, 0:T],
                                               kv_pos[:, p, n, :, :].rearrange("p a d -> p (a d)"), ident[:])
                last.then_inc(S("kvT_done"), 1)

            def front(i):
                for p in range(2):
                    transposes(2 * i + p, p)
                for p in range(2):
                    project(2 * i + p, p)

            def back(i):
                for p in range(2):
                    kv_transposes(2 * i + p, p)

            overlapped(pe, B // 2, front, back)

        def proj_scalar(act):
            ln_stats_scalar(act, 1)

            def front(i):
                for p in range(2):
                    act.wait_ge(S("xT_done"), 2 * i + p + 1)
                    act.wait_ge(S("proj_done"), 2 * i + p)
                    nc.scalar.copy(xnT[:, p, :], bank[p][:, 0:D]).then_inc(S("xnT_ready"), 1)
                for p in range(2):
                    b = 2 * i + p
                    act.wait_ge(S("proj_done"), b + 1)
                    nc.scalar.copy(proj[:, ds(b, 1), :].rearrange("p a n -> p (a n)"),
                                   bank[2 + p][:, 0:PROJ]).then_inc(S("proj_kept"), 1)

            def back(i):
                for p in range(2):
                    b = 2 * i + p
                    act.wait_ge(S("kvT_done"), b + 1)
                    pair_columns(nc.scalar.copy, b, p, 1).then_inc(S("block_v_ready"), 1)

            overlapped(act, B // 2, front, back)

        def comp_tensor(pe):
            pe.wait_ge(S("block_k_ready"), B)
            pe.wait_ge(S("block_v_ready"), B)
            for n in range(2):
                pe.wait_ge(S("ld_w1k" if n == 0 else "ld_w1v"), 256)
                if n == 1:
                    pe.wait_ge(S("hid_kept"), 2)
                for half in range(2):
                    for i in range(8):
                        lhsT = block_k[:, n * NT + 2 * i:(n + 1) * NT:BLK]
                        last = nc.tensor.matmul(bank[half][:], lhsT, w1_diag[:, i, half * 512:half * 512 + 512],
                                                start=i == 0, stop=i == 7)
                last.then_inc(S("hidden_done"), 1)
                pe.wait_ge(S("hid_kept"), 2 * n + 2)
                if n == 1:
                    pe.wait_ge(S("hidT_kept"), 2)
                for kv in range(KV):
                    last = nc.tensor.transpose(bank[2 + kv // 4][:, kv % 4 * 128:kv % 4 * 128 + 128],
                                               hid[:, kv * 128:kv * 128 + 128], ident[:])
                last.then_inc(S("hidT_done"), 1)
                if n == 1:
                    continue
                pe.wait_ge(S("ld_comp"), 11 * 16)
                pe.wait_ge(S("hidT_kept"), 2)
                for g2 in range(2):
                    for kv in range(KV):
                        off = 120 - (g2 * HD + kv * DH)
                        o = bank[4 + 2 * g2 + kv // 4][:, kv % 4 * 128:kv % 4 * 128 + 128]
                        nc.tensor.matmul(o, w2k[:, off:off + 128], hidT[:, kv * 128:kv * 128 + 128],
                                         start=True, stop=False)
                        last = nc.tensor.matmul(o, b2k[:, off:off + 128], ones_row[:], start=False, stop=True)
                last.then_inc(S("ck_done"), 1)
            pe.wait_ge(S("hidT_kept"), 4)
            for b in range(B):
                last = nc.tensor.matmul(bank[0][0:64, b * DH:b * DH + DH], hid_v[:, b * 64:b * 64 + 64], w2v[:],
                                        start=True, stop=True)
            last.then_inc(S("cv_done"), 1)

        def comp_scalar(act):
            act.wait_ge(S("gate_steps"), 1)
            nc.scalar.activation(gates[:], gates[:], ACT.Exp, scale=-1.0).then_inc(S("gate_steps"), 1)
            for n in range(2):
                act.wait_ge(S("hidden_done"), n + 1)
                if n == 1:
                    act.wait_ge(S("hidT_done"), 1)
                for half in range(2):
                    nc.scalar.copy(hid[:, half * 512:half * 512 + 512], bank[half][:]).then_inc(S("hid_kept"), 1)
                act.wait_ge(S("hidT_done"), n + 1)
                if n == 0:
                    act.wait_ge(S("ld_comp"), 11 * 16)
                for half in range(2):
                    if n == 0:
                        o = hidT[:, half * 512:half * 512 + 512]
                        src = bank[2 + half][:]
                    else:
                        o = hid_v[:, :].rearrange("p (b kv c) -> p kv b c", b=B, kv=KV)[:, half * 4:half * 4 + 4]
                        src = bank[2 + half][:].rearrange("p (kv b c) -> p kv b c", kv=4, b=B)
                    nc.scalar.activation(o, src, ACT.Relu, bias=cb1[:, n:n + 1]).then_inc(S("hidT_kept"), 1)

        def comp_vector(dve):
            nc.vector.tensor_tensor(gates[:], proj[:, :, QKV:PROJ],
                                    gate_bias[:].rearrange("p (a n) -> p a n", a=1).to_broadcast([128, B, 96]),
                                    ALU.add).then_inc(S("gate_steps"), 1)
            dve.wait_ge(S("ld_comp"), 11 * 16)
            nc.vector.tensor_scalar(mem_diag[:], kv_rows[:], mem_k[:, 0:1], None, ALU.mult).then_inc(S("mem_diag_ok"), 1)
            dve.wait_ge(S("mem_diag_ok"), 1)
            ck5 = ck[:].rearrange("p b (g n) -> p b g n", g=2)
            for g2 in range(2):
                nc.vector.tensor_copy(ck5[:, :, g2, 64:72],
                                      mem_diag[:, g2 * KV:g2 * KV + KV].rearrange("p (a n) -> p a n", a=1)
                                      .to_broadcast([128, B, KV]))
            nc.vector.tensor_copy(cv_raw[64:72, 1:B, :], cv_raw[64:72, 0:1, :].to_broadcast([8, B - 1, DH]))
            dve.wait_ge(S("gate_steps"), 2)
            nc.vector.tensor_scalar(gates[:], gates[:], 1.0, None, ALU.add).then_inc(S("gate_steps"), 1)
            dve.wait_ge(S("gate_steps"), 3)
            nc.vector.reciprocal(gates[:], gates[:]).then_inc(S("gate_steps"), 1)
            dve.wait_ge(S("gate_steps"), 4)
            dve.wait_ge(S("ld_attn"), 5 * 16)
            nc.vector.tensor_copy(identb[:], ident[:])
            nc.vector.tensor_copy(causal[:], masks[:, 0, :])
            nc.vector.tensor_copy(window[:], masks[:, 1, :]).then_inc(S("masks_ready"), 1)
            dve.wait_ge(S("ck_done"), 1)
            for g2 in range(2):
                for half in range(2):
                    o = ck5[:, :, g2, half * 32:half * 32 + 32].rearrange("p b (kv c) -> p kv b c", kv=4)
                    last = nc.vector.tensor_copy(o, bank[4 + 2 * g2 + half][:]
                                                 .rearrange("p (kv b c) -> p kv b c", kv=4, b=B))
            last.then_inc(S("ck_ready"), 1)
            dve.wait_ge(S("cv_done"), 1)
            nc.vector.tensor_tensor(cv_raw[0:64], bank[0][0:64, 0:128].rearrange("p (b d) -> p b d", b=B),
                                    b2v[:].rearrange("p (a d) -> p a d", a=1).to_broadcast([64, B, DH]),
                                    ALU.add).then_inc(S("cv_raw_ok"), 1)
            dve.wait_ge(S("cv_raw_ok"), 1)
            o = cv[:].rearrange("p b (kv d) -> p b kv d", kv=KV)
            i0 = cv_raw[:].rearrange("p b (a d) -> p b a d", a=1).to_broadcast([72, B, KV, DH])
            i1 = cv_rows[0:72].rearrange("p (a kv c) -> p a kv c", a=1, c=1).to_broadcast([72, B, KV, DH])
            nc.vector.tensor_tensor(o, i0, i1, ALU.mult).then_inc(S("cv_ready"), 1)

        phase_memory()
        probs = sb("probs", [128, 8, 512])
        raw = sb("raw", [128, (G + 1) * HD])
        rot = sb("rot", [128, (G + 1) * 2 * HD])
        rope_a = sb("rope_a", [128, 40, 4])
        rope_b = sb("rope_b", [128, 40, 4])
        query = [[sb(f"query{br}{p}", [128, 512], F32R) for p in range(2)] for br in range(2)]
        query_rest = [sb(f"query_rest{p}", [128, 512], F32R) for p in range(2)]
        key_diag = [sb(f"key_diag{p}", [128, KV, 128], F32R) for p in range(2)]
        key_rest = [sb(f"key_rest{p}", [128, KV, 128], F32R) for p in range(2)]
        key_parts = sb("key_parts", [128, 128], F32R)
        key_high = sb("key_high", [64, 128], F32R)
        part_rows = sb("part_rows", [128, KV])
        query_b = sb("query_b", [128, 512], BF16)
        key_b = sb("key_b", [128, KV, 128], BF16)
        rawT = sb("rawT", [128, 256])
        csim = sb("csim", [128, G, 72])
        cexp = sb("cexp", [128, G, 72])
        cprob = sb("cprob", [128, G, 72])
        cprobT = sb("cprobT", [72, 512])
        cmax = sb("cmax", [128, G, KV])
        csum = sb("csum", [128, G, KV])
        imp = sb("imp", [128, 72])
        impmax = sb("impmax", [128, KV])
        impe = sb("impe", [128, 72])
        impsum = sb("impsum", [128, KV])
        skip = sb("skip", [128, HD])
        blockmax = sb("blockmax", [128, G, KV, NB])
        farmax = sb("farmax", [128, G, KV])
        finemax = sb("finemax", [128, G, KV, NB])
        nearmax = sb("nearmax", [128, G, KV])
        rows = [sb(f"rows{br}", [128, G, 128]) for br in range(2)]
        value = [sb(f"value{p}", [128, KV, 32]) for p in range(2)]
        pv = sb("pv", [128, 2, 512])
        weight = sb("weight", [128, G, 4])
        part = sb("part", [128, G, 4, DH])
        attn = [sb(f"attn{p}", [128, G, KV, DH]) for p in range(2)]
        attnT = sb("attnT", [128, 256])

        SMAX = [bank[0], bank[1]]
        SCORE = [bank[2], bank[3]]
        PV = [bank[4], bank[5]]
        T0, T1 = bank[6], bank[7]
        BR = [0, 1, 0, 1]
        HALF = [0, 0, 1, 1]

        COMP_AT, ROWS_AT, STATS_AT = 12, 14, 10

        def halves(engine, half_body, tail, lead=1):
            for b in range(lead):
                half_body(b, b % 2, b > 0, True, None)
            with engine.Fori(0, (B - 1 - lead) // 2) as i:
                half_body(2 * i + lead, 1, True, True, i)
                half_body(2 * i + lead + 1, 0, True, True, i)
            half_body(B - 1, 1, True, False, None)
            tail(B - 1, 1)

        key_rows = probs[64:128, 0:2, :].rearrange("p a (kv k) -> p (a kv) k", k=128)

        def attn_tensor(pe):
            def qk_transposes(b):
                pe.wait_ge(S("rot_ready"), b + 1)
                if not isinstance(b, int) or b > 1:
                    pe.wait_ge(S("part_ready"), 4 * b - 5)
                for c in range(2):
                    nc.tensor.transpose(T1[:, 128 + c * 128:256 + c * 128], raw[:, c * 128:c * 128 + 128], ident[:])
                nc.tensor.transpose(T1[:, 0:128], rot[:, G * 128:(G + 1) * 128], ident[:]).then_inc(S("rawT_done"), 1)
                for g in range(G):
                    last = nc.tensor.transpose(T0[:, g * 128:g * 128 + 128], rot[:, g * 128:g * 128 + 128], ident[:])
                last.then_inc(S("rqT_done"), 1)

            def block_scores(b):
                pe.wait_ge(S("rawT_ready"), b + 1)
                for c in range(2):
                    last = nc.tensor.matmul(T1[:, c * 144:c * 144 + 144], rawT[:, c * 128:c * 128 + 128],
                                            ck[:, ds(b, 1), :].rearrange("p a n -> p (a n)"), start=True, stop=True)
                last.then_inc(S("csim_done"), 1)

            def max_scores(b, m):
                if m == 0:
                    pe.wait_ge(S("query_b_ready"), b + 1)
                    pe.wait_ge(S("key_b_ready"), b + 1)
                pe.wait_ge(S(f"smax_read{m % 2}"), 6 * b + m // 2)
                g, half = (m // 2, m % 2) if m < 8 else (m - 8, 0)
                kvs, keys = (slice(half * 4, half * 4 + 4), 128) if m < 8 else (slice(0, 8), 64)
                out = SMAX[m % 2][:, :].rearrange("p (h k) -> p h k", k=keys)
                nc.tensor.matmul(out, query_b[:, g * 128:g * 128 + 128], key_b[:, kvs, 0:keys], start=True, stop=False)
                mask = (causal if m < 8 else window)[:, 0:keys].rearrange("p (a k) -> p a k", a=1)
                nc.tensor.matmul(out, identb[:], mask.to_broadcast([128, 512 // keys, keys]), start=False,
                                 stop=True).then_inc(S("smax_done"), 1)

            def row_transposes(b):
                pe.wait_ge(S("query_rest_ready"), b + 1)
                if not isinstance(b, int) or b > 0:
                    pe.wait_ge(S("part_ready"), 4 * b - 2)
                pe.wait_ge(S("cout_kept"), b + 1)
                for br in range(2):
                    pe.wait_ge(S(f"rows_ready{br}"), b + 1)
                    for g in range(G):
                        last = nc.tensor.transpose((T0, T1)[br][:, g * 128:g * 128 + 128], rows[br][:, g, :], ident[:])
                    last.then_inc(S(f"rowsT_done{br}"), 1)

            def comp_transposes(b):
                pe.wait_ge(S("cprob_ready"), b + 1)
                if not isinstance(b, int) or b > 1:
                    pe.wait_ge(S("attnT_ready"), b - 1)
                for g in range(G):
                    last = nc.tensor.transpose(T1[0:72, g * 128:g * 128 + 128], cprob[:, g, :], ident[:])
                last.then_inc(S("cprobT_done"), 1)

            def comp_values(b):
                pe.wait_ge(S("cprobT_ready"), b + 1)
                for g in range(G):
                    last = nc.tensor.matmul(T1[:, g * HD:g * HD + HD], cprobT[:, g * 128:g * 128 + 128],
                                            cv[:, ds(b, 1), :].rearrange("p a n -> p (a n)"), start=True, stop=True)
                last.then_inc(S("cout_done"), 1)

            def score(b, p, u):
                gr, kv = u // 4, HALF[u // 4] * 4 + u % 4
                if u == 0:
                    pe.wait_ge(S("rows_kept0"), b + 1)
                    pe.wait_ge(S("rows_kept1"), b + 1)
                    pe.wait_ge(S("query_rest_ready"), b + 1)
                    pe.wait_ge(S("key_rest_ready"), b + 1)
                pe.wait_ge(S(f"prob_ready{u % 2}"), 8 * b + u // 2)
                nc.tensor.matmul(SCORE[u % 2][:], key_diag[p][:, kv, :], query[BR[gr]][p][:], start=True, stop=False)
                nc.tensor.matmul(SCORE[u % 2][:], key_rest[p][:, kv, :], query_rest[p][:], start=False, stop=False)
                eye = identb[:].rearrange("p (a k) -> p a k", a=1).to_broadcast([128, G, 128])
                nc.tensor.matmul(SCORE[u % 2][:].rearrange("p (g t) -> p g t", g=G), (causal, window)[BR[gr]][:], eye,
                                 start=False, stop=True).then_inc(S("score_done"), 1)

            def values(b, p, gr):
                if gr == 0:
                    pe.wait_ge(S("value_ready"), b + 1)
                for j in range(4):
                    u = gr * 4 + j
                    pe.wait_ge(S(f"prob_ready{u % 2}"), 8 * b + u // 2 + 1)
                pe.wait_ge(S(f"pv_kept{gr % 2}"), 2 * b + gr // 2)
                for j in range(4):
                    u = gr * 4 + j
                    last = nc.tensor.matmul(PV[gr % 2][32 * j:32 * j + 32, :], value[p][:, HALF[gr] * 4 + j, :],
                                            probs[:, u % 8, :], start=True, stop=True)
                last.then_inc(S("pv_done"), 1)

            def pv_transposes(b, gr):
                pe.wait_ge(S(f"pv_kept{gr % 2}"), 2 * b + gr // 2 + 1)
                if gr == 0:
                    pe.wait_ge(S("attn_added"), b)
                    if not isinstance(b, int) or b < B - 1:
                        pe.wait_ge(S("query_rest_ready"), b + 2)
                elif gr == 2 and (not isinstance(b, int) or b < B - 1):
                    pe.wait_ge(S("rows_kept0"), b + 2)
                elif gr == 3 and (not isinstance(b, int) or b < B - 2):
                    pe.wait_ge(S("query_rest_ready"), b + 3)
                else:
                    pe.wait_ge(S("part_ready"), 4 * b + gr)
                for g in range(G):
                    last = nc.tensor.transpose(T0[:, g * 128:g * 128 + 128], pv[:, gr % 2, g * 128:g * 128 + 128],
                                               ident[:])
                last.then_inc(S("pvT_done"), 1)

            def out_transposes(b, p):
                pe.wait_ge(S("attn_ready"), b + 1)
                if not isinstance(b, int) or b < B - 2:
                    pe.wait_ge(S("csim_kept"), b + 3)
                a = attn[p][:].rearrange("p g kv d -> p (g kv d)")
                for c in range(2):
                    last = nc.tensor.transpose(T1[:, c * 128:c * 128 + 128], a[:, c * 128:c * 128 + 128], ident[:])
                last.then_inc(S("attnT_done"), 1)

            def out_project(b):
                pe.wait_ge(S("attnT_ready"), b + 1)
                pe.wait_ge(S("part_ready"), 4 * b + 4)
                for c in range(2):
                    last = nc.tensor.matmul(T0[:, 0:D], attnT[:, c * 128:c * 128 + 128], w_out[:, c, :],
                                            start=c == 0, stop=c == 1)
                last.then_inc(S("out_done"), 1)

            def half_body(b, p, previous, following, i):
                for u in range(16):
                    score(b, p, u)
                    if u == 1:
                        if previous:
                            values(b - 1, 1 - p, 3)
                        if following:
                            qk_transposes(b + 1)
                    if u == 3 and following:
                        block_scores(b + 1)
                    if u == 3 and previous:
                        pv_transposes(b - 1, 3)
                    if u == 4 and previous:
                        out_transposes(b - 1, 1 - p)
                    if following and 4 <= u < 10:
                        max_scores(b + 1, 2 * (u - 4))
                        max_scores(b + 1, 2 * (u - 4) + 1)
                    if u == 6 and previous:
                        out_project(b - 1)
                    if u in (5, 9, 13):
                        values(b, p, (u - 5) // 4)
                    if following and u == ROWS_AT:
                        row_transposes(b + 1)
                    if u in (7, 11, 15):
                        pv_transposes(b, (u - 7) // 4)
                    if following and u == COMP_AT:
                        comp_transposes(b + 1)
                    if following and u == COMP_AT + 1:
                        comp_values(b + 1)

            def tail(b, p):
                values(b, p, 3)
                pv_transposes(b, 3)
                out_transposes(b, p)
                out_project(b)

            pe.wait_ge(S("ld_attn"), 5 * 16)
            pe.wait_ge(S("attn_zeroed"), 1)
            pe.wait_ge(S("masks_ready"), 1)
            pe.wait_ge(S("ck_ready"), 1)
            pe.wait_ge(S("cv_ready"), 1)
            qk_transposes(0)
            block_scores(0)
            for m in range(12):
                max_scores(0, m)
            comp_transposes(0)
            comp_values(0)
            row_transposes(0)
            halves(pe, half_body, tail)

        def attn_scalar(act):
            def after_qk(b, p):
                act.wait_ge(S("rqT_done"), b + 1)
                nc.scalar.copy(query_b[0:64, :], T0[0:64, :]).then_inc(S("query_b_ready"), 1)
                nc.scalar.copy(query_rest[p][:], T0[:]).then_inc(S("query_high_ready"), 1)
                act.wait_ge(S("key_parts_ready"), b + 1)
                nc.scalar.copy(rawT[:], T1[:, 128:384]).then_inc(S("rawT_ready"), 1)
                act.wait_ge(S("query_high_ready"), b + 1)
                for br in range(2):
                    nc.scalar.copy(query[br][p][0:64, :], query_rest[p][0:64, :])

            def comp_exp(b):
                act.wait_ge(S("cexp_in"), b + 1)
                nc.scalar.activation(cexp[:], cexp[:], ACT.Exp, scale=SCALE).then_inc(S("cexp_done"), 1)
                act.wait_ge(S("impe_in"), b + 1)
                nc.scalar.activation(impe[:], impe[:], ACT.Exp, scale=SCALE / G).then_inc(S("impe_done"), 1)

            def comp_keep(b):
                act.wait_ge(S("cprobT_done"), b + 1)
                nc.scalar.copy(cprobT[:], T1[0:72, :]).then_inc(S("cprobT_ready"), 1)

            def rows_keep(b, p):
                for br in range(2):
                    act.wait_ge(S(f"rowsT_done{br}"), b + 1)
                    nc.scalar.copy(query[br][p][64:128, :], (T0, T1)[br][64:128, :])\
                        .then_inc(S(f"rows_kept{br}"), 1)

            def softmax(b, u):
                act.wait_ge(S("score_done"), 16 * b + u + 1)
                if not (isinstance(b, int) and b == 0 and u < 8):
                    act.wait_ge(S("pv_done"), 4 * b + u // 4 - 1)
                nc.scalar.activation(probs[:, u % 8, :], SCORE[u % 2][:], ACT.Exp, scale=SCALE)\
                    .then_inc(S(f"prob_ready{u % 2}"), 1)

            def pv_keep(b, gr):
                act.wait_ge(S("pv_done"), 4 * b + gr + 1)
                nc.scalar.copy(pv[:, gr % 2, :], PV[gr % 2][:]).then_inc(S(f"pv_kept{gr % 2}"), 1)

            def out_keep(b):
                act.wait_ge(S("attnT_done"), b + 1)
                nc.scalar.copy(attnT[:], T1[:, 0:256]).then_inc(S("attnT_ready"), 1)

            def half_body(b, p, previous, following, i):
                for u in range(16):
                    softmax(b, u)
                    if u == 1:
                        if previous:
                            pv_keep(b - 1, 3)
                        if following:
                            after_qk(b + 1, 1 - p)
                    if u == 5 and previous:
                        out_keep(b - 1)
                    if u in (6, 10, 14):
                        pv_keep(b, (u - 6) // 4)
                    if following and u == 8:
                        comp_exp(b + 1)
                    if following and u == COMP_AT:
                        comp_keep(b + 1)
                    if following and u == ROWS_AT:
                        rows_keep(b + 1, 1 - p)

            def tail(b, p):
                pv_keep(b, 3)
                out_keep(b)

            act.wait_ge(S("attn_zeroed"), 1)
            after_qk(0, 0)
            comp_exp(0)
            comp_keep(0)
            rows_keep(0, 0)
            halves(act, half_body, tail)

        def attn_vector(dve):
            chain = Tally(S("attn_chain"))

            def link(ins):
                ins.then_inc(chain.sem, 1)
                chain.add(1)
                dve.wait_ge(chain.sem, chain.value())

            def gkc(ap, n):
                return ap.rearrange("p g (kv c) -> p g kv c", c=n)

            def keys(b, p):
                dve.wait_ge(S("rawT_done"), b + 1)
                nc.vector.tensor_copy(key_parts[64:128], T1[64:128, 0:128])
                link(nc.vector.tensor_copy(key_high[:], T1[0:64, 0:128]))
                nc.vector.tensor_tensor(key_parts[0:64], T1[0:64, 0:128], key_high[:], ALU.subtract)\
                    .then_inc(S("key_parts_ready"), 1)
                src = key_high[:].rearrange("p (a k) -> p a k", a=1).to_broadcast([64, KV, 128])
                m = kv_rows[0:64, 0:KV].rearrange("p (kv a) -> p kv a", a=1).to_broadcast([64, KV, 128])
                nc.vector.tensor_tensor(key_diag[p][0:64], src, m, ALU.mult).then_inc(S("key_diag_ready"), 1)
                dve.wait_ge(S("query_high_ready"), b + 1)
                nc.vector.tensor_tensor(query_rest[p][64:128], T0[64:128, :], query_rest[p][64:128], ALU.subtract)\
                    .then_inc(S("query_rest_ready"), 1)
                dve.wait_ge(S("key_parts_ready"), b + 1)
                src = key_parts[:].rearrange("p (a k) -> p a k", a=1).to_broadcast([128, KV, 128])
                m = part_rows[:].rearrange("p (kv a) -> p kv a", a=1).to_broadcast([128, KV, 128])
                nc.vector.tensor_tensor(key_rest[p][:], src, m, ALU.mult).then_inc(S("key_rest_ready"), 1)

            def comp_softmax(b):
                dve.wait_ge(S("csim_done"), b + 1)
                s = T1[:, 0:288].rearrange("p (g n) -> p g n", g=G)
                for g in range(G):
                    nc.vector.tensor_tensor(csim[:, g, 0:64].rearrange("p (kv c) -> p kv c", c=NB),
                                            s[:, g, 0:64].rearrange("p (kv c) -> p kv c", c=NB),
                                            block_mask[:].rearrange("p (a c) -> p a c", a=1)
                                            .to_broadcast([128, KV, NB]), ALU.add)
                nc.vector.tensor_copy(csim[:, :, 64:72], s[:, :, 64:72]).then_inc(S("csim_kept"), 1)
                dve.wait_ge(S("csim_kept"), b + 1)
                cs, ce = gkc(csim[:, :, 0:64], NB), gkc(cexp[:, :, 0:64], NB)
                link(nc.vector.tensor_reduce(cmax[:], cs, AX, ALU.max))
                link(nc.vector.tensor_tensor(cmax[:], cmax[:], csim[:, :, 64:72], ALU.max))
                mb = cmax[:].rearrange("p g (kv a) -> p g kv a", a=1).to_broadcast([128, G, KV, NB])
                nc.vector.tensor_tensor(ce, cs, mb, ALU.subtract)
                nc.vector.tensor_tensor(cexp[:, :, 64:72], csim[:, :, 64:72], cmax[:], ALU.subtract)\
                    .then_inc(S("cexp_in"), 1)
                link(nc.vector.tensor_reduce(imp[:, 0:64], csim[:, :, 0:64].rearrange("p g n -> p n g"), AX, ALU.add))
                im = imp[:, 0:64].rearrange("p (kv c) -> p kv c", c=NB)
                link(nc.vector.tensor_reduce(impmax[:], im, AX, ALU.max))
                link(nc.vector.tensor_scalar(impmax[:], impmax[:], NO_BLOCK, None, ALU.max))
                nc.vector.tensor_scalar(impe[:, 64:72], impmax[:], -1.0, NO_BLOCK, ALU.mult, ALU.add)
                ib = impmax[:].rearrange("p (kv a) -> p kv a", a=1).to_broadcast([128, KV, NB])
                nc.vector.tensor_tensor(impe[:, 0:64].rearrange("p (kv c) -> p kv c", c=NB), im, ib,
                                        ALU.subtract).then_inc(S("impe_in"), 1)

            def comp_weights(b):
                dve.wait_ge(S("cexp_done"), b + 1)
                ce = gkc(cexp[:, :, 0:64], NB)
                link(nc.vector.tensor_reduce(csum[:], ce, AX, ALU.add))
                link(nc.vector.tensor_tensor(csum[:], csum[:], cexp[:, :, 64:72], ALU.add))
                link(nc.vector.reciprocal(csum[:], csum[:]))
                gt = gates[:, ds(b, 1), 0:32].rearrange("p a (g kv) -> p (a g) kv", g=G)
                link(nc.vector.tensor_tensor(csum[:], csum[:], gt, ALU.mult))
                dve.wait_ge(S("cprobT_done"), b)
                sbc = csum[:].rearrange("p g (kv a) -> p g kv a", a=1).to_broadcast([128, G, KV, NB])
                nc.vector.tensor_tensor(gkc(cprob[:, :, 0:64], NB), ce, sbc, ALU.mult)
                nc.vector.tensor_tensor(cprob[:, :, 64:72], cexp[:, :, 64:72], csum[:], ALU.mult)\
                    .then_inc(S("cprob_ready"), 1)
                dve.wait_ge(S("impe_done"), b + 1)
                ie = impe[:, 0:64].rearrange("p (kv c) -> p kv c", c=NB)
                link(nc.vector.tensor_reduce(impsum[:], ie, AX, ALU.add))
                link(nc.vector.tensor_tensor(impsum[:], impsum[:], impe[:, 64:72], ALU.add))
                link(nc.vector.tensor_scalar(impsum[:], impsum[:], 1e-10, None, ALU.mult))
                th = impsum[:].rearrange("p (kv a) -> p kv a", a=1).to_broadcast([128, KV, NB])
                sk = skip[:].rearrange("p (kv c) -> p kv c", c=NB)
                link(nc.vector.tensor_tensor(sk, ie, th, ALU.is_le))
                pn = past_neg[:].rearrange("p (a c) -> p a c", a=1).to_broadcast([128, KV, NB])
                link(nc.vector.tensor_tensor(sk, sk, pn, ALU.mult))

            def reduce_max(b, m):
                dve.wait_ge(S("smax_done"), 12 * b + m + 1)
                if m < 8:
                    g, half = m // 2, m % 2
                    src = SMAX[m % 2][:].rearrange("p (h c k) -> p h c k", h=4, k=BLK)
                    ins = nc.vector.tensor_reduce(blockmax[:, g, half * 4:half * 4 + 4, :], src, AX, ALU.max)
                else:
                    src = SMAX[m % 2][:].rearrange("p (h k) -> p h k", k=64)
                    ins = nc.vector.tensor_reduce(farmax[:, m - 8, :], src, AX, ALU.max)
                ins.then_inc(S(f"smax_read{m % 2}"), 1)

            def maxima(b):
                for n in range(2):
                    dve.wait_ge(S(f"smax_read{n}"), 6 * b + 6)
                sk = skip[:].rearrange("p (kv c) -> p kv c", c=NB)
                for g in range(G):
                    last = nc.vector.tensor_tensor(finemax[:, g], blockmax[:, g], sk, ALU.add)
                link(last)
                dve.wait_ge(S("rowsT_done0"), b)
                dve.wait_ge(S("rowsT_done1"), b)
                nc.vector.tensor_reduce(rows[0][:, :, 120:128], finemax[:], AX, ALU.max)
                nc.vector.tensor_copy(rows[0][:, :, 64:120].rearrange("p g (kv c) -> p g kv c", c=7),
                                      sk[:, :, 0:7].rearrange("p (a kv) c -> p a kv c", a=1)
                                      .to_broadcast([128, G, KV, 7])).then_inc(S("rows_ready0"), 1)
                link(nc.vector.tensor_reduce(nearmax[:], blockmax[:, :, :, 4:8], AX, ALU.max))
                nc.vector.tensor_tensor(rows[1][:, :, 120:128], nearmax[:], farmax[:], ALU.max)\
                    .then_inc(S("rows_ready1"), 1)

            def comp_out(b, p):
                dve.wait_ge(S("cout_done"), b + 1)
                if not isinstance(b, int) or b > 1:
                    dve.wait_ge(S("attnT_done"), b - 1)
                nc.vector.tensor_copy(attn[p][:].rearrange("p g kv d -> p (g kv d)"), T1[:, 0:256])\
                    .then_inc(S("cout_kept"), 1)

            def add_branch(b, p, gr):
                dve.wait_ge(S("pvT_done"), 4 * b + gr + 1)
                src = T0[:].rearrange("p (g kv c) -> p g kv c", g=G, c=32)
                link(nc.vector.reciprocal(weight[:], src[:, :, :, DH]))
                k0 = 32 + 32 * BR[gr]
                gt = gates[:, ds(b, 1), k0:k0 + 32].rearrange("p a (g kv) -> p (a g) kv", g=G)
                link(nc.vector.tensor_tensor(weight[:], weight[:], gt[:, :, HALF[gr] * 4:HALF[gr] * 4 + 4], ALU.mult))
                wb = weight[:].rearrange("p g (kv a) -> p g kv a", a=1).to_broadcast([128, G, 4, DH])
                nc.vector.tensor_tensor(part[:], src[:, :, :, 0:DH], wb, ALU.mult).then_inc(S("part_ready"), 1)
                dve.wait_ge(S("part_ready"), 4 * b + gr + 1)
                if gr == 0:
                    dve.wait_ge(S("cout_kept"), b + 1)
                a = attn[p][:, :, HALF[gr] * 4:HALF[gr] * 4 + 4, :]
                ins = nc.vector.tensor_tensor(a, a, part[:], ALU.add)
                if gr == 3:
                    ins.then_inc(S("attn_ready"), 1)
                else:
                    link(ins)

            def residual(b):
                dve.wait_ge(S("out_done"), b + 1)
                x = X[:, ds(b, 1), :].rearrange("p a d -> p (a d)")
                nc.vector.tensor_tensor(x, x, T0[:, 0:D], ALU.add).then_inc(S("attn_added"), 1)

            def next_stats(b):
                dve.wait_ge(S("attn_added"), b + 1)
                settle(nc.vector)
                batch_stats(b)

            def half_body(b, p, previous, following, i):
                if i is not None and p == 1:
                    chain.begin(i, CHAIN_ATTN)
                for u in range(16):
                    if u == 1 and following:
                        keys(b + 1, 1 - p)
                    if u == 2 and previous:
                        add_branch(b - 1, 1 - p, 3)
                    if u == 3 and following:
                        comp_softmax(b + 1)
                    if following and 4 <= u < 10:
                        reduce_max(b + 1, 2 * (u - 4))
                        reduce_max(b + 1, 2 * (u - 4) + 1)
                    if u == 6 and previous:
                        residual(b - 1)
                    if u in (7, 11, 15):
                        add_branch(b, p, (u - 7) // 4)
                    if u == STATS_AT and previous:
                        next_stats(b - 1)
                    if following and u == 9:
                        comp_weights(b + 1)
                        maxima(b + 1)
                    if following and u == COMP_AT + 1:
                        comp_out(b + 1, 1 - p)
                if i is not None and p == 0:
                    chain.end(7, "CHAIN_ATTN")

            def tail(b, p):
                add_branch(b, p, 3)
                residual(b)
                next_stats(b)

            for br in range(2):
                nc.vector.memset(rows[br][:], 0.0)
            for p in range(2):
                nc.vector.memset(value[p][:], 0.0)
            nc.vector.memset(query_b[64:128], 0.0)
            link(nc.vector.memset(key_b[64:128], 0.0))
            nc.vector.memset(value[0][:, :, DH:DH + 1], 1.0)
            nc.vector.memset(value[1][:, :, DH:DH + 1], 1.0).then_inc(S("attn_zeroed"), 1)
            nc.vector.tensor_tensor(part_rows[:], kv_rows[:, 0:KV], kv_rows[:, KV:2 * KV], ALU.add)\
                .then_inc(S("part_rows_ready"), 1)
            dve.wait_ge(S("ld_key_rows"), 16)
            for p in range(2):
                nc.vector.tensor_copy(key_diag[p][64:128], key_rows)
            dve.wait_ge(S("part_rows_ready"), 1)
            keys(0, 0)
            comp_softmax(0)
            for m in range(12):
                reduce_max(0, m)
            comp_weights(0)
            maxima(0)
            comp_out(0, 0)
            halves(dve, half_body, tail)

        def attn_pool(pool):
            chain = Tally(S("rope_chain"))

            def link(ins):
                ins.then_inc(chain.sem, 1)
                chain.add(1)
                pool.wait_ge(chain.sem, chain.value())

            def rotate(b):
                pool.wait_ge(S("rqT_done"), b)
                pool.wait_ge(S("rawT_done"), b)
                settle(nc.gpsimd)
                nc.gpsimd.tensor_copy(raw[:], proj[:, ds(b, 1), 0:(G + 1) * HD].rearrange("p a n -> p (a n)"))\
                    .then_inc(S("raw_ready"), 1)
                pool.wait_ge(S("raw_ready"), b + 1)
                x = raw[:].rearrange("p (h d two) -> p h d two", d=4, two=2)
                o = rot[:].rearrange("p (g r h two) -> p g r h two", g=G + 1, r=2, two=2)

                def grouped(ap):
                    return ap.rearrange("p (g h) d -> p g (h d)", g=G + 1)
                cos = rope_cs[:, 0:1, :].to_broadcast([128, 40, 4])
                sin = rope_cs[:, 1:2, :].to_broadcast([128, 40, 4])
                nc.gpsimd.tensor_tensor(rope_a[:], x[:, :, :, 0], cos, ALU.mult)
                link(nc.gpsimd.tensor_tensor(rope_b[:], x[:, :, :, 1], sin, ALU.mult))
                link(nc.gpsimd.tensor_tensor(o[:, :, 0, :, 0], grouped(rope_a[:]), grouped(rope_b[:]), ALU.subtract))
                nc.gpsimd.tensor_tensor(rope_a[:], x[:, :, :, 0], sin, ALU.mult)
                link(nc.gpsimd.tensor_tensor(rope_b[:], x[:, :, :, 1], cos, ALU.mult))
                link(nc.gpsimd.tensor_tensor(o[:, :, 0, :, 1], grouped(rope_a[:]), grouped(rope_b[:]), ALU.add))
                twice = rot[:].rearrange("p (g r n) -> p g r n", g=G + 1, r=2)
                settle(nc.gpsimd)
                nc.gpsimd.tensor_copy(twice[:, :, 1, :], twice[:, :, 0, :]).then_inc(S("rot_ready"), 1)

            def narrow_keys(b, p):
                pool.wait_ge(S("key_diag_ready"), b + 1)
                settle(nc.gpsimd)
                nc.gpsimd.tensor_copy(key_b[0:64], key_diag[p][0:64]).then_inc(S("key_b_ready"), 1)

            def take_values(b, p):
                if not isinstance(b, int) or b > 1:
                    pool.wait_ge(S("pv_done"), 4 * b - 3)
                src = proj[:, ds(b, 1), (G + 1) * HD:QKV].rearrange("p a (kv d) -> p (a kv) d", d=DH)
                settle(nc.gpsimd)
                nc.gpsimd.tensor_copy(value[p][:, :, 0:DH], src).then_inc(S("value_ready"), 1)

            pool.wait_ge(S("attn_zeroed"), 1)
            pool.wait_ge(S("ld_first"), 64)
            pool.wait_ge(S("ld_attn"), 5 * 16)
            pool.wait_ge(S("proj_kept"), B)
            rotate(0)
            narrow_keys(0, 0)

            def half_body(b, p, previous, following, i):
                if i is not None and p == 1:
                    chain.begin(i, 8)
                take_values(b, p)
                if following:
                    rotate(b + 1)
                    narrow_keys(b + 1, 1 - p)
                if i is not None and p == 0:
                    chain.end(7, "rope_chain")

            halves(pool, half_body, lambda b, p: None)

        phase_memory()
        probs4 = sb("probs4", [128, 8, 512])
        head_sel_f = sb("head_sel_f", [XH, XH, 128])
        xq = [sb(f"xq{p}", [128, D]) for p in range(2)]
        xq_hi = [sb(f"xq_hi{p}", [128, D], F32R) for p in range(2)]
        xq_lo = [sb(f"xq_lo{p}", [128, D], F32R) for p in range(2)]
        ctx_hi = sb("ctx_hi", [128, D], F32R)
        ctx_lo = sb("ctx_lo", [128, D], F32R)
        xdiag = [sb(f"xdiag{p}", [128, XH, D], F32R) for p in range(2)]
        xdiag_lo = [sb(f"xdiag_lo{p}", [128, XH, D], F32R) for p in range(2)]
        xq_b = sb("xq_b", [128, D], BF16)
        xdiag_b = sb("xdiag_b", [128, XH, D], BF16)
        ctx_in = [sb(f"ctx_in{p}", [128, D]) for p in range(2)]
        xvalue = [sb(f"xvalue{p}", [128, 2, XH, 32]) for p in range(2)]
        xmax = sb("xmax", [128, 2, XH])
        xshift = [sb(f"xshift{p}", [XH, D], BF16) for p in range(2)]
        xpv = sb("xpv", [128, 512])
        xden = sb("xden", [128, D])
        xout = sb("xout", [128, D])

        def cross_loads(sp):
            with sp.Fori(0, (B - 2) // 2) as i:
                for p in range(2):
                    b = 2 * i + p
                    sp.wait_ge(S("xdiag_ready"), b + 1)
                    sp.wait_ge(S("ctxT_done"), b + 1)
                    sp.dma_start(ctx_in[p][:], io["ctx_2048"][ds(b + 2, 1)].rearrange("a t d -> (a t) d"))\
                        .then_inc(S(f"ld_ctx{p}"), 16)

        def ctx_loaded(eng, b, p):
            eng.wait_ge(S(f"ld_ctx{p}"), 8 * (b - p) + 16)

        def cross_tensor(pe):
            def ctx_transposes(b, p):
                ctx_loaded(pe, b, p)
                for c in range(2):
                    last = nc.tensor.transpose(T0[:, c * 128:c * 128 + 128], ctx_in[p][:, c * 128:c * 128 + 128],
                                               ident[:])
                last.then_inc(S("ctxT_done"), 1)

            def max_scores(b, m):
                if m == 0:
                    pe.wait_ge(S("xq_b_ready"), b + 1)
                    pe.wait_ge(S("xdiag_b_ready"), b + 1)
                pe.wait_ge(S(f"xmax_read{m % 2}"), 4 * b + m // 2)
                hs = 2 * (m % 4)
                nc.tensor.matmul(SMAX[m % 2][:].rearrange("p (h n) -> p h n", h=2),
                                 xq_b[:, m // 4 * 128:m // 4 * 128 + 128], xdiag_b[:, hs:hs + 2, :],
                                 start=True, stop=True).then_inc(S("xmax_scored"), 1)

            def shift_transposes(b):
                pe.wait_ge(S("xvalue_ready"), b + 1)
                pe.wait_ge(S("xmax_read0"), 4 * b + 4)
                pe.wait_ge(S("xmax_read1"), 4 * b + 4)
                for c in range(2):
                    last = nc.tensor.transpose(T0[0:XH, c * 128:c * 128 + 128], xmax[:, c, :], ident[:])
                last.then_inc(S("xmaxT_done"), 1)

            def score(b, p, h):
                if h == 0:
                    pe.wait_ge(S("xshift_ready"), b + 1)
                    pe.wait_ge(S("xdiag_ready"), b + 1)
                    pe.wait_ge(S("xdiag_low_ready"), b + 1)
                    pe.wait_ge(S("xq_low_ready"), b + 1)
                pe.wait_ge(S(f"xprob_ready{h % 2}"), 4 * b + h // 2)
                out = SCORE[h % 2]
                for c in range(2):
                    o = out[:, c * D:c * D + D]
                    nc.tensor.matmul(o, head_sel[:, h, :], xshift[p][:], start=True, stop=False)
                    for k, (keys, query_part) in enumerate(((xdiag, xq_hi), (xdiag, xq_lo), (xdiag_lo, xq_hi))):
                        last = nc.tensor.matmul(o, keys[p][:, h, c * 128:c * 128 + 128], query_part[p][:],
                                                start=False, stop=k == 2)
                last.then_inc(S("xscore_done"), 1)

            def values(b, p, gr):
                pe.wait_ge(S("xprob_ready0"), 4 * b + 2 * gr + 2)
                pe.wait_ge(S("xprob_ready1"), 4 * b + 2 * gr + 2)
                pe.wait_ge(S(f"xpv_kept{gr}"), b)
                for c in range(2):
                    for j in range(4):
                        last = nc.tensor.matmul(PV[gr][32 * j:32 * j + 32, 0:D], xvalue[p][:, c, gr * 4 + j, :],
                                                probs4[:, gr * 4 + j, c * D:c * D + D], start=c == 0, stop=c == 1)
                last.then_inc(S("xpv_done"), 1)

            def gather_rows(b):
                pe.wait_ge(S("xpv_kept1"), b + 1)
                pe.wait_ge(S("xadded"), b)
                for n in range(2):
                    for gr in range(2):
                        last = nc.tensor.matmul(T1[:, n * D:n * D + D], gather[:, 2 * n + gr, :],
                                                xpv[:, gr * D:gr * D + D], start=gr == 0, stop=gr == 1)
                last.then_inc(S("xgathered"), 1)

            def half_body(b, p, previous, following, i):
                for h in range(XH):
                    score(b, p, h)
                    if h == 1 and previous:
                        values(b - 1, 1 - p, 1)
                    if h == 3 and previous:
                        gather_rows(b - 1)
                    if h == 5:
                        values(b, p, 0)
                    if following:
                        if h == 1:
                            ctx_transposes(b + 1, 1 - p)
                        if 2 <= h < 6:
                            max_scores(b + 1, 2 * (h - 2))
                            max_scores(b + 1, 2 * (h - 2) + 1)
                        if h == 7:
                            shift_transposes(b + 1)

            def tail(b, p):
                values(b, p, 1)
                gather_rows(b)

            pe.wait_ge(S("cross_zeroed"), 1)
            pe.wait_ge(S("ld_cross"), 64)
            pe.wait_ge(S("attn_added"), B)
            ctx_transposes(0, 0)
            for m in range(8):
                max_scores(0, m)
            shift_transposes(0)
            halves(pe, half_body, tail, 3)

        def cross_scalar(act):
            def prepare(b, p):
                act.wait_ge(S("xq_ready"), b + 1)
                nc.scalar.copy(xq_b[:], xq[p][:]).then_inc(S("xq_b_ready"), 1)
                act.wait_ge(S("xdiag_ready"), b + 1)
                nc.scalar.copy(xdiag_b[:], xdiag[p][:]).then_inc(S("xdiag_b_ready"), 1)

            def keep_values(b, p):
                act.wait_ge(S("ctxT_done"), b + 1)
                nc.scalar.copy(xvalue[p][:, :, :, 0:XC],
                               T0[:, 0:256].rearrange("p (c h x) -> p c h x", c=2, h=XH)).then_inc(S("xvalue_ready"), 1)

            def keep_shift(b, p):
                act.wait_ge(S("xmaxT_done"), b + 1)
                nc.scalar.mul(xshift[p][:], T0[0:XH, 0:D], -1.0).then_inc(S("xshift_ready"), 1)

            def softmax(b, h):
                act.wait_ge(S("xscore_done"), 8 * b + h + 1)
                if not (isinstance(b, int) and b == 0):
                    act.wait_ge(S("xpv_done"), 2 * b - 1 + h // 4)
                nc.scalar.activation(probs4[:, h, :], SCORE[h % 2][:], ACT.Exp, scale=XSCALE)\
                    .then_inc(S(f"xprob_ready{h % 2}"), 1)

            def pv_keep(b, gr):
                act.wait_ge(S("xpv_done"), 2 * b + gr + 1)
                act.wait_ge(S("xgathered"), b)
                nc.scalar.copy(xpv[:, gr * D:gr * D + D], PV[gr][:, 0:D]).then_inc(S(f"xpv_kept{gr}"), 1)

            def half_body(b, p, previous, following, i):
                for h in range(XH):
                    softmax(b, h)
                    if h == 0 and following:
                        prepare(b + 1, 1 - p)
                    if h == 2 and previous:
                        pv_keep(b - 1, 1)
                    if h == 2 and following:
                        keep_values(b + 1, 1 - p)
                    if h == 6:
                        pv_keep(b, 0)
                    if h == 7 and following:
                        keep_shift(b + 1, 1 - p)

            act.wait_ge(S("cross_zeroed"), 1)
            ln_stats_scalar(act, 2)
            prepare(0, 0)
            keep_values(0, 0)
            keep_shift(0, 0)
            halves(act, half_body, lambda b, p: pv_keep(b, 1), 3)

        def cross_vector(dve):
            def query_(b, p):
                if not isinstance(b, int) or b > 1:
                    dve.wait_ge(S("xscore_done"), 8 * b - 8)
                normalise(xq_hi[p][:], b)
                normalise(xq[p][:], b).then_inc(S("xq_ready"), 1)
                dve.wait_ge(S("xq_ready"), b + 1)
                nc.vector.tensor_tensor(xq_lo[p][:], xq[p][:], xq_hi[p][:], ALU.subtract)\
                    .then_inc(S("xq_low_ready"), 1)

            def reduce_max(b, m):
                dve.wait_ge(S("xmax_scored"), 8 * b + m + 1)
                if m == 0:
                    dve.wait_ge(S("xmaxT_done"), b)
                hs = 2 * (m % 4)
                nc.vector.tensor_reduce(xmax[:, m // 4, hs:hs + 2], SMAX[m % 2][:].rearrange("p (h n) -> p h n", h=2),
                                        AX, ALU.max).then_inc(S(f"xmax_read{m % 2}"), 1)

            def residual(b):
                dve.wait_ge(S("xgathered"), b + 1)
                nc.vector.reciprocal(xden[:], T1[:, D:2 * D]).then_inc(S("xden_ready"), 1)
                dve.wait_ge(S("xden_ready"), b + 1)
                nc.vector.tensor_tensor(xout[:], T1[:, 0:D], xden[:], ALU.mult).then_inc(S("xadded"), 1)
                dve.wait_ge(S("xadded"), b + 1)
                x = X[:, ds(b, 1), :].rearrange("p a d -> p (a d)")
                nc.vector.tensor_tensor(x, x, xout[:], ALU.add).then_inc(S("xdone"), 1)

            def next_stats(b):
                dve.wait_ge(S("xdone"), b + 1)
                settle(nc.vector)
                batch_stats(b)

            def half_body(b, p, previous, following, i):
                for h in range(XH):
                    if h == 0 and following:
                        query_(b + 1, 1 - p)
                    if following and 2 <= h < 6:
                        reduce_max(b + 1, 2 * (h - 2))
                        reduce_max(b + 1, 2 * (h - 2) + 1)
                    if h == 4 and previous:
                        residual(b - 1)
                    if h == 5 and previous:
                        next_stats(b - 1)

            dve.wait_ge(S("attn_added"), B)
            for p in range(2):
                last = nc.vector.memset(xvalue[p][:], 0.0)
            last.then_inc(S("xvalue_zero"), 1)
            dve.wait_ge(S("xvalue_zero"), 1)
            dve.wait_ge(S("ld_cross"), 64)
            nc.vector.tensor_copy(head_sel[:], head_sel_f[:])
            nc.vector.memset(xvalue[0][:, :, :, XC:XC + 1], 1.0)
            nc.vector.memset(xvalue[1][:, :, :, XC:XC + 1], 1.0).then_inc(S("cross_zeroed"), 1)
            ln_stats_vector(dve, 2)
            query_(0, 0)
            for m in range(8):
                reduce_max(0, m)
            def tail(b, p):
                residual(b)
                next_stats(b)

            halves(dve, half_body, tail, 3)

        def cross_pool(pool):
            def spread(b, p):
                ctx_loaded(pool, b, p)
                if later(b):
                    pool.wait_ge(S("xdiag_low_ready"), b)
                settle(nc.gpsimd)
                nc.gpsimd.tensor_copy(ctx_hi[:], ctx_in[p][:]).then_inc(S("ctx_split"), 1)
                pool.wait_ge(S("ctx_split"), 2 * b + 1)
                nc.gpsimd.tensor_tensor(ctx_lo[:], ctx_in[p][:], ctx_hi[:], ALU.subtract)\
                    .then_inc(S("ctx_split"), 1)
                if not isinstance(b, int) or b > 1:
                    pool.wait_ge(S("xscore_done"), 8 * b - 8)
                src = ctx_hi[:].rearrange("p (a n) -> p a n", a=1).to_broadcast([128, XH, D])
                m = head_rows[:].rearrange("p (h a) -> p h a", a=1).to_broadcast([128, XH, D])
                nc.gpsimd.tensor_tensor(xdiag[p][:], src, m, ALU.mult).then_inc(S("xdiag_ready"), 1)
                pool.wait_ge(S("ctx_split"), 2 * b + 2)
                src = ctx_lo[:].rearrange("p (a n) -> p a n", a=1).to_broadcast([128, XH, D])
                nc.gpsimd.tensor_tensor(xdiag_lo[p][:], src, m, ALU.mult).then_inc(S("xdiag_low_ready"), 1)

            def half_body(b, p, previous, following, i):
                if following:
                    spread(b + 1, 1 - p)

            pool.wait_ge(S("ld_cross"), 64)
            pool.wait_ge(S("attn_added"), B)
            spread(0, 0)
            halves(pool, half_body, lambda b, p: None, 3)

        phase_memory()
        xn4 = sb("xn4", [128, ROUTED, D])
        xn4T = sb("xn4T", [128, ROUTED, D])
        logits = sb("logits", [128, ROUTED, E + 1])
        top = sb("top", [128, ROUTED, 8])
        left = sb("left", [128, ROUTED, E])
        chosen = sb("chosen", [128, ROUTED, E])
        route_e = sb("route_e", [128, ROUTED, E + 1])
        route_n = sb("route_n", [128, ROUTED])
        route_s = sb("route_s", [128, ROUTED])
        combine = sb("combine", [128, ROUTED, CROWS])
        combineT = sb("combineT", [CROWS, ROUTED * T])
        x_hi = sb("x_hi", [128, 2, NT], F32R)
        x_lo = sb("x_lo", [128, 2, NT], F32R)
        up_in = [sb(f"up_in{p}", [128, 2, 2, 128]) for p in range(2)]
        up_hi = [sb(f"up_hi{p}", [128, 2, 2, 128], F32R) for p in range(2)]
        up_lo = [sb(f"up_lo{p}", [128, 2, 2, 128], F32R) for p in range(2)]
        down_in = [sb(f"down_in{p}", [128, D]) for p in range(2)]
        down_hi = [sb(f"down_hi{p}", [128, D], F32R) for p in range(2)]
        down_lo = [sb(f"down_lo{p}", [128, D], F32R) for p in range(2)]
        comb = [sb(f"comb{p}", [128, PASS]) for p in range(2)]
        act_g = [sb(f"act_g{h}", [128, 512]) for h in range(2)]
        act_u = [sb(f"act_u{h}", [128, 512]) for h in range(2)]
        hidden = [sb(f"hidden{h}", [128, 512]) for h in range(2)]
        h_hi = [sb(f"h_hi{h}", [128, 512], F32R) for h in range(2)]
        h_lo = [sb(f"h_lo{h}", [128, 512], F32R) for h in range(2)]
        zero_b = sb("zero_b", [128, 128], BF16)
        zero_b4 = sb("zero_b4", [128, 512], BF16)
        scratch = nc.dram_tensor("combine_scratch", [CROWS, NT], F32, kind="Internal").ap()
        GATE = [bank[0], bank[1]]
        UP = [bank[2], bank[3]]
        OUT = [bank[4 + n] for n in range(4)]
        NPASS = NT // PASS
        LAST = NPASS * PAIRS - 1
        assert NPASS == 2 and PAIRS % 2 == 1

        def moe_loads(sp):
            with sp.Fori(0, B // ROUTED) as i:
                sp.wait_ge(S("combineT_ready"), i + 1)
                sp.dma_start(scratch[:, ds(i * (ROUTED * T), ROUTED * T)], combineT[:]).then_inc(S("combine_out"), 16)
            sp.wait_ge(S("combine_out"), 16 * (B // ROUTED))
            sp.wait_ge(S("xdone"), B)

            def loads(n, j, p, t0):
                later = not isinstance(n, int) or n > 1
                if later:
                    sp.wait_ge(S("up_split"), n - 1)
                sp.dma_start(up_in[p][:], io["w_up"][ds(j, 1)].rearrange("a p n -> (a p) n")
                             .rearrange("p (c s m) -> p c s m", c=2, s=2)).then_inc(S(f"ld_up{p}"), 16)
                if later:
                    sp.wait_ge(S("weighed1"), n - 1)
                for r in range(2):
                    sp.dma_start(comb[p][64 * r:64 * r + 64, :],
                                 scratch[ds(2 * j + r, 1), t0:t0 + PASS].to_broadcast([64, PASS]))\
                        .then_inc(S(f"ld_comb{p}"), 16)
                if later:
                    sp.wait_ge(S("down_split"), n - 1)
                sp.dma_start(down_in[p][:], io["w_down"][ds(j, 1)].rearrange("a p n -> (a p) n"))\
                    .then_inc(S(f"ld_down{p}"), 16)

            def store(ps):
                sp.wait_ge(S("final_ready"), ps + 1)
                sp.dma_start(io["out"].rearrange("b t d -> t b d")[:, 8 * ps:8 * ps + 8, :],
                             X[:, 8 * ps:8 * ps + 8, :]).then_inc(S("stored"), 16)

            for ps in range(NPASS):
                n0, first = ps * PAIRS, 3
                for j in range(first):
                    loads(n0 + j, j, (n0 + j) % 2, ps * PASS)
                if ps:
                    store(ps - 1)
                with sp.Fori(0, (PAIRS - first) // 2) as i:
                    for h in range(2):
                        j = 2 * i + first + h
                        loads(j + n0, j, (n0 + first + h) % 2, ps * PASS)
            store(NPASS - 1)
            sp.wait_ge(S("stored"), 16 * NPASS)

        def moe_tensor(pe):
            pe.wait_ge(S("ld_cross"), 64)

            def front(i):
                for p in range(ROUTED):
                    b = ROUTED * i + p
                    pe.wait_ge(S("xn3_ready"), b + 1)
                    if later(i):
                        pe.wait_ge(S("xn3T_ready"), b + 1 - ROUTED)
                    for c in range(2):
                        last = nc.tensor.transpose(bank[p][:, c * 128:c * 128 + 128],
                                                   xn4[:, p, c * 128:c * 128 + 128], ident[:])
                    last.then_inc(S("x3T_done"), 1)
                if later(i):
                    pe.wait_ge(S("logits_kept"), i)
                for p in range(ROUTED):
                    pe.wait_ge(S("xn3T_ready"), ROUTED * i + p + 1)
                    for c in range(2):
                        last = nc.tensor.matmul(bank[4][:, p * (E + 1):(p + 1) * (E + 1)],
                                                xn4T[:, p, c * 128:c * 128 + 128],
                                                w_router[:, c, :], start=c == 0, stop=c == 1)
                last.then_inc(S("logits_done"), 1)

            def back(i):
                pe.wait_ge(S("combine_ready"), i + 1)
                if later(i):
                    pe.wait_ge(S("combineT_ready"), i)
                for p in range(ROUTED):
                    last = nc.tensor.transpose(bank[5][0:CROWS, p * T:p * T + T], combine[:, p, :], ident[:])
                last.then_inc(S("combineT_done"), 1)

            overlapped(pe, B // ROUTED, front, back)

            def up(n, p, t0, h):
                if h == 0:
                    pe.wait_ge(S("up_split"), n + 1)
                pe.wait_ge(S(f"gated{h}"), n)
                pe.wait_ge(S(f"upped{h}"), n)
                t = t0 + 512 * h
                for s, out in enumerate((GATE[h], UP[h])):
                    for k in range(6):
                        c, (wp, xp) = k // 3, ((up_hi, x_hi), (up_hi, x_lo), (up_lo, x_hi))[k % 3]
                        last = nc.tensor.matmul(out[:], wp[p][:, c, s, :], xp[:, c, t:t + 512],
                                                start=k == 0, stop=k == 5)
                    last.then_inc(S(("gate_done", "up_done")[s]), 1)

            def down(n, p, h):
                if h == 0:
                    pe.wait_ge(S("down_split"), n + 1)
                pe.wait_ge(S(f"h_ready{h}"), n + 1)
                for q in range(4):
                    k = 4 * h + q
                    for hp, wp in ((h_hi, down_hi), (h_hi, down_lo), (h_lo, down_hi)):
                        last = nc.tensor.matmul(OUT[k // 2][:, k % 2 * D:k % 2 * D + D],
                                                hp[h][:, q * 128:q * 128 + 128], wp[p][:],
                                                start=False, stop=True, skip_group_check=True)
                last.then_inc(S("down_done"), 1)

            def start_sums():
                for k in range(4):
                    nc.tensor.matmul(OUT[k][:], zero_b[:], zero_b4[:], start=True, stop=True, skip_group_check=True)

            def slot(n, p, t0):
                for h in range(2):
                    up(n, p, t0, h)
                    down(n - 1, 1 - p, h)

            pe.wait_ge(S("xn3T_ready"), B)
            pe.wait_ge(S("combineT_ready"), B // ROUTED)
            pe.wait_ge(S("x_lo_ready"), B)
            start_sums()
            up(0, 0, 0, 0)
            up(0, 0, 0, 1)
            slot(1, 1, 0)
            slot(2, 0, 0)
            with pe.Fori(1, (PAIRS - 1) // 2) as i:
                slot(2 * i + 1, 1, 0)
                slot(2 * i + 2, 0, 0)
            slot(PAIRS, 1, PASS)
            pe.wait_ge(S("final_ready"), 1)
            start_sums()
            with pe.Fori(0, (PAIRS - 1) // 2) as i:
                slot(2 * i + PAIRS + 1, 0, PASS)
                slot(2 * i + PAIRS + 2, 1, PASS)
            down(LAST, 1, 0)
            down(LAST, 1, 1)

        def all_pairs(engine, body, middle=None):
            for n in range(3):
                body(n, n % 2)
            with engine.Fori(1, (PAIRS - 1) // 2) as i:
                body(2 * i + 1, 1)
                body(2 * i + 2, 0)
            body(PAIRS, 1)
            if middle:
                middle()
            with engine.Fori(0, (PAIRS - 3) // 2) as i:
                body(2 * i + PAIRS + 1, 0)
                body(2 * i + PAIRS + 2, 1)
            body(LAST - 1, 0)
            body(LAST, 1)

        def moe_scalar(act):
            ln_stats_scalar(act, 3)

            def front(i):
                if later(i):
                    act.wait_ge(S("logits_done"), i)
                    act.wait_ge(S("x_lo_ready"), ROUTED * i)
                for p in range(ROUTED):
                    b = ROUTED * i + p
                    act.wait_ge(S("x3T_done"), b + 1)
                    nc.scalar.copy(x_hi[:, :, ds(b * T, T)], bank[p][:, 0:D].rearrange("p (c t) -> p c t", c=2))\
                        .then_inc(S("x_hi_ready"), 1)
                    nc.scalar.copy(xn4T[:, p, :], bank[p][:, 0:D]).then_inc(S("xn3T_ready"), 1)

            def back(i):
                act.wait_ge(S("logits_done"), i + 1)
                if later(i):
                    act.wait_ge(S("combine_ready"), i)
                nc.scalar.copy(logits[:].rearrange("p b e -> p (b e)"), bank[4][:, 0:ROUTED * (E + 1)])\
                    .then_inc(S("logits_kept"), 1)
                act.wait_ge(S("route_max"), i + 1)
                for p in range(ROUTED):
                    nc.scalar.activation(route_e[:, p, 0:E], logits[:, p, 0:E], ACT.Exp, bias=route_n[:, p:p + 1])
                nc.scalar.activation(route_e[:, :, E], logits[:, :, E], ACT.Exp, scale=-1.0)\
                    .then_inc(S("route_exp"), 1)
                act.wait_ge(S("combineT_done"), i + 1)
                if later(i):
                    act.wait_ge(S("combine_out"), 16 * i)
                nc.scalar.copy(combineT[:], bank[5][0:CROWS, :]).then_inc(S("combineT_ready"), 1)

            overlapped(act, B // ROUTED, front, back)

            def gate(n, h):
                act.wait_ge(S("gate_done"), 2 * n + h + 1)
                act.wait_ge(S(f"upped{h}"), n)
                nc.scalar.activation(act_g[h][:], GATE[h][:], ACT.Silu).then_inc(S(f"gated{h}"), 1)

            def hidden_high(n, h):
                act.wait_ge(S(f"weighed{h}"), n + 1)
                if not isinstance(n, int) or n:
                    act.wait_ge(S("down_done"), 2 * n - 1 + h)
                nc.scalar.copy(h_hi[h][:], hidden[h][:]).then_inc(S(f"h_hi_ready{h}"), 1)

            def up_high(n, p):
                act.wait_ge(S(f"ld_up{p}"), 8 * (n - p) + 16)
                if not isinstance(n, int) or n > 1:
                    act.wait_ge(S("up_done"), 2 * n - 2)
                nc.scalar.copy(up_hi[p][:], up_in[p][:]).then_inc(S("up_hi_ready"), 1)

            def down_high(n, p):
                act.wait_ge(S(f"ld_down{p}"), 8 * (n - p) + 16)
                if not isinstance(n, int) or n > 1:
                    act.wait_ge(S("down_done"), 2 * n - 2)
                nc.scalar.copy(down_hi[p][:], down_in[p][:]).then_inc(S("down_hi_ready"), 1)

            def pair(n, p):
                gate(n, 0)
                if not isinstance(n, int) or n:
                    hidden_high(n - 1, 1)
                if not isinstance(n, int) or n < LAST:
                    up_high(n + 1, 1 - p)
                gate(n, 1)
                hidden_high(n, 0)
                down_high(n, p)

            up_high(0, 0)
            all_pairs(act, pair)
            hidden_high(LAST, 1)

        def moe_vector(dve):
            dve.wait_ge(S("xdone"), B)
            nc.vector.memset(zero_b[:], 0.0)
            nc.vector.memset(zero_b4[:], 0.0)
            nc.vector.memset(combine[:], 0.0).then_inc(S("moe_zeroed"), 1)
            ln_stats_vector(dve, 3)
            chain = Tally(S("route_chain"))

            def link(ins):
                ins.then_inc(chain.sem, 1)
                chain.add(1)
                dve.wait_ge(chain.sem, chain.value())

            def front(i):
                for p in range(ROUTED):
                    b = ROUTED * i + p
                    if later(i):
                        dve.wait_ge(S("x3T_done"), b + 1 - ROUTED)
                    normalise(xn4[:, p, :], b).then_inc(S("xn3_ready"), 1)
                for p in range(ROUTED):
                    b = ROUTED * i + p
                    dve.wait_ge(S("xn3T_ready"), b + 1)
                    dve.wait_ge(S("x_hi_ready"), b + 1)
                    nc.vector.tensor_tensor(x_lo[:, :, ds(b * T, T)], xn4T[:, p, :].rearrange("p (c t) -> p c t", c=2),
                                            x_hi[:, :, ds(b * T, T)], ALU.subtract).then_inc(S("x_lo_ready"), 1)

            def back(i):
                if not isinstance(i, int):
                    chain.begin(i - 1, CHAIN_ROUTE)
                dve.wait_ge(S("logits_kept"), i + 1)
                settle(nc.vector)
                for p in range(ROUTED):
                    last = nc.vector.max(top[:, p, :], logits[:, p, 0:E])
                link(last)
                nc.vector.tensor_scalar(route_n[:], top[:, :, 0], -1.0, None, ALU.mult).then_inc(S("route_max"), 1)
                for p in range(ROUTED):
                    last = nc.vector.match_replace(left[:, p, :], top[:, p, :], logits[:, p, 0:E], -3.0e38)
                link(last)
                link(nc.vector.tensor_tensor(chosen[:], logits[:, :, 0:E], left[:], ALU.not_equal))
                dve.wait_ge(S("route_exp"), i + 1)
                link(nc.vector.tensor_tensor(chosen[:], chosen[:], route_e[:, :, 0:E], ALU.mult))
                link(nc.vector.tensor_reduce(route_s[:], chosen[:], AX, ALU.add))
                link(nc.vector.reciprocal(route_s[:], route_s[:]))
                if later(i):
                    dve.wait_ge(S("combineT_done"), i)
                sums = route_s[:].rearrange("p (b a) -> p b a", a=1).to_broadcast([128, ROUTED, E])
                nc.vector.tensor_tensor(combine[:, :, 0:E], chosen[:], sums, ALU.mult)
                link(nc.vector.tensor_scalar(route_e[:, :, E], route_e[:, :, E], 1.0, None, ALU.add))
                nc.vector.reciprocal(combine[:, :, E], route_e[:, :, E]).then_inc(S("combine_ready"), 1)
                if not isinstance(i, int):
                    chain.end(B // ROUTED - 2, "CHAIN_ROUTE")

            overlapped(dve, B // ROUTED, front, back)

            def gated(n, h):
                dve.wait_ge(S(f"gated{h}"), n + 1)
                dve.wait_ge(S("up_done"), 2 * n + h + 1)
                dve.wait_ge(S(f"weighed{h}"), n)
                nc.vector.tensor_tensor(act_u[h][:], act_g[h][:], UP[h][:], ALU.mult).then_inc(S(f"upped{h}"), 1)

            def hidden_low(n, h):
                dve.wait_ge(S(f"h_hi_ready{h}"), n + 1)
                nc.vector.tensor_tensor(h_lo[h][:], hidden[h][:], h_hi[h][:], ALU.subtract)\
                    .then_inc(S(f"h_ready{h}"), 1)

            def pair(n, p):
                gated(n, 0)
                if not isinstance(n, int) or n:
                    hidden_low(n - 1, 1)
                gated(n, 1)
                hidden_low(n, 0)

            def final(ps):
                dve.wait_ge(S("down_done"), 2 * PAIRS * (ps + 1))
                for k in range(4):
                    x = X[:, 8 * ps + 2 * k:8 * ps + 2 * k + 2, :].rearrange("p b d -> p (b d)")
                    last = nc.vector.tensor_tensor(x, x, OUT[k][:], ALU.add)
                last.then_inc(S("final_ready"), 1)

            all_pairs(dve, pair, lambda: final(0))
            hidden_low(LAST, 1)
            final(1)

        def moe_pool(pool):
            def weigh(n, p, h):
                if h == 0:
                    pool.wait_ge(S(f"ld_comb{p}"), 16 * (n - p) + 32)
                pool.wait_ge(S(f"upped{h}"), n + 1)
                pool.wait_ge(S(f"h_ready{h}"), n)
                nc.gpsimd.tensor_tensor(hidden[h][:], act_u[h][:], comb[p][:, 512 * h:512 * h + 512], ALU.mult)\
                    .then_inc(S(f"weighed{h}"), 1)

            def up_low(n, p):
                pool.wait_ge(S("up_hi_ready"), n + 1)
                nc.gpsimd.tensor_tensor(up_lo[p][:], up_in[p][:], up_hi[p][:], ALU.subtract)\
                    .then_inc(S("up_split"), 1)

            def down_low(n, p):
                pool.wait_ge(S("down_hi_ready"), n + 1)
                nc.gpsimd.tensor_tensor(down_lo[p][:], down_in[p][:], down_hi[p][:], ALU.subtract)\
                    .then_inc(S("down_split"), 1)

            def pair(n, p):
                weigh(n, p, 0)
                if not isinstance(n, int) or n < LAST:
                    up_low(n + 1, 1 - p)
                weigh(n, p, 1)
                down_low(n, p)

            up_low(0, 0)
            all_pairs(pool, pair)

        place[0].close()
        block = ctx.enter_context(nc.Block())

        @block.gpsimd
        def _(pool):
            attn_pool(pool)
            cross_pool(pool)
            moe_pool(pool)

        @block.vector
        def _(dve):
            proj_vector(dve)
            comp_vector(dve)
            attn_vector(dve)
            cross_vector(dve)
            moe_vector(dve)

        @block.scalar
        def _(act):
            proj_scalar(act)
            comp_scalar(act)
            attn_scalar(act)
            cross_scalar(act)
            moe_scalar(act)

        @block.tensor
        def _(pe):
            proj_tensor(pe)
            comp_tensor(pe)
            attn_tensor(pe)
            cross_tensor(pe)
            moe_tensor(pe)

        @block.sync
        def _(sp):
            def load(dst, src, s):
                sp.dma_start(dst, src).then_inc(S(s), 16)

            xv = io["x"].rearrange("b t d -> t b d")
            load(ident[:], io["c_ident"], "ld_first")
            for c in range(2):
                load(X[:, 8 * c:8 * c + 8, :], xv[:, 8 * c:8 * c + 8, :], "ld_x")
            load(w_proj[:], io["w_proj"].rearrange("(c p) n -> p c n", p=128), "ld_first")
            load(pos[:], io["pos"], "ld_first")
            load(gate_bias[:], io["gate_bias"].partition_broadcast(128), "ld_first")
            for n, name in enumerate(("L0_attn_k_cb1", "L0_attn_v_cb1")):
                load(cb1[:, n:n + 1], io[name].rearrange("(p a) -> p a", a=1), "ld_comp")
            sp.wait_ge(S("zeroed"), 1)
            load(w2k[:, 120:128], io["L0_attn_k_cw2"], "ld_comp")
            load(b2k[:, 120:128], io["L0_attn_k_cb2"].rearrange("(a d) -> a d", a=1), "ld_comp")
            load(w2v[:], io["L0_attn_v_cw2"], "ld_comp")
            load(b2v[:], io["L0_attn_v_cb2"].partition_broadcast(64), "ld_comp")
            for g in range(2):
                load(mem_k[64 * g:64 * g + 64, :], io["L0_attn_mem_ck"].rearrange("h a d -> (h d) a"), "ld_comp")
            load(cv_raw[64:72, 0, :], io["L0_attn_mem_cv"].rearrange("h a d -> (h a) d"), "ld_comp")
            load(kv_rows[:], io["c_kv_rows"], "ld_comp")
            load(cv_rows[:], io["c_cv_rows"], "ld_comp")

            def load_w1(name, s):
                src = io[name].rearrange("(i r d) n -> r d i n", r=2, d=DH)
                for r in range(2):
                    for kv in range(KV):
                        p0 = r * HD + kv * DH
                        load(w1_diag[p0:p0 + DH, :, kv * 128:kv * 128 + 128], src[r], s)

            load_w1("L0_attn_k_cw1", "ld_w1k")
            for dst, name in ((masks, "c_masks"), (rope_cs, "c_rope"), (block_mask, "c_block_mask"), (past_neg, "c_past_neg")):
                load(dst[:], io[name], "ld_attn")
            load(w_out[:], io["w_out"].rearrange("(c p) n -> p c n", p=128), "ld_attn")
            load(head_rows[:], io["c_head_rows"], "ld_cross")
            load(gather[:], io["c_gather"], "ld_cross")
            load(w_router[:], io["w_router"].rearrange("(c p) n -> p c n", p=128), "ld_cross")
            sp.wait_ge(S("hidden_done"), 1)
            load_w1("L0_attn_v_cw1", "ld_w1v")
            sp.wait_ge(S("cv_ready"), 1)
            load(key_rows, io["c_key_rows"], "ld_key_rows")
            sp.wait_ge(S("attn_added"), B)
            for i in range(2):
                load(ctx_in[i][:], io["ctx_2048"][i], f"ld_ctx{i}")
            load(head_sel_f[:], io["c_head_sel"], "ld_cross")
            cross_loads(sp)
            moe_loads(sp)



def constants():
    import numpy as np

    f4, neg = np.float32, -1e30
    t = np.arange(T)
    past = (np.arange(NB)[None] + 1) * BLK - 1 < t[:, None]
    ahead = t[None] > t[:, None]
    inv = f4(1.0) / f4(10000.0) ** (np.arange(0, DH, 2, dtype=f4) / f4(DH))
    ang = t.astype(f4)[:, None] * inv[None]
    key_rows = np.zeros((64, KV, T), f4)
    for kv in range(KV):
        for c in range(NB - 1):
            key_rows[kv * 7 + c, kv, c * BLK:c * BLK + BLK] = 1.0
        key_rows[56 + kv, kv] = -1.0
    kv_rows = np.zeros((128, 2 * KV), f4)
    kv_rows[np.arange(128), np.arange(128) // DH] = 1.0
    cv_rows = np.zeros((128, KV), f4)
    cv_rows[np.arange(64), np.arange(64) // NB] = 1.0
    cv_rows[64 + np.arange(KV), np.arange(KV)] = 1.0
    head_rows = np.zeros((128, XH), f4)
    head_rows[t, t // XC] = 1.0
    head_sel = np.zeros((XH, XH, 128), f4)
    head_sel[np.arange(XH), np.arange(XH)] = 1.0
    gather = np.zeros((128, 4, 128), f4)
    for h in range(XH):
        for c in range(XC):
            gather[h % 4 * 32 + c, h // 4, h * XC + c] = 1.0
            gather[h % 4 * 32 + XC, 2 + h // 4, h * XC + c] = 1.0
    return {
        "c_ident": np.eye(128, dtype=f4),
        "c_masks": np.stack([np.where(ahead, neg, 0.0),
                             np.where(ahead | (t[:, None] - t[None] > 64), neg, 0.0)], 1).astype(f4),
        "c_rope": np.stack([np.cos(ang), np.sin(ang)], 1).astype(f4),
        "c_block_mask": np.where(past, 0.0, neg).astype(f4), "c_past_neg": np.where(past, neg, 0.0).astype(f4),
        "c_kv_rows": kv_rows, "c_cv_rows": cv_rows, "c_head_rows": head_rows,
        "c_head_sel": head_sel, "c_gather": gather, "c_key_rows": key_rows,
    }


def layouts(a):
    import numpy as np

    q = a["L0_attn_w_qkv"][:, :G * HD].reshape(D, KV, G, DH).transpose(0, 2, 1, 3).reshape(D, G * HD)
    gate = a["L0_attn_w_gate"].reshape(D, KV, G, 3).transpose(0, 3, 2, 1).reshape(D, 96)
    none = np.zeros((1, D, I), np.float32)
    up = [np.concatenate([a[f"L0_ffn_expert_{s}_w"], a[f"L0_ffn_shared_{s}_w"][None], none]) for s in ("gate", "up")]
    up = np.stack(up).reshape(2, PAIRS, 2, 2, 128, I)
    down = np.concatenate([a["L0_ffn_expert_down_w"], a["L0_ffn_shared_down_w"][None], none.reshape(1, I, D)])
    pos = [np.tile(a[n].transpose(1, 0, 2).reshape(BLK, HD), (NB, 1)) for n in ("L0_attn_k_pos", "L0_attn_v_pos")]
    return {
        "w_proj": np.concatenate([q, a["L0_attn_w_qkv"][:, G * HD:], gate], 1),
        "gate_bias": a["L0_attn_b_gate"].reshape(KV, G, 3).transpose(2, 1, 0).reshape(96),
        "w_out": a["L0_attn_w_out"].reshape(KV, G, DH, D).transpose(1, 0, 2, 3).reshape(D, D),
        "pos": np.stack(pos, 1),
        "w_router": np.concatenate([a["L0_ffn_gate_w"], a["L0_ffn_shared_expert_gate_w"]], 1),
        "w_up": up.transpose(1, 4, 3, 0, 2, 5).reshape(PAIRS, 128, 512),
        "w_down": down.reshape(PAIRS, 128, D),
    }


PLAIN = ["x", "ctx_2048", "L0_attn_k_cw1", "L0_attn_k_cb1", "L0_attn_k_cw2", "L0_attn_k_cb2", "L0_attn_v_cw1",
         "L0_attn_v_cb1", "L0_attn_v_cw2", "L0_attn_v_cb2", "L0_attn_mem_ck", "L0_attn_mem_cv"]


def kernel(**inputs):
    import numpy as np
    import concourse.bacc as bacc
    from concourse.bass_utils import run_bass_kernel_spmd

    a = {k: np.asarray(v) for k, v in inputs.items()}
    sent = {n: a[n] for n in PLAIN} | layouts(a) | constants()
    nc = bacc.Bacc("TRN2", target_bir_lowering=False, num_devices=1)
    arrays, io = {}, {}
    for name, v in sent.items():
        v = np.ascontiguousarray(v)
        arrays[f"in_{name}"] = v
        io[name] = nc.dram_tensor(f"in_{name}", v.shape, mybir.dt.from_np(v.dtype), kind="ExternalInput").ap()
    io["out"] = nc.dram_tensor("out_0", (B, T, D), F32, kind="ExternalOutput").ap()
    build(nc, io)
    r = run_bass_kernel_spmd(nc, [arrays], core_ids=[0])
    return r.results[0]["out_0"]
```
